# Optimizing a Trainium2 kernel written in Bass

```python
import numpy as np
import jax
import jax.numpy as jnp

def _softmax(x, axis=-1):
    return jax.nn.softmax(x, axis=axis)

def _gelu(x):
    return jax.nn.gelu(x, approximate=True)

def _silu(x):
    return jax.nn.silu(x)

def _sigmoid(x):
    return jax.nn.sigmoid(x)

def _layernorm(x, axis=-1, eps=1e-05):
    m = jnp.mean(x, axis=axis, keepdims=True)
    v = jnp.var(x, axis=axis, keepdims=True)
    return (x - m) / jnp.sqrt(v + eps)

def _scatter_add(tgt, idx, src, axis=0):
    return tgt.at[idx].add(src)

def _segment_sum(src, seg, n):
    return jax.ops.segment_sum(src, seg, n)
kernel_name = 'mk_hybrid_d1_jaxref_r8_3fbc50'

def setup_inputs(seed: int=0):
    np.random.seed(seed)
    _w = jnp.asarray

    def _L0_attn_a_setup():
        import jax, jax.numpy as jnp
        import numpy as np
        B, T, C = (4, 512, 128)
        H = 16
        D = C // H
        W_SCALE = 0.02
        key = jax.random.key(seed)
        ks = jax.random.split(key, 9)
        inp = {'x': jax.random.normal(ks[0], (B, T, C), dtype=jnp.float32)}
        for i, nm in enumerate(['q', 'k', 'v', 'o']):
            inp[f'W{nm}'] = jax.random.normal(ks[1 + i], (C, C), dtype=jnp.float32) * W_SCALE
            inp[f'b{nm}'] = jnp.zeros((C,), dtype=jnp.float32)
        return inp
    _L0_attn_a_in = _L0_attn_a_setup()

    def _L0_attn_b_setup():
        import jax, jax.numpy as jnp
        import numpy as np
        B, N, D, H = (4, 256, 128, 16)
        DH = D // H
        EPS = 1e-05
        key = jax.random.key(seed)
        k1, k2, k3, k4 = jax.random.split(key, 4)
        return {'x': jax.random.normal(k1, (B, N, D), dtype=jnp.float32), 'g_ln': jnp.ones((D,), dtype=jnp.float32), 'Wq': jax.random.normal(k2, (D, D), dtype=jnp.float32) * 0.02, 'Wkv': jax.random.normal(k3, (D, 2 * D), dtype=jnp.float32) * 0.02, 'Wo': jax.random.normal(k4, (D, D), dtype=jnp.float32) * 0.02}
    _L0_attn_b_in = _L0_attn_b_setup()

    def _L0_ffn_setup():
        import jax, jax.numpy as jnp
        import numpy as np
        B, S, D = (2, 256, 128)
        H, E, P, K = (8, 8, 128, 2)
        SCALE = 1.0 / np.sqrt(P)

        def _get_sel_gate(x, w, route_scale):
            logits = jnp.einsum('bsd,ed->bse', x, w).astype(jnp.float32)
            raw = logits.reshape(x.shape[0], x.shape[1], H, E)
            probs = jax.nn.sigmoid(raw)
            vals, idx = jax.lax.top_k(probs, K)
            vals = vals / jnp.clip(vals.sum(-1, keepdims=True), 1e-09)
            vals = vals * route_scale
            gate = (jax.nn.one_hot(idx, E, dtype=vals.dtype) * vals[..., None]).sum(-2)
            return gate
        key = jax.random.key(seed)
        ks = jax.random.split(key, 8)
        std = 1.0 / np.sqrt(D)
        return {'x': jax.random.normal(ks[0], (B, S, D), jnp.float32), 'q_w': jax.random.normal(ks[1], (H * P, D), jnp.float32) * std, 'k_w': jax.random.normal(ks[2], (H * P, D), jnp.float32) * std, 'v_w': jax.random.normal(ks[3], (H * E, D, P), jnp.float32) * std, 'o_w': jax.random.normal(ks[4], (H * E, P, D), jnp.float32) * (1.0 / np.sqrt(H * P)), 'sel_v_w': jax.random.normal(ks[5], (H * E, D), jnp.float32) * std, 'sel_o_w': jax.random.normal(ks[6], (H * E, D), jnp.float32) * std, 'route_scale': jnp.ones((1,), jnp.float32)}
    _L0_ffn_in = _L0_ffn_setup()
    _d = {'L0_attn_a_x': _L0_attn_a_in['x'], 'L0_attn_a_Wq': _L0_attn_a_in['Wq'], 'L0_attn_a_bq': _L0_attn_a_in['bq'], 'L0_attn_a_Wk': _L0_attn_a_in['Wk'], 'L0_attn_a_bk': _L0_attn_a_in['bk'], 'L0_attn_a_Wv': _L0_attn_a_in['Wv'], 'L0_attn_a_bv': _L0_attn_a_in['bv'], 'L0_attn_a_Wo': _L0_attn_a_in['Wo'], 'L0_attn_a_bo': _L0_attn_a_in['bo'], 'L0_attn_b_g_ln': _L0_attn_b_in['g_ln'], 'L0_attn_b_Wq': _L0_attn_b_in['Wq'], 'L0_attn_b_Wkv': _L0_attn_b_in['Wkv'], 'L0_attn_b_Wo': _L0_attn_b_in['Wo'], 'L0_ffn_q_w': _L0_ffn_in['q_w'], 'L0_ffn_k_w': _L0_ffn_in['k_w'], 'L0_ffn_v_w': _L0_ffn_in['v_w'], 'L0_ffn_o_w': _L0_ffn_in['o_w'], 'L0_ffn_sel_v_w': _L0_ffn_in['sel_v_w'], 'L0_ffn_sel_o_w': _L0_ffn_in['sel_o_w'], 'L0_ffn_route_scale': _L0_ffn_in['route_scale']}
    _x0 = _d['L0_attn_a_x']
    _d['L0_attn_a_x'] = jax.random.normal(jax.random.fold_in(jax.random.key(seed), 1), (1, 2048, 128), dtype=_x0.dtype)
    del _x0
    return _d

def reference(L0_attn_a_x, L0_attn_a_Wq, L0_attn_a_bq, L0_attn_a_Wk, L0_attn_a_bk, L0_attn_a_Wv, L0_attn_a_bv, L0_attn_a_Wo, L0_attn_a_bo, L0_attn_b_g_ln, L0_attn_b_Wq, L0_attn_b_Wkv, L0_attn_b_Wo, L0_ffn_q_w, L0_ffn_k_w, L0_ffn_v_w, L0_ffn_o_w, L0_ffn_sel_v_w, L0_ffn_sel_o_w, L0_ffn_route_scale):

    def _L0_attn_a_ref(x, Wq, bq, Wk, bk, Wv, bv, Wo, bo):
        import jax, jax.numpy as jnp
        import numpy as np
        B, T, C = (4, 512, 128)
        H = 16
        D = C // H
        W_SCALE = 0.02
        Bx, Tx, Cx = x.shape
        q = (x @ Wq.T + bq).reshape(Bx, Tx, H, D)
        k = (x @ Wk.T + bk).reshape(Bx, Tx, H, D)
        v = (x @ Wv.T + bv).reshape(Bx, Tx, H, D)
        q = jax.nn.elu(q) + 1.0
        k = jax.nn.elu(k) + 1.0
        kv = jnp.einsum('bthd,bthe->bhde', k, v)
        denom = jnp.einsum('bthd,bhd->bth', q, k.sum(axis=1))
        num = jnp.einsum('bthd,bhde->bthe', q, kv)
        out = num / jnp.clip(denom, 1e-06, None)[..., None]
        out = out.reshape(Bx, Tx, Cx)
        return out @ Wo.T + bo

    def _L0_attn_b_ref(x, g_ln, Wq, Wkv, Wo):
        import jax, jax.numpy as jnp
        import numpy as np
        B, N, D, H = (4, 256, 128, 16)
        DH = D // H
        EPS = 1e-05
        mu = jnp.mean(x, axis=-1, keepdims=True)
        var = jnp.mean(jnp.square(x - mu), axis=-1, keepdims=True)
        xn = (x - mu) * jax.lax.rsqrt(var + EPS) * g_ln
        b, n, d = xn.shape
        q = (xn @ Wq).reshape(b, n, H, DH).transpose(0, 2, 1, 3)
        kv = xn @ Wkv
        k, v = jnp.split(kv, 2, axis=-1)
        k = k.reshape(b, n, H, DH).transpose(0, 2, 1, 3)
        v = v.reshape(b, n, H, DH).transpose(0, 2, 1, 3)
        scale = DH ** (-0.5)
        dots = jnp.einsum('bhid,bhjd->bhij', q, k) * scale
        mask_value = -jnp.finfo(dots.dtype).max
        causal = jnp.triu(jnp.ones((n, n), dtype=bool), k=1)
        dots = jnp.where(causal, mask_value, dots)
        attn = jax.nn.softmax(dots.astype(jnp.float32), axis=-1).astype(dots.dtype)
        out = jnp.einsum('bhij,bhjd->bhid', attn, v)
        out = out.transpose(0, 2, 1, 3).reshape(b, n, d)
        return out @ Wo

    def _L0_ffn_ref(x, q_w, k_w, v_w, o_w, sel_v_w, sel_o_w, route_scale):
        import jax, jax.numpy as jnp
        import numpy as np
        B, S, D = (2, 256, 128)
        H, E, P, K = (8, 8, 128, 2)
        SCALE = 1.0 / np.sqrt(P)

        def _get_sel_gate(x, w, route_scale):
            logits = jnp.einsum('bsd,ed->bse', x, w).astype(jnp.float32)
            raw = logits.reshape(x.shape[0], x.shape[1], H, E)
            probs = jax.nn.sigmoid(raw)
            vals, idx = jax.lax.top_k(probs, K)
            vals = vals / jnp.clip(vals.sum(-1, keepdims=True), 1e-09)
            vals = vals * route_scale
            gate = (jax.nn.one_hot(idx, E, dtype=vals.dtype) * vals[..., None]).sum(-2)
            return gate
        rs = route_scale[0]
        gate_v = _get_sel_gate(x, sel_v_w, rs)
        gate_o = _get_sel_gate(x, sel_o_w, rs)
        q = jnp.einsum('bsd,hpd->bhsp', x, q_w.reshape(H, P, D))
        k = jnp.einsum('bsd,hpd->bhsp', x, k_w.reshape(H, P, D))
        xv = jnp.einsum('bsd,hedp->bshep', x, v_w.reshape(H, E, D, P))
        v = jnp.einsum('bshep,bshe->bhsp', xv, gate_v)
        att = jax.nn.softmax(jnp.einsum('bhqp,bhkp->bhqk', q, k) * SCALE, axis=-1)
        ctx = jnp.einsum('bhqk,bhkp->bqhp', att, v)
        weighted = ctx[:, :, :, None, :] * gate_o[..., None]
        out = jnp.einsum('bshep,hepd->bsd', weighted, o_w.reshape(H, E, P, D))
        return out
    x = L0_attn_a_x
    x = x + _L0_attn_a_ref(_layernorm(x, axis=-1), L0_attn_a_Wq, L0_attn_a_bq, L0_attn_a_Wk, L0_attn_a_bk, L0_attn_a_Wv, L0_attn_a_bv, L0_attn_a_Wo, L0_attn_a_bo)
    x = x + _L0_ffn_ref(_layernorm(x, axis=-1), L0_ffn_q_w, L0_ffn_k_w, L0_ffn_v_w, L0_ffn_o_w, L0_ffn_sel_v_w, L0_ffn_sel_o_w, L0_ffn_route_scale)
    x = x + _L0_attn_b_ref(_layernorm(x, axis=-1), L0_attn_b_g_ln, L0_attn_b_Wq, L0_attn_b_Wkv, L0_attn_b_Wo)
    x = x + _L0_ffn_ref(_layernorm(x, axis=-1), L0_ffn_q_w, L0_ffn_k_w, L0_ffn_v_w, L0_ffn_o_w, L0_ffn_sel_v_w, L0_ffn_sel_o_w, L0_ffn_route_scale)
    return x

_drawn_inputs = setup_inputs


def setup_inputs(seed=0):
    import zlib

    import numpy as np

    out = dict(_drawn_inputs(seed))
    spreads = {'L0_attn_a_bq': (0.0, 2.0),
     'L0_attn_a_bk': (0.0, 2.0),
     'L0_attn_a_bv': (0.0, 0.1),
     'L0_attn_a_bo': (0.0, 0.1),
     'L0_attn_b_g_ln': (1.0, 0.6)}
    factors = {'L0_attn_a_Wq': 8.0,
     'L0_attn_a_Wk': 8.0,
     'L0_attn_a_Wv': 8.0,
     'L0_attn_b_Wq': 8.0,
     'L0_attn_b_Wkv': 8.0,
     'L0_attn_b_Wo': 8.0}
    for name, (base, spread) in spreads.items():
        noise = np.random.default_rng([zlib.crc32(name.encode()), seed]).standard_normal(out[name].shape)
        drawn = base * np.exp(spread * noise) if base else spread * noise
        out[name] = jnp.asarray(drawn.astype(out[name].dtype))
    for name, factor in factors.items():
        out[name] = (out[name] * factor).astype(out[name].dtype)
    return out
```

```python
from contextlib import ExitStack
import math

import concourse.bass as bass
from concourse import mybir

F32 = mybir.dt.float32
F16 = mybir.dt.float16
BF16 = mybir.dt.bfloat16
ALU = mybir.AluOpType
ACT = mybir.ActivationFunctionType
AX = mybir.AxisListType

P = 128
T = 2048
NT = T // P
BLK = 512
NB = T // BLK
TPB = BLK // P
EPS = 1e-5

HA = 16
DA = P // HA
SCALE_A = DA ** -0.5
ROWS = 32
GROUPS = P // ROWS

HF = 8
EX = 8
SCALE_F = P ** -0.5
QUADS = HF * EX // 4

G_X = 64.0
G_W = 1024.0
G_Y = 128.0
G_C = 256.0
G_S = G_X * G_Y
ONE_K = 2048.0
G_M = G_S / ONE_K
LOG_P = 8 * math.log(2.0)


def hybrid_program(nc, x_in, Wq, bq, Wk, bk, Wv, bv, Wo, bo, g_ln, Wbq, Wbkv, Wbo,
                   q_w, k_w, v_w, o_w, sel_v_w, sel_o_w, route_scale, out):
    with ExitStack() as ctx:
        def sem(name):
            return ctx.enter_context(nc.semaphore(name))

        def sb(name, shape, dt=F32, stack=ctx):
            return stack.enter_context(nc.sbuf_tensor(name, shape, dt))

        x_res = sb("x_res", [P, NT, P])
        xn = sb("xn", [P, NT, P])
        xT = sb("xT", [P, T])
        stats = sb("stats", [P, NT, 6])
        mv = sb("mv", [P, NT, 2])
        lnv = sb("lnv", [P, 6, NT])
        ident = sb("ident", [P, P])
        ident16 = sb("ident16", [P, P], F16)
        ones = sb("ones", [P, P])
        selT = sb("selT", [P, P])
        rs_col = sb("rs_col", [P, 1])
        m_hi = sb("m_hi", [P, HF, P], F16)
        m_lo = sb("m_lo", [P, HF, P], F16)
        vw_hi = sb("vw_hi", [P, HF * EX, P], F16)
        vw_lo = sb("vw_lo", [P, HF * EX, P], F16)
        ow_hi = sb("ow_hi", [P, HF * EX, P], F16)
        ow_lo = sb("ow_lo", [P, HF * EX, P], F16)
        wbq = sb("wbq", [P, P])
        wbkv = sb("wbkv", [P, 2 * P])
        wbo = sb("wbo", [P, P])
        g_row = sb("g_row", [P, P])

        with ExitStack() as a:
            def sa(name, shape, dt=F32):
                return sb(name, shape, dt, a)
            w_nat = sa("w_nat", [P, 4, P])
            wT = sa("wT", [P, 4, P])
            sel_nat = sa("sel_nat", [P, P])
            bq_col = sa("bq_col", [P, 1])
            bkv_row = sa("bkv_row", [1, 2 * P])
            bo_row = sa("bo_row", [1, P])
            qk_w = sa("qk_w", [P, 2, HF, P])
            stage = sa("stage", [P, 4, 8 * P])
            cen = sa("cen", [P, 2, HF])
            head_mask = sa("head_mask", [P, P])
            qT = sa("qT", [P, T])
            q_exp = sa("q_exp", [P, 2, BLK])
            q_pos = sa("q_pos", [P, 2, BLK])
            k_exp = sa("k_exp", [P, 2, 2, P])
            k_pos = sa("k_pos", [P, 2, 2, P])
            k_nat = sa("k_nat", [P, NT, P])
            v_nat = sa("v_nat", [P, NT, P + 1])
            kv_sb = sa("kv_sb", [P, P])
            ks_sb = sa("ks_sb", [P, P])
            den = sa("den", [P, 2, BLK])
            rden = sa("rden", [P, 2, BLK])
            aT = sa("aT", [P, T])

        with ExitStack() as a:
            def sf(name, shape, dt=F32):
                return sb(name, shape, dt, a)
            x_hi = sf("x_hi", [P, T], F16)
            x_lo = sf("x_lo", [P, T], F16)
            xk_hi = sf("xk_hi", [P, T], F16)
            xk_lo = sf("xk_lo", [P, T], F16)
            gates = sf("gates", [P, NT, P])
            gp = sf("gp", [P, NT, P])
            gt = sf("gt", [P, 2, NT, P // 2])
            g1 = sf("g1", [P, 2, NT * HF])
            tie = sf("tie", [P, EX])
            y_hi = sf("y_hi", [P, NB, BLK], F16)
            y_lo = sf("y_lo", [P, NB, BLK], F16)
            mx = sf("mx", [P, TPB, NB])
            negm = sf("negm", [P, TPB])
            shift = sf("shift", [P, TPB], F16)
            p32 = sf("p32", [P, 4, BLK])
            p_lo = sf("p_lo", [P, 4, BLK], F16)
            va = sf("va", [P, 4, 2, P])
            v32 = sf("v32", [P, 4, P])
            v_hi = sf("v_hi", [P, 2, NT, P + 2], F16)
            v_lo = sf("v_lo", [P, 2, NT, P], F16)
            o_b = sf("o_b", [P, 2, P])
            c_raw = sf("c_raw", [P, TPB, P + 1])
            c_rec = sf("c_rec", [P, TPB])
            c32 = sf("c32", [P, TPB, P])
            c16 = sf("c16", [P, 2, TPB, P], F16)
            cT = sf("cT", [P, 2, BLK], F16)

        with ExitStack() as a:
            def sc(name, shape, dt=F32):
                return sb(name, shape, dt, a)
            xn2 = sc("xn2", [P, NT, P])
            wst = sc("wst", [P, 2, P // ROWS, P])
            s_hi = sc("s_hi", [P, 2, BLK], F16)
            s_lo = sc("s_lo", [P, 2, BLK], F16)
            s_ab = sc("s_ab", [P, 2, BLK], F16)
            k_st = sc("k_st", [P, GROUPS, T], F16)
            q_st = sc("q_st", [P, GROUPS, T], F16)
            q_hd = sc("q_hd", [P, 2, T], F16)
            row_mask = sc("row_mask", [P, 2, 2])
            row_one = sc("row_one", [P, 2])
            mk = sc("mk", [P, 4, 2 * DA * GROUPS])
            hd_mask = sc("hd_mask", [P, GROUPS])
            hd_mk = sc("hd_mk", [P, GROUPS, ROWS])
            dg = sc("dg", [P, 2, P], BF16)
            big_id = sc("big_id", [P, P], BF16)
            v17 = sc("v17", [P, NT, HA, 2 * DA + 2], F16)
            cmx = sc("cmx", [P, NT, NB])
            cneg = sc("cneg", [P, NT])
            csh = sc("csh", [P, NT], F16)
            p_c = sc("p_c", [P, 4, BLK])
            pl_c = sc("pl_c", [P, 4, BLK], F16)
            o_raw = sc("o_raw", [P, NT, 2 * DA + 1])
            o_sum = sc("o_sum", [P, NT, DA])
            c_rec2 = sc("c_rec2", [P, NT])
            o_nat = sc("o_nat", [P, NT, P])
            oT = sc("oT", [P, T])

        B = [ctx.enter_context(nc.psum_tensor(f"bank{i}", [P, BLK], F32)) for i in range(8)]
        ds = bass.ds

        def quarter(i):
            return i >> 2 if isinstance(i, int) else (i >> 2).with_bounds(min_val=i.min_val >> 2, max_val=i.max_val >> 2)

        ld_x, ld_w, ld_qk, ld_b, ld_c = (sem("ld_" + n) for n in ("x", "w", "qk", "b", "c"))
        ld_e = [sem(f"ld_e{n}") for n in range(4)]
        e_hi, e_lo = sem("e_hi"), sem("e_lo")
        zeroed = sem("zeroed")
        consts = sem("consts")
        vconst = sem("vconst")
        qk_cen = sem("qk_cen")
        out_done = sem("out_done")
        a_s = {n: sem("a_" + n) for n in (
            "wt_ps", "wt", "sel_ps", "sel", "xt_ps", "xt", "m_ps", "m_hi", "m_lo",
            "q_ps", "q_exp", "q_pos", "q", "k_ps", "k_exp", "v", "k_pos", "k",
            "kv_ps", "kv", "cen", "nd_ps", "den", "rden", "at", "y_ps", "res")}
        ln_names = ("stats", "mv", "var", "root", "chain", "xn")
        ln_s = {n: sem("ln_" + n) for n in ln_names}
        f_s = [{n: sem(f"f{k}_{n}") for n in (
            "xt_ps", "xt", "x_hi", "x_lo", "xk", "lg_ps", "lg", "choice", "gates", "ones",
            "y_ps", "y_hi", "y_lo", "mx_ps", "mx", "negm", "shift", "sh_ps", "row",
            "vo_ps", "gated", "vsum", "v_hi", "v_lo", "st_ps", "p", "p_lo", "pv_ps",
            "c_raw", "c_rec", "c32", "c_hi", "c_lo", "ct_ps", "ct", "res")} for k in range(2)]
        c_s = {n: sem("c_" + n) for n in (
            "zero", "mask", "xg", "xt_ps", "xt", "wst", "st_ps", "s_hi", "s_lo", "s_a", "stack",
            "v_ps", "v_hi", "v_lo", "qh", "mx_ps", "mx", "neg", "shift", "sh_ps", "row", "s_ps", "p",
            "lo_v", "lo_g", "pv_ps", "raw", "rec", "o", "ot_ps", "ot", "y_ps", "res")}

        block = ctx.enter_context(nc.Block())

        def top_half(x):
            return x.bitcast(BF16)[:, 1::2]

        def norm_vector(v, k, src, dst):
            s = ln_s
            for t in range(NT):
                v.bn_stats(stats[:, t, :], src[:, t, :]).then_inc(s["stats"], 1)
            for t in range(NT):
                v.wait_ge(s["stats"], NT * k + t + 1)
                v.bn_aggr(mv[:, t, :], stats[:, t, :]).then_inc(s["mv"], 1)
            v.wait_ge(s["mv"], NT * (k + 1))
            v.tensor_scalar(lnv[:, 0, :], mv[:, :, 1], EPS, None, ALU.add).then_inc(s["var"], 1)
            v.wait_ge(s["var"], k + 1)
            v.wait_ge(s["root"], k + 1)
            v.reciprocal(lnv[:, 2, :], lnv[:, 1, :]).then_inc(s["chain"], 1)
            v.wait_ge(s["chain"], 5 * k + 1)
            v.tensor_tensor(lnv[:, 3, :], lnv[:, 2, :], lnv[:, 2, :], ALU.mult).then_inc(s["chain"], 1)
            v.wait_ge(s["chain"], 5 * k + 2)
            v.tensor_tensor(lnv[:, 4, :], lnv[:, 3, :], lnv[:, 0, :], ALU.mult).then_inc(s["chain"], 1)
            v.wait_ge(s["chain"], 5 * k + 3)
            v.tensor_scalar(lnv[:, 3, :], lnv[:, 4, :], -0.5, 1.5, ALU.mult, ALU.add).then_inc(s["chain"], 1)
            v.wait_ge(s["chain"], 5 * k + 4)
            v.tensor_tensor(lnv[:, 5, :], lnv[:, 3, :], lnv[:, 2, :], ALU.mult).then_inc(s["chain"], 1)
            v.wait_ge(s["chain"], 5 * k + 5)
            for t in range(NT):
                v.tensor_scalar(dst[:, t, :], src[:, t, :], mv[:, t, 0:1], lnv[:, 5, t:t + 1],
                                ALU.subtract, ALU.mult).then_inc(s["xn"], 1)

        def norm_scalar(a, k):
            a.wait_ge(ln_s["var"], k + 1)
            a.activation(lnv[:, 1, :], lnv[:, 0, :], ACT.Sqrt).then_inc(ln_s["root"], 1)

        def linear_tensor(pe):
            s = a_s
            pe.wait_ge(consts, 2)
            pe.wait_ge(ld_w, 16 * 4)
            for w in range(4):
                mm = pe.transpose(B[0][:, w * P:(w + 1) * P], w_nat[:, w, :], ident[:, :])
            mm.then_inc(s["wt_ps"], 1)
            pe.wait_ge(ld_b, 16 * 8)
            pe.transpose(B[1][:, 0:P], sel_nat[:, :], ident[:, :]).then_inc(s["sel_ps"], 1)
            for b in range(NB):
                pe.wait_ge(ln_s["xn"], TPB * (b + 1))
                for t in range(TPB):
                    mm = pe.transpose(B[2 + b][:, t * P:(t + 1) * P], xn[:, b * TPB + t, :], ident[:, :])
                mm.then_inc(s["xt_ps"], 1)
            for g in range(2):
                pe.wait_ge(qk_cen, 2 * HF // 2 * (g + 1))
                for h in range(HF // 2):
                    hh = g * HF // 2 + h
                    mm = pe.matmul(B[6 + g][:, h * P:(h + 1) * P], qk_w[:, 0, hh, :], qk_w[:, 1, hh, :],
                                   start=True, stop=True)
                mm.then_inc(s["m_ps"], 1)
            pe.wait_ge(s["wt"], 1)
            pe.wait_ge(s["sel"], 1)
            for b in range(NB):
                pe.wait_ge(s["xt"], b + 1)
                if b >= 2:
                    pe.wait_ge(s["q_pos"], b - 1)
                pe.matmul(B[b % 2][:, :], wT[:, 0, :], xT[:, b * BLK:(b + 1) * BLK],
                          start=True, stop=True).then_inc(s["q_ps"], 1)
            pe.wait_ge(consts, 3)
            for n in range(NT // 2):
                bank = B[2 + n % 2]
                pe.wait_ge(s["xt"], NB)
                if n >= 2:
                    pe.wait_ge(s["v"], n - 1)
                for r in range(2):
                    t = 2 * n + r
                    o = bank[:, r * 2 * P:(r + 1) * 2 * P]
                    pe.matmul(o, ones[0:1, :], bkv_row[:, :], start=True, stop=False)
                    mm = pe.matmul(o, xT[:, t * P:(t + 1) * P],
                                   wT[:, 1:3, :].rearrange("p a b -> p (a b)"), start=False, stop=True)
                mm.then_inc(s["k_ps"], 1)
            pe.wait_ge(vconst, 1)
            for t in range(NT):
                if t % 2 == 0:
                    pe.wait_ge(s["k"], t // 2 + 1)
                    pe.wait_ge(s["v"], t // 2 + 1)
                mm = pe.matmul(B[4][:, 0:P + 1], k_nat[:, t, :], v_nat[:, t, :],
                               start=(t == 0), stop=(t == NT - 1))
            mm.then_inc(s["kv_ps"], 1)
            pe.wait_ge(s["kv"], 2)
            pe.wait_ge(s["q"], NB)
            for b in range(NB):
                if b >= 2:
                    pe.wait_ge(s["at"], b - 1)
                pe.matmul(B[b % 2][:, :], ks_sb[:, :], qT[:, b * BLK:(b + 1) * BLK], start=True, stop=True)
                pe.matmul(B[2 + b % 2][:, :], kv_sb[:, :], qT[:, b * BLK:(b + 1) * BLK],
                          start=True, stop=True).then_inc(s["nd_ps"], 1)
            pe.wait_ge(s["m_lo"], 2)
            for b in range(NB):
                pe.wait_ge(s["at"], b + 1)
                for t in range(TPB):
                    o = B[4 + b][:, t * P:(t + 1) * P]
                    pe.matmul(o, ones[0:1, :], bo_row[:, :], start=True, stop=False)
                    mm = pe.matmul(o, aT[:, (b * TPB + t) * P:(b * TPB + t + 1) * P], wT[:, 3, :],
                                   start=False, stop=True)
                mm.then_inc(s["y_ps"], 1)

        def linear_scalar(a):
            s = a_s
            norm_scalar(a, 0)
            a.wait_ge(s["wt_ps"], 1)
            a.activation(wT[:, :, :].rearrange("p a b -> p (a b)"), B[0][:, :], ACT.Copy).then_inc(s["wt"], 1)
            a.wait_ge(s["sel_ps"], 1)
            a.activation(selT[:, :], B[1][:, 0:P], ACT.Copy).then_inc(s["sel"], 1)
            for b in range(NB):
                a.wait_ge(s["xt_ps"], b + 1)
                a.activation(xT[:, b * BLK:(b + 1) * BLK], B[2 + b][:, :], ACT.Copy).then_inc(s["xt"], 1)
            for g in range(2):
                a.wait_ge(s["m_ps"], g + 1)
                a.activation(m_hi[:, 4 * g:4 * g + 4, :].rearrange("p a b -> p (a b)"), B[6 + g][:, :],
                             ACT.Copy, scale=SCALE_F * G_W).then_inc(s["m_hi"], 1)
            for b in range(NB):
                a.wait_ge(s["q_ps"], b + 1)
                if b >= 2:
                    a.wait_ge(s["q"], b - 1)
                a.activation(q_exp[:, b % 2, :], B[b % 2][:, :], ACT.Exp,
                             bias=bq_col[:, 0:1]).then_inc(s["q_exp"], 1)
                a.activation(q_pos[:, b % 2, :], B[b % 2][:, :], ACT.Relu,
                             bias=bq_col[:, 0:1]).then_inc(s["q_pos"], 1)
            a.wait_ge(vconst, 1)
            for n in range(NT // 2):
                ps = B[2 + n % 2][:, :].rearrange("p (r a c) -> p r a c", r=2, a=2)
                a.wait_ge(s["k_ps"], n + 1)
                if n >= 2:
                    a.wait_ge(s["k"], n - 1)
                a.activation(k_exp[:, n % 2, :, :], ps[:, :, 0, :], ACT.Exp).then_inc(s["k_exp"], 1)
                a.activation(k_pos[:, n % 2, :, :], ps[:, :, 0, :], ACT.Relu).then_inc(s["k_pos"], 1)
                a.activation(v_nat[:, 2 * n:2 * n + 2, 0:P], ps[:, :, 1, :], ACT.Copy).then_inc(s["v"], 1)
            experts_scalar(a)

        def linear_vector(v):
            s = a_s
            v.memset(v_nat[:, :, P:P + 1], 1.0).then_inc(vconst, 1)
            v.wait_ge(ld_x, 16)
            norm_vector(v, 0, x_res, xn)
            v.wait_ge(ld_qk, 32)
            v.tensor_copy(cen[:, :, :], qk_w[:, :, :, 0]).then_inc(s["cen"], 1)
            v.wait_ge(s["cen"], 1)
            for h in range(HF):
                for w in range(2):
                    v.tensor_scalar(qk_w[:, w, h, :], qk_w[:, w, h, :], cen[:, w, h:h + 1], None,
                                    ALU.subtract).then_inc(qk_cen, 1)
            for g in range(2):
                v.wait_ge(s["m_hi"], g + 1)
                v.scalar_tensor_tensor(m_lo[:, 4 * g:4 * g + 4, :].rearrange("p a b -> p (a b)"),
                                       B[6 + g][:, :], SCALE_F * G_W,
                                       m_hi[:, 4 * g:4 * g + 4, :].rearrange("p a b -> p (a b)"),
                                       ALU.mult, ALU.subtract).then_inc(s["m_lo"], 1)
            for b in range(NB):
                v.wait_ge(s["q_pos"], b + 1)
                v.scalar_tensor_tensor(qT[:, b * BLK:(b + 1) * BLK], q_exp[:, b % 2, :], 1.0,
                                       q_pos[:, b % 2, :], ALU.min, ALU.add).then_inc(s["q"], 1)
            for n in range(NT // 2):
                v.wait_ge(s["k_pos"], n + 1)
                v.scalar_tensor_tensor(k_nat[:, 2 * n:2 * n + 2, :].rearrange("p a b -> p (a b)"),
                                       k_exp[:, n % 2, :, :].rearrange("p a b -> p (a b)"), 1.0,
                                       k_pos[:, n % 2, :, :].rearrange("p a b -> p (a b)"),
                                       ALU.min, ALU.add).then_inc(s["k"], 1)
            v.wait_ge(s["kv_ps"], 1)
            v.wait_ge(consts, 5)
            v.tensor_tensor(kv_sb[:, :], B[4][:, 0:P], head_mask[:, :], ALU.mult).then_inc(s["kv"], 1)
            v.tensor_scalar(ks_sb[:, :], head_mask[:, :], B[4][:, P:P + 1], None, ALU.mult).then_inc(s["kv"], 1)
            for b in range(NB):
                v.wait_ge(s["nd_ps"], b + 1)
                v.tensor_scalar(den[:, b % 2, :], B[b % 2][:, :], 1e-6, None, ALU.max).then_inc(s["den"], 1)
                v.wait_ge(s["den"], b + 1)
                v.reciprocal(rden[:, b % 2, :], den[:, b % 2, :]).then_inc(s["rden"], 1)
                v.wait_ge(s["rden"], b + 1)
                v.tensor_tensor(aT[:, b * BLK:(b + 1) * BLK], B[2 + b % 2][:, :], rden[:, b % 2, :],
                                ALU.mult).then_inc(s["at"], 1)
            for b in range(NB):
                v.wait_ge(s["y_ps"], b + 1)
                xr = x_res[:, b * TPB:(b + 1) * TPB, :].rearrange("p a b -> p (a b)")
                v.tensor_tensor(xr, B[4 + b][:, :], xr, ALU.add).then_inc(s["res"], 1)
            experts_vector(v)

        def expert_parts(n):
            hi, lo = ((vw_hi, vw_lo), (ow_hi, ow_lo))[n // HF]
            h = n % HF
            return (x[:, h * EX:(h + 1) * EX, :].rearrange("p a b -> p (a b)") for x in (hi, lo))

        def experts_scalar(a):
            for n in range(2 * HF):
                hi, _ = expert_parts(n)
                a.wait_ge(ld_e[n % 4], 16 * (n // 4 + 1))
                a.activation(hi, stage[:, n % 4, :], ACT.Copy, scale=G_W).then_inc(e_hi, 1)

        def experts_vector(v):
            for n in range(2 * HF):
                hi, lo = expert_parts(n)
                v.wait_ge(e_hi, n + 1)
                v.scalar_tensor_tensor(lo, stage[:, n % 4, :], G_W, hi,
                                       ALU.mult, ALU.subtract).then_inc(e_lo, 1)

        def loads(sp):
            sp.dma_start(x_res[:, :, :], x_in.rearrange("b (t p) c -> p (b t) c", p=P)).then_inc(ld_x, 16)
            for w, src in enumerate((Wq, Wk, Wv, Wo)):
                sp.dma_start(w_nat[:, w, :], src).then_inc(ld_w, 16)
            col = lambda x: x.rearrange("(p a) -> p a", a=1)
            row = lambda x: x.rearrange("(a c) -> a c", a=1)
            sp.dma_start(bq_col[:, :], col(bq)).then_inc(ld_b, 16)
            sp.dma_start(bkv_row[:, 0:P], row(bk)).then_inc(ld_b, 16)
            sp.dma_start(bkv_row[:, P:2 * P], row(bv)).then_inc(ld_b, 16)
            sp.dma_start(bo_row[:, :], row(bo)).then_inc(ld_b, 16)
            sp.dma_start(sel_nat[0:P // 2, :], sel_v_w).then_inc(ld_b, 16)
            sp.dma_start(sel_nat[P // 2:P, :], sel_o_w).then_inc(ld_b, 16)
            sp.dma_start(rs_col[:, :], row(route_scale).broadcast_to([P, 1])).then_inc(ld_b, 16)
            sp.dma_start(g_row[:, :], row(g_ln).broadcast_to([P, P])).then_inc(ld_b, 16)
            sp.dma_start(qk_w[:, 0, :, :], q_w.rearrange("(h p) d -> p h d", p=P)).then_inc(ld_qk, 16)
            sp.dma_start(qk_w[:, 1, :, :], k_w.rearrange("(h p) d -> p h d", p=P)).then_inc(ld_qk, 16)
            sp.dma_start(wbq[:, :], Wbq).then_inc(ld_c, 16)
            sp.dma_start(wbkv[:, :], Wbkv).then_inc(ld_c, 16)
            sp.dma_start(wbo[:, :], Wbo).then_inc(ld_c, 16)
            for n in range(2 * HF):
                src, h = (v_w, o_w)[n // HF], n % HF
                if n >= 4:
                    sp.wait_ge(e_lo, n - 3)
                sp.dma_start(stage[:, n % 4, :].rearrange("p (e c) -> p e c", e=EX),
                             src[h * EX:(h + 1) * EX].rearrange("e p c -> p e c")).then_inc(ld_e[n % 4], 16)

        def constants_pool(g):
            g.memset(ident[:, :], 0.0).then_inc(zeroed, 1)
            g.memset(head_mask[:, :], 1.0).then_inc(zeroed, 1)
            g.wait_ge(zeroed, 1)
            g.affine_select(out=ident[:, :], in_=ident[:, :], compare_op=ALU.not_equal, fill=1.0,
                            base=0, pattern=[[-1, P]], channel_multiplier=1).then_inc(consts, 1)
            g.wait_ge(consts, 1)
            g.tensor_copy(ident16[:, :], ident[:, :]).then_inc(consts, 1)
            g.memset(ones[:, :], 1.0).then_inc(consts, 1)
            hm = head_mask[:, :].rearrange("p (h c) -> p h c", c=DA)
            g.wait_ge(zeroed, 2)
            g.affine_select(out=hm, in_=hm, compare_op=ALU.is_ge, fill=0.0, base=0,
                            pattern=[[-DA, HA], [0, DA]], channel_multiplier=1).then_inc(consts, 1)
            g.wait_ge(consts, 4)
            g.affine_select(out=hm, in_=hm, compare_op=ALU.is_ge, fill=0.0, base=DA - 1,
                            pattern=[[DA, HA], [0, DA]], channel_multiplier=-1).then_inc(consts, 1)

        NI = HF * NB
        EXTRA_MX = (3, 6, 9)
        MX_AT = [[] for _ in range(NT)]
        for u in range(NT):
            MX_AT[[k for k in range(13) for _ in range(1 + (k in EXTRA_MX))][u]].append(u)

        def parts(i):
            lo, hi = (i, i) if isinstance(i, int) else (i.min_val, i.max_val)
            return dict(att=hi < NI, mx=hi + 1 < NI, y=hi + 2 < NI, v=hi < NI - NB, o=lo >= 1)

        def unit_base(i):
            if isinstance(i, int) and i == 0:
                return 2 * NT
            lo = i if isinstance(i, int) else i.min_val
            if lo < NI - NB:
                return i * 16 + (2 * NT + 8 - 16)
            return i * 8 + (2 * NT + 8 - 16 + 8 * (NI - NB))

        def over_iterations(eng, body):
            body(0)
            with eng.Fori(1, NI - NB) as i:
                body(i)
            with eng.Fori(NI - NB, NI - 2) as i:
                body(i)
            body(NI - 2)
            body(NI - 1)
            body(NI)

        def switch_tensor(pe, k):
            s = f_s[k]

            def queries(j):
                h, b = quarter(j), j & 3
                xs = [x[:, ds(b * BLK, BLK)] for x in (x_hi, x_lo)]
                pe.matmul(B[7][:, :], m_hi[:, h, :], xs[0], start=True, stop=False)
                pe.matmul(B[7][:, :], m_hi[:, h, :], xs[1], start=False, stop=False)
                pe.matmul(B[7][:, :], m_lo[:, h, :], xs[0], start=False, stop=True).then_inc(s["y_ps"], 1)

            def max_unit(j, u):
                t, kb = u // NB, u % NB
                if u == 0:
                    pe.wait_ge(s["y_hi"], j + 1)
                if not (isinstance(j, int) and 16 * j + u == 0):
                    pe.wait_ge(s["mx"], j * 16 + u)
                pe.matmul(B[4][:, :], y_hi[:, j & 3, t * P:(t + 1) * P], xk_hi[:, kb * BLK:(kb + 1) * BLK],
                          start=True, stop=True).then_inc(s["mx_ps"], 1)

            def shift_rows(j):
                pe.wait_ge(s["shift"], j + 1)
                for t in range(TPB):
                    mm = pe.matmul(B[7][0:1, t * P:(t + 1) * P], shift[:, t:t + 1], ident16[:, :],
                                   start=True, stop=True)
                mm.then_inc(s["sh_ps"], 1)

            def scores(j, kt):
                if kt == 0:
                    pe.wait_ge(s["row"], j + 1)
                    pe.wait_ge(s["y_lo"], j + 1)
                if not (isinstance(j, int) and 16 * j + kt < 2):
                    pe.wait_ge(s["p"], j * 16 + (kt - 1))
                o, ks, b = B[kt % 2][:, :], slice(kt * P, (kt + 1) * P), j & 3
                pe.matmul(o, xk_hi[:, ks], y_hi[:, b, :], start=True, stop=False)
                pe.matmul(o, xk_hi[:, ks], y_lo[:, b, :], start=False, stop=False)
                pe.matmul(o, xk_lo[:, ks], y_hi[:, b, :], start=False, stop=True).then_inc(s["st_ps"], 1)

            def context(i, kt):
                n = i * 16 + kt
                if kt == 0:
                    if not (isinstance(i, int) and i == 0):
                        pe.wait_ge(s["c_raw"], i * 2)
                    pe.wait_ge(s["v_hi"], quarter(i) * NT + NT)
                    pe.wait_ge(s["v_lo"], quarter(i) * NT + NT)
                pe.wait_ge(s["p_lo"], n + 1)
                slot = quarter(i) & 1
                vh = v_hi[:, slot, kt, 0:P + 1]
                vl = v_lo[:, slot, kt, :]
                for t in range(TPB):
                    o = B[2 + t // 2][:, (t % 2) * (P + 1):(t % 2 + 1) * (P + 1)]
                    ph = top_half(p32[:, kt % 4, t * P:(t + 1) * P])
                    pl = p_lo[:, kt % 4, t * P:(t + 1) * P]
                    pe.matmul(o, ph, vh, start=(kt == 0 and t % 2 == 0), stop=False, skip_group_check=True)
                    pe.matmul(o[:, 0:P], ph, vl, start=False, stop=False, skip_group_check=True)
                    mm = pe.matmul(o, pl, vh, start=False, stop=(kt == NT - 1), skip_group_check=True)
                mm.then_inc(s["pv_ps"], 1)

            def unit(n, par, parts3, w_hi, w_lo, first):
                if not first:
                    pe.wait_ge(s["gated"], n * 4 - 4)
                hi, lo = parts3
                o = B[5 + par][:, :]
                wh, wl = (w.rearrange("p a b -> p (a b)") for w in (w_hi, w_lo))
                pe.matmul(o, hi, wh, start=True, stop=False)
                pe.matmul(o, hi, wl, start=False, stop=False)
                pe.matmul(o, lo, wh, start=False, stop=True).then_inc(s["vo_ps"], 1)

            def v_unit(n, par, h, t, q, first=False):
                ts = ds(t * P, P)
                ws = ds(h * EX + 4 * q, 4)
                unit(n, par, (x_hi[:, ts], x_lo[:, ts]), vw_hi[:, ws, :], vw_lo[:, ws, :], first)

            def o_unit(n, par, h, t, q):
                ts = slice(t * P, (t + 1) * P)
                ws = ds(h * EX + 4 * q, 4)
                unit(n, par, (cT[:, 0, ts], cT[:, 1, ts]), ow_hi[:, ws, :], ow_lo[:, ws, :], False)

            def turn_context(i):
                if parts(i)["att"]:
                    pe.wait_ge(s["row"], i + 1)
                pe.wait_ge(s["c_hi"], i)
                pe.wait_ge(s["c_lo"], i)
                turned = B[7][:, :].bitcast(F16)
                for w in range(2):
                    for t in range(TPB):
                        mm = pe.transpose(turned[:, w * BLK + t * P:w * BLK + (t + 1) * P],
                                          c16[:, w, t, :], ident16[:, :])
                mm.then_inc(s["ct_ps"], 1)

            def body(i):
                f = parts(i)
                ub = unit_base(i)
                for kt in range(NT):
                    if f["mx"] and MX_AT[kt]:
                        max_unit(i + 1, MX_AT[kt][0])
                    if f["v"] and kt < 8:
                        v_unit(ub + kt, kt % 2, quarter(i) + 1, (i & 3) * TPB + kt // 2, kt % 2)
                    if f["o"] and kt == 3:
                        turn_context(i)
                    if f["o"] and kt >= 8:
                        if kt == 8:
                            pe.wait_ge(s["ct"], i)
                        j = i - 1
                        m = kt - 8
                        o_unit(ub + (8 if f["v"] else 0) + m, m % 2, quarter(j), m // 2, m % 2)
                    if f["y"] and kt == 8:
                        if f["o"]:
                            pe.wait_ge(s["ct"], i)
                        else:
                            pe.wait_ge(s["row"], i + 1)
                        queries(i + 2)
                    if f["mx"] and kt == 13:
                        if f["y"]:
                            pe.wait_ge(s["y_lo"], i + 3)
                        else:
                            pe.wait_ge(s["ct"], i)
                        shift_rows(i + 1)
                    if f["att"]:
                        context(i, kt)
                        if f["mx"] and len(MX_AT[kt]) > 1:
                            max_unit(i + 1, MX_AT[kt][1])
                        if kt < NT - 2:
                            scores(i, kt + 2)
                        elif f["mx"]:
                            scores(i + 1, kt + 2 - NT)

            pe.wait_ge(ln_s["xn"], NT * (2 + 3 * k))
            for b in range(NB):
                for t in range(TPB):
                    mm = pe.transpose(B[b][:, t * P:(t + 1) * P], xn[:, b * TPB + t, :], ident[:, :])
                mm.then_inc(s["xt_ps"], 1)
            for b in range(NB):
                pe.wait_ge(s["xt"], b + 1)
                for t in range(TPB):
                    tt = b * TPB + t
                    mm = pe.matmul(B[4 + b][:, t * P:(t + 1) * P], xT[:, tt * P:(tt + 1) * P], selT[:, :],
                                   start=True, stop=True)
                mm.then_inc(s["lg_ps"], 1)
            pe.wait_ge(s["lg"], NB)
            pe.wait_ge(s["x_lo"], NB)
            queries(0)
            pe.wait_ge(s["y_lo"], 1)
            queries(1)
            pe.wait_ge(s["xk"], 4)
            for u in range(NT):
                max_unit(0, u)
            pe.wait_ge(s["y_lo"], 2)
            shift_rows(0)
            scores(0, 0)
            scores(0, 1)
            if k == 0:
                pe.wait_ge(e_lo, 2 * HF)
            for n in range(2 * NT):
                v_unit(n, n % 2, 0, n // 2, n % 2, first=n < 2)
            over_iterations(pe, body)

        def switch_scalar(a, k):
            s = f_s[k]
            norm_scalar(a, 1 + 3 * k)
            for b in range(NB):
                bs = slice(b * BLK, (b + 1) * BLK)
                a.wait_ge(s["xt_ps"], b + 1)
                a.activation(xT[:, bs], B[b][:, :], ACT.Copy).then_inc(s["xt"], 1)
                a.activation(x_hi[:, bs], B[b][:, :], ACT.Copy, scale=G_X).then_inc(s["x_hi"], 1)
            for b in range(NB):
                a.wait_ge(s["lg_ps"], b + 1)
                a.activation(gp[:, b * TPB:(b + 1) * TPB, :].rearrange("p a b -> p (a b)"), B[4 + b][:, :],
                             ACT.Exp, scale=-1.0).then_inc(s["lg"], 1)

            def queries(j):
                a.wait_ge(s["y_ps"], j + 1)
                a.activation(y_hi[:, j & 3, :], B[7][:, :], ACT.Copy,
                             scale=G_Y / (G_X * G_W)).then_inc(s["y_hi"], 1)

            def row(j):
                a.wait_ge(s["sh_ps"], j + 1)
                a.activation(y_hi[0:1, j & 3, :], B[7][0:1, :], ACT.Copy).then_inc(s["row"], 1)

            def exps(j, kt):
                n = j * 16 + kt
                a.wait_ge(s["st_ps"], n + 1)
                early = isinstance(j, int) and j == 0
                if not (early and kt < 4):
                    a.wait_ge(s["pv_ps"], n - 3)
                a.activation(p32[:, kt % 4, :], B[kt % 2][:, :], ACT.Exp,
                             scale=1.0 / G_S).then_inc(s["p"], 1)

            def v_part(h, t, tt, n):
                a.wait_ge(s["vsum"], n + 1)
                a.activation(v_hi[:, h & 1, t, 0:P], v32[:, tt, :], ACT.Copy).then_inc(s["v_hi"], 1)

            def body(i):
                f = parts(i)
                for kt in range(NT):
                    if f["att"] and kt == NT - 1:
                        a.wait_ge(s["pv_ps"], i * 16 + 16)
                        if f["o"]:
                            a.wait_ge(s["c32"], i)
                        for t in range(2):
                            a.activation(c_raw[:, 2 * t:2 * t + 2, :].rearrange("p a b -> p (a b)"),
                                         B[2 + t][:, 0:2 * (P + 1)], ACT.Copy).then_inc(s["c_raw"], 1)
                    if f["mx"] and kt == 13:
                        row(i + 1)
                    if f["att"]:
                        if kt < NT - 2:
                            exps(i, kt + 2)
                        elif f["mx"]:
                            exps(i + 1, kt + 2 - NT)
                    if f["o"] and kt == 1:
                        a.wait_ge(s["c32"], i)
                        a.activation(c16[:, 0, :, :].rearrange("p a b -> p (a b)"),
                                     c32[:, :, :].rearrange("p a b -> p (a b)"), ACT.Copy).then_inc(s["c_hi"], 1)
                    if f["o"] and kt == 4:
                        a.wait_ge(s["ct_ps"], i)
                        a.activation(cT[:, :, :].rearrange("p a b -> p (a b)"),
                                     B[7][:, :].bitcast(F16), ACT.Copy).then_inc(s["ct"], 1)
                    if f["v"] and kt in (2, 4, 6, 8):
                        tt = kt // 2 - 1
                        v_part(quarter(i) + 1, (i & 3) * TPB + tt, tt, i * TPB + (NT + tt))
                    if f["y"] and kt == 8:
                        queries(i + 2)

            queries(0)
            queries(1)
            row(0)
            exps(0, 0)
            exps(0, 1)
            a.wait_ge(s["ones"], 1)
            for t in range(NT):
                v_part(0, t, t % TPB, t)
            over_iterations(a, body)

        def switch_pool(g, k):
            s = f_s[k]

            def p_part(j, kt):
                g.wait_ge(s["p"], j * 16 + (kt + 1))
                if not (isinstance(j, int) and j == 0 and kt < 4):
                    g.wait_ge(s["pv_ps"], j * 16 + (kt - 3))
                g.tensor_tensor(p_lo[:, kt % 4, :], p32[:, kt % 4, :], top_half(p32[:, kt % 4, :]),
                                ALU.subtract).then_inc(s["p_lo"], 1)

            def v_part(h, t, tt, n):
                g.wait_ge(s["v_hi"], n + 1)
                g.tensor_tensor(v_lo[:, h & 1, t, :], v32[:, tt, :], v_hi[:, h & 1, t, 0:P],
                                ALU.subtract).then_inc(s["v_lo"], 1)

            def body(i):
                f = parts(i)
                for kt in range(NT):
                    if f["att"]:
                        if kt < NT - 2:
                            p_part(i, kt + 2)
                        elif f["mx"]:
                            p_part(i + 1, kt + 2 - NT)
                    if f["v"] and kt in (3, 5, 7, 9):
                        tt = kt // 2 - 1
                        v_part(quarter(i) + 1, (i & 3) * TPB + tt, tt, i * TPB + (NT + tt))

            p_part(0, 0)
            p_part(0, 1)
            for t in range(NT):
                v_part(0, t, t % TPB, t)
            over_iterations(g, body)

        def switch_vector(v, k):
            s = f_s[k]
            prev = a_s["res"] if k == 0 else c_s["res"]
            v.wait_ge(prev, NB)
            norm_vector(v, 1 + 3 * k, x_res, xn)
            for b in range(NB):
                bs = slice(b * BLK, (b + 1) * BLK)
                v.wait_ge(s["x_hi"], b + 1)
                v.scalar_tensor_tensor(x_lo[:, bs], B[b][:, :], G_X, x_hi[:, bs],
                                       ALU.mult, ALU.subtract).then_inc(s["x_lo"], 1)
            v.wait_ge(s["x_lo"], NB)
            v.tensor_copy(xk_hi[:, :], x_hi[:, :]).then_inc(s["xk"], 1)
            v.tensor_copy(xk_lo[:, :], x_lo[:, :]).then_inc(s["xk"], 1)
            v.wait_ge(s["xk"], 2)
            v.memset(xk_hi[0:1, :], ONE_K).then_inc(s["xk"], 1)
            v.memset(xk_lo[0:1, :], 0.0).then_inc(s["xk"], 1)
            v.memset(v_hi[:, :, :, P:P + 1], G_X / G_C).then_inc(s["ones"], 1)
            for e in range(EX):
                v.memset(tie[:, e:e + 1], float(EX - e)).then_inc(s["choice"], 1)
            chain = [EX]

            def link(ins):
                ins.then_inc(s["choice"], 1)
                chain[0] += 1
                v.wait_ge(s["choice"], chain[0])

            def queries(j):
                v.wait_ge(s["y_hi"], j + 1)
                v.scalar_tensor_tensor(y_lo[:, j & 3, :], B[7][:, :], G_Y / (G_X * G_W), y_hi[:, j & 3, :],
                                       ALU.mult, ALU.subtract).then_inc(s["y_lo"], 1)

            def max_unit(j, u):
                v.wait_ge(s["mx_ps"], j * 16 + (u + 1))
                v.tensor_reduce(mx[:, u // NB, u % NB:u % NB + 1], B[4][:, :], AX.X, ALU.max).then_inc(s["mx"], 1)

            def shift_of(j):
                v.wait_ge(s["mx"], j * 16 + 16)
                v.tensor_reduce(negm[:, :], mx[:, :, :], AX.X, ALU.max, negate=True).then_inc(s["negm"], 1)
                v.wait_ge(s["negm"], j + 1)
                v.tensor_scalar(shift[:, :], negm[:, :], G_M / G_S, G_M * LOG_P,
                                ALU.mult, ALU.add).then_inc(s["shift"], 1)

            def choose(half, gain):
                cs = slice(half * 64, half * 64 + 64)
                prob = gp[:, :, cs]
                g_out = gates[:, :, cs]
                four = lambda x: x.rearrange("p t (h e) -> p t h e", e=EX)
                flat = lambda x: x.rearrange("p t c -> p (t c)")
                one = lambda n: g1[:, n, :]
                over = lambda n: g1[:, n, :].rearrange("p (t h a) -> p t h a", h=HF, a=1).broadcast_to([P, NT, HF, EX])
                ties = tie[:, :].rearrange("p (a b e) -> p a b e", a=1, b=1).broadcast_to([P, NT, HF, EX])
                A, C = gt[:, 0], gt[:, 1]
                link(v.tensor_reduce(one(0), four(prob), AX.X, ALU.max))
                link(v.tensor_tensor(four(A), four(prob), over(0), ALU.is_equal))
                link(v.tensor_tensor(four(C), four(A), ties, ALU.mult))
                link(v.tensor_reduce(one(1), four(C), AX.X, ALU.max))
                link(v.tensor_tensor(four(A), four(C), over(1), ALU.is_equal))
                link(v.scalar_tensor_tensor(C, A, -4.0, prob, ALU.mult, ALU.add))
                link(v.tensor_reduce(one(0), four(C), AX.X, ALU.max))
                link(v.tensor_tensor(four(g_out), four(C), over(0), ALU.is_equal))
                link(v.tensor_tensor(four(C), four(g_out), ties, ALU.mult))
                link(v.tensor_reduce(one(1), four(C), AX.X, ALU.max))
                link(v.tensor_tensor(four(g_out), four(C), over(1), ALU.is_equal))
                link(v.tensor_tensor(C, A, g_out, ALU.add))
                link(v.tensor_tensor(A, C, prob, ALU.mult))
                link(v.tensor_reduce(one(0), four(A), AX.X, ALU.add))
                link(v.tensor_scalar(one(1), one(0), 1e-9, None, ALU.max))
                link(v.reciprocal(one(0), one(1)))
                link(v.tensor_scalar(one(1), one(0), rs_col[:, 0:1], gain, ALU.mult, ALU.mult))
                link(v.tensor_tensor(four(g_out), four(A), over(1), ALU.mult))

            def gate_unit(n, par, tile, col, q, even, odd):
                v.wait_ge(s["vo_ps"], n + 1)
                for r in range(4):
                    acc = (even, odd)[r % 2]
                    ps = B[5 + par][:, r * P:(r + 1) * P]
                    gate = gates[:, tile, ds(col + r, 1)]
                    fresh = q == 0 and r < 2 and (acc is odd or even is not odd and fresh_even[0])
                    if fresh:
                        v.tensor_scalar(acc, ps, gate, None, ALU.mult).then_inc(s["gated"], 1)
                    else:
                        if not (q == 0 and r < 2):
                            v.wait_ge(s["gated"], n * 4 + (r - 1))
                        v.scalar_tensor_tensor(acc, ps, gate, acc, ALU.mult, ALU.add).then_inc(s["gated"], 1)
                if q == 1:
                    v.wait_ge(s["gated"], n * 4 + 4)

            fresh_even = [True]

            def v_gates(n, par, h, t, tt, q, first):
                fresh_even[0] = True
                gate_unit(n, par, t, h * EX + 4 * q, q, va[:, tt, 0, :], va[:, tt, 1, :])
                if q == 1:
                    if first is not None:
                        v.wait_ge(s["v_lo"], first)
                    v.tensor_tensor(v32[:, tt, :], va[:, tt, 0, :], va[:, tt, 1, :], ALU.add).then_inc(s["vsum"], 1)

            def o_gates(n, par, h, t, tt, q):
                fresh_even[0] = False
                xr = x_res[:, t, :]
                gate_unit(n, par, t, P // 2 + h * EX + 4 * q, q, xr, o_b[:, tt % 2, :])
                if q == 1:
                    v.tensor_tensor(xr, xr, o_b[:, tt % 2, :], ALU.add).then_inc(s["res"], 1)

            def body(i):
                f = parts(i)
                ub = unit_base(i)
                j = i - 1
                for kt in range(NT):
                    if f["mx"] and MX_AT[kt]:
                        max_unit(i + 1, MX_AT[kt][0])
                        if kt == 12:
                            shift_of(i + 1)
                    if f["o"] and kt == 1:
                        v.wait_ge(s["c_raw"], i * 2)
                        v.reciprocal(c_rec[:, :], c_raw[:, :, P]).then_inc(s["c_rec"], 1)
                        v.wait_ge(s["c_rec"], i)
                        v.tensor_tensor(c32[:, :, :], c_raw[:, :, 0:P],
                                        c_rec[:, :].rearrange("p (t a) -> p t a", a=1).broadcast_to([P, TPB, P]),
                                        ALU.mult).then_inc(s["c32"], 1)
                    if f["o"] and kt == 2:
                        v.wait_ge(s["c_hi"], i)
                        v.tensor_tensor(c16[:, 1], c32[:, :, :], c16[:, 0], ALU.subtract).then_inc(s["c_lo"], 1)
                    if f["v"] and kt < 8:
                        tt = kt // 2
                        v_gates(ub + kt, kt % 2, quarter(i) + 1, (i & 3) * TPB + tt, tt, kt % 2,
                                i * TPB + (NT + tt - TPB + 1))
                    if f["o"] and kt >= 8:
                        m = kt - 8
                        if m == 0 and not (isinstance(i, int) and i == 1):
                            v.wait_ge(s["res"], j * TPB)
                        o_gates(ub + (8 if f["v"] else 0) + m, m % 2, quarter(j), (j & 3) * TPB + m // 2,
                                m // 2, m % 2)
                    if f["mx"] and len(MX_AT[kt]) > 1:
                        max_unit(i + 1, MX_AT[kt][1])
                    if f["y"] and kt == 9:
                        queries(i + 2)

            v.wait_ge(s["lg"], NB)
            link(v.tensor_scalar(gp[:, :, :], gp[:, :, :], 1.0, None, ALU.add))
            queries(0)
            queries(1)
            for u in range(NT):
                max_unit(0, u)
            shift_of(0)
            link(v.reciprocal(gp[:, :, :], gp[:, :, :]))
            choose(0, G_X / (G_X * G_W))
            for n in range(2 * NT):
                t, q = n // 2, n % 2
                v_gates(n, q, 0, t, t % TPB, q, t - TPB + 1 if t >= TPB else None)
            choose(1, 1.0 / (G_C * G_W))
            over_iterations(v, body)

        UNITS = [(t, kb) for t in range(NT) for kb in range(t // TPB + 1)]
        STEPS = [(b, kt) for b in range(NB) for kt in range(TPB * (b + 1))]
        NS = len(STEPS)
        UNIT_AT = [[] for _ in range(NS)]
        for u in range(NS):
            UNIT_AT[[k for k in range(NS - 4) for _ in range(1 + (k % 9 == 7))][u]].append(u)

        ON_VECTOR = [n % 3 == 2 for n in range(NS)]
        LO_RANK = [sum(x == ON_VECTOR[n] for x in ON_VECTOR[:n + 1]) for n in range(NS)]

        def lo_part(eng, s, h, n):
            _, q0, q1, _ = step_span(n)
            eng.wait_ge(s["p"], h * NS + (n + 1))
            eng.tensor_tensor(pl_c[:, n % 4, 0:q1 - q0], p_c[:, n % 4, 0:q1 - q0],
                              top_half(p_c[:, n % 4, 0:q1 - q0]),
                              ALU.subtract).then_inc(s["lo_v" if ON_VECTOR[n] else "lo_g"], 1)

        def unit_span(u):
            t, kb = UNITS[u]
            return t, kb, min(BLK, (t + 1) * P - kb * BLK)

        def step_span(n):
            b, kt = STEPS[n]
            return kt, max(b * BLK, kt * P), (b + 1) * BLK, kt * P >= b * BLK

        def over_heads(eng, body):
            body(0, True, True)
            with eng.Fori(1, HA - 2) as h:
                body(h, True, True)
            body(HA - 2, True, False)
            body(HA - 1, False, False)

        def causal_tensor(pe):
            s = c_s
            pe.wait_ge(s["xg"], NT)
            for b in range(NB):
                for t in range(TPB):
                    mm = pe.transpose(B[b][:, t * P:(t + 1) * P], xn[:, b * TPB + t, :], ident[:, :])
                mm.then_inc(s["xt_ps"], 1)
            pe.wait_ge(s["wst"], 6)
            n = 0
            for w in (1, 0):
                for g in range(GROUPS):
                    for b in range(NB):
                        pe.wait_ge(s["xt"], b + 1)
                        if n >= 4:
                            pe.wait_ge(s["s_lo"], n - 3)
                        pe.matmul(B[4 + n % 4][:, :], wst[:, w, g, :], xT[:, b * BLK:(b + 1) * BLK],
                                  start=True, stop=True).then_inc(s["st_ps"], 1)
                        n += 1
            for b in range(NB):
                for t in range(TPB):
                    tt = b * TPB + t
                    mm = pe.matmul(B[b][:, t * P:(t + 1) * P], xT[:, tt * P:(tt + 1) * P],
                                   wbkv[:, P:2 * P], start=True, stop=True)
                mm.then_inc(s["v_ps"], 1)

            def max_unit(h, u):
                t, kb, w = unit_span(u)
                if u == 0:
                    pe.wait_ge(s["qh"], h + 1)
                if not (isinstance(h, int) and h == 0 and u < 2):
                    pe.wait_ge(s["mx"], h * NS + (u - 1))
                o = B[4 + u % 2]
                last = kb == t // TPB
                mm = pe.matmul(o[:, 0:w], q_hd[:, h & 1, t * P:(t + 1) * P],
                               k_st[:, quarter(h), kb * BLK:kb * BLK + w], start=True, stop=not last)
                if last:
                    mm = pe.matmul(o[:, w - P:w], big_id[:, :], dg[:, 0, :], start=False, stop=True)
                mm.then_inc(s["mx_ps"], 1)

            def shift_rows(h, b):
                if b == 0:
                    pe.wait_ge(s["shift"], h + 1)
                if not (isinstance(h, int) and h == 0 and b < 2):
                    pe.wait_ge(s["row"], h * NB + (b - 1))
                for t in range(TPB):
                    mm = pe.matmul(B[6 + b % 2][0:1, t * P:(t + 1) * P], csh[:, b * TPB + t:b * TPB + t + 1],
                                   ident16[:, :], start=True, stop=True)
                mm.then_inc(s["sh_ps"], 1)

            def scores(h, n):
                kt, q0, q1, diag = step_span(n)
                if n == 0:
                    pe.wait_ge(s["row"], h * NB + NB)
                if not (isinstance(h, int) and h == 0 and n < 2):
                    pe.wait_ge(s["p"], h * NS + (n - 1))
                o = B[n % 2]
                mm = pe.matmul(o[:, 0:q1 - q0], k_st[:, quarter(h), kt * P:(kt + 1) * P],
                               q_hd[:, h & 1, q0:q1], start=True, stop=not diag)
                if diag:
                    mm = pe.matmul(o[:, 0:P], big_id[:, :], dg[:, 1, :], start=False, stop=True)
                mm.then_inc(s["s_ps"], 1)

            def context(h, n):
                kt, q0, q1, _ = step_span(n)
                if n == 0 and not (isinstance(h, int) and h == 0):
                    pe.wait_ge(s["raw"], h)
                kind = ON_VECTOR[n]
                pe.wait_ge(s["lo_v" if kind else "lo_g"], h * ON_VECTOR.count(kind) + LO_RANK[n])
                for t in range(q0 // P, q1 // P):
                    c = t * P - q0
                    o = B[2][:, t * (2 * DA + 1):(t + 1) * (2 * DA + 1)]
                    pe.matmul(o, top_half(p_c[:, n % 4, c:c + P]), v17[:, kt, h, 0:2 * DA + 1],
                              start=(n == 0 and t == 0), stop=False, skip_group_check=True)
                    mm = pe.matmul(o[:, 0:DA + 1], pl_c[:, n % 4, c:c + P], v17[:, kt, h, 0:DA + 1],
                                   start=False, stop=(n == NS - 1), skip_group_check=True)
                mm.then_inc(s["pv_ps"], 1)

            def body(h, nxt, _):
                for n in range(NS):
                    if nxt:
                        for u in UNIT_AT[n]:
                            max_unit(h + 1, u)
                        if n == NS - 3:
                            for b in range(NB):
                                shift_rows(h + 1, b)
                    context(h, n)
                    if n < NS - 2:
                        scores(h, n + 2)
                    elif nxt:
                        scores(h + 1, n + 2 - NS)

            pe.wait_ge(s["s_lo"], 2 * GROUPS * NB)
            pe.wait_ge(s["stack"], 2 * GROUPS * NB)
            for u in range(NS):
                max_unit(0, u)
            for b in range(NB):
                shift_rows(0, b)
            pe.wait_ge(s["v_lo"], NB)
            scores(0, 0)
            scores(0, 1)
            over_heads(pe, body)
            for b in range(NB):
                pe.wait_ge(s["o"], HA)
                for t in range(TPB):
                    mm = pe.transpose(B[4 + b % 2][:, t * P:(t + 1) * P], o_nat[:, b * TPB + t, :], ident[:, :])
                mm.then_inc(s["ot_ps"], 1)
                pe.wait_ge(s["ot"], b + 1)
                if b >= 2:
                    pe.wait_ge(s["res"], b - 1)
                for t in range(TPB):
                    tt = b * TPB + t
                    mm = pe.matmul(B[6 + b % 2][:, t * P:(t + 1) * P], oT[:, tt * P:(tt + 1) * P], wbo[:, :],
                                   start=True, stop=True)
                mm.then_inc(s["y_ps"], 1)

        def causal_scalar(a):
            s = c_s
            norm_scalar(a, 2)
            norm_scalar(a, 3)
            for b in range(NB):
                a.wait_ge(s["xt_ps"], b + 1)
                a.activation(xT[:, b * BLK:(b + 1) * BLK], B[b][:, :], ACT.Copy).then_inc(s["xt"], 1)
            n = 0
            for gain in (G_X, G_Y * SCALE_A):
                for _ in range(GROUPS * NB):
                    a.wait_ge(s["st_ps"], n + 1)
                    if n >= 2:
                        a.wait_ge(s["stack"], n - 1)
                    a.activation(s_hi[:, n % 2, :], B[4 + n % 4][:, :], ACT.Copy, scale=gain).then_inc(s["s_hi"], 1)
                    n += 1
            a.wait_ge(s["zero"], 2)
            for b in range(NB):
                a.wait_ge(s["v_ps"], b + 1)
                a.activation(v17[:, b * TPB:(b + 1) * TPB, :, 0:DA],
                             B[b][:, :].rearrange("p (t h c) -> p t h c", t=TPB, h=HA), ACT.Copy,
                             scale=G_X).then_inc(s["v_hi"], 1)

            def rows(h):
                for b in range(NB):
                    a.wait_ge(s["sh_ps"], h * NB + (b + 1))
                    a.activation(q_hd[0:1, h & 1, b * BLK:(b + 1) * BLK], B[6 + b % 2][0:1, :],
                                 ACT.Copy).then_inc(s["row"], 1)

            def exps(h, n):
                _, q0, q1, _ = step_span(n)
                a.wait_ge(s["s_ps"], h * NS + (n + 1))
                if not (isinstance(h, int) and h == 0 and n < 4):
                    a.wait_ge(s["pv_ps"], h * NS + (n - 3))
                a.activation(p_c[:, n % 4, 0:q1 - q0], B[n % 2][:, 0:q1 - q0], ACT.Exp,
                             scale=1.0 / G_S).then_inc(s["p"], 1)

            def body(h, nxt, _):
                for n in range(NS):
                    if nxt and n == NS - 3:
                        rows(h + 1)
                    if n == NS - 1:
                        a.wait_ge(s["pv_ps"], h * NS + NS)
                        if not (isinstance(h, int) and h == 0):
                            a.wait_ge(s["o"], h)
                        a.activation(o_raw[:, :, :].rearrange("p a b -> p (a b)"),
                                     B[2][:, 0:NT * (2 * DA + 1)], ACT.Copy).then_inc(s["raw"], 1)
                    if n < NS - 2:
                        exps(h, n + 2)
                    elif nxt:
                        exps(h + 1, n + 2 - NS)

            rows(0)
            exps(0, 0)
            exps(0, 1)
            over_heads(a, body)
            for b in range(NB):
                a.wait_ge(s["ot_ps"], b + 1)
                a.activation(oT[:, b * BLK:(b + 1) * BLK], B[4 + b % 2][:, :], ACT.Copy).then_inc(s["ot"], 1)

        def causal_pool(g):
            s = c_s
            g.wait_ge(f_s[0]["res"], NT * HF)
            g.memset(mk[:, :, :], 0.0).then_inc(s["mask"], 1)
            g.memset(hd_mk[:, :, :], 0.0).then_inc(s["mask"], 1)
            g.memset(dg[:, :, :], 0.0).then_inc(s["mask"], 1)
            g.memset(big_id[:, :], 0.0).then_inc(s["mask"], 1)
            g.wait_ge(s["mask"], 4)
            sel = dict(compare_op=ALU.not_equal, fill=1.0, channel_multiplier=1)

            def rows(slot, base, pattern, n):
                v = mk[:, slot, 0:n]
                for _, m in reversed(pattern[1:]):
                    pass
                shape = {2: "p (j d) -> p j d", 3: "p (j b d) -> p j b d"}[len(pattern)]
                kw = dict(d=pattern[-1][1])
                if len(pattern) == 3:
                    kw["b"] = pattern[1][1]
                v = v.rearrange(shape, **kw)
                g.affine_select(out=v, in_=v, base=base, pattern=pattern, **sel).then_inc(s["mask"], 1)

            rows(0, -1, [[-ROWS, GROUPS], [-1, 2 * DA]], 2 * DA * GROUPS)
            rows(1, -1 - 2 * DA, [[-ROWS, GROUPS], [-1, DA]], DA * GROUPS)
            rows(2, -1, [[-ROWS, GROUPS], [-2 * DA, 2], [-1, DA]], 2 * DA * GROUPS)
            rows(3, -1 - DA, [[-ROWS, GROUPS], [-1, DA]], DA * GROUPS)
            g.affine_select(out=hd_mk[:, :, :], in_=hd_mk[:, :, :], base=0,
                            pattern=[[-ROWS, GROUPS], [-1, ROWS]], **sel).then_inc(s["mask"], 1)
            g.affine_select(out=big_id[:, :], in_=big_id[:, :], base=0, pattern=[[-1, P]],
                            compare_op=ALU.not_equal, fill=2.0 ** 60, channel_multiplier=1).then_inc(s["mask"], 1)
            g.affine_select(out=dg[:, 0, :], in_=dg[:, 0, :], base=0, pattern=[[-1, P]],
                            compare_op=ALU.is_ge, fill=-2.0 ** 60, channel_multiplier=1).then_inc(s["mask"], 1)
            g.affine_select(out=dg[:, 1, :], in_=dg[:, 1, :], base=0, pattern=[[1, P]],
                            compare_op=ALU.is_ge, fill=-2.0 ** 60, channel_multiplier=-1).then_inc(s["mask"], 1)

            def body(h, nxt, _):
                for n in range(NS):
                    m = (n + 2) % NS
                    if not ON_VECTOR[m] and (n < NS - 2 or nxt):
                        lo_part(g, s, h if n < NS - 2 else h + 1, m)

            lo_part(g, s, 0, 0)
            lo_part(g, s, 0, 1)
            over_heads(g, body)

        def causal_vector(v):
            s = c_s
            v.wait_ge(f_s[0]["res"], NT * HF)
            norm_vector(v, 2, x_res, xn)
            v.wait_ge(ln_s["xn"], 3 * NT)
            norm_vector(v, 3, xn, xn2)
            for t in range(NT):
                if t == 0:
                    v.wait_ge(ln_s["xn"], 4 * NT)
                v.tensor_tensor(xn[:, t, :], xn2[:, t, :], g_row[:, :], ALU.mult).then_inc(s["xg"], 1)
            v.memset(wst[:, :, :, :], 0.0).then_inc(s["zero"], 1)
            v.memset(v17[:, :, :, DA:DA + 1], G_X).then_inc(s["zero"], 1)
            v.memset(cmx[:, :, :], -3.0e38).then_inc(s["zero"], 1)
            v.memset(row_one[:, :], 0.0).then_inc(s["zero"], 1)
            v.wait_ge(s["zero"], 4)
            v.memset(row_one[0:1, 0:1], ONE_K).then_inc(s["zero"], 1)
            v.wait_ge(ld_c, 48)
            for w, src in ((0, wbq[:, :]), (1, wbkv[:, 0:P])):
                for b in range(3):
                    v.tensor_copy(
                        wst[:, w, :, :].rearrange("p g (j r) -> p (g j) r", r=ROWS)[:, :, 1 + b * DA:1 + (b + 1) * DA],
                        src.rearrange("p (h c) -> p h c", c=DA)).then_inc(s["wst"], 1)
            v.wait_ge(s["mask"], 12)
            for slot, (kind, part), n in ((0, (0, 0), 64), (1, (0, 1), 32), (2, (1, 0), 64), (3, (1, 1), 32)):
                v.tensor_reduce(row_mask[:, kind, part:part + 1], mk[:, slot, 0:n], AX.X, ALU.add).then_inc(s["zero"], 1)
            v.tensor_reduce(hd_mask[:, :], hd_mk[:, :, :], AX.X, ALU.add).then_inc(s["zero"], 1)
            v.wait_ge(s["zero"], 10)
            n = 0
            for kind, dst, gain in ((0, k_st, G_X), (1, q_st, G_Y * SCALE_A)):
                for g in range(GROUPS):
                    for b in range(NB):
                        v.wait_ge(s["s_hi"], n + 1)
                        v.scalar_tensor_tensor(s_lo[:, n % 2, :], B[4 + n % 4][:, :], gain, s_hi[:, n % 2, :],
                                               ALU.mult, ALU.subtract).then_inc(s["s_lo"], 1)
                        v.tensor_scalar(s_ab[:, n % 2, :], s_hi[:, n % 2, :], row_mask[:, kind, 0:1],
                                        row_one[:, kind:kind + 1], ALU.mult, ALU.add).then_inc(s["s_a"], 1)
                        v.wait_ge(s["s_lo"], n + 1)
                        v.wait_ge(s["s_a"], n + 1)
                        v.scalar_tensor_tensor(dst[:, g, b * BLK:(b + 1) * BLK], s_lo[:, n % 2, :],
                                               row_mask[:, kind, 1:2], s_ab[:, n % 2, :],
                                               ALU.mult, ALU.add).then_inc(s["stack"], 1)
                        n += 1
            for b in range(NB):
                v.wait_ge(s["v_hi"], b + 1)
                v.scalar_tensor_tensor(
                    v17[:, b * TPB:(b + 1) * TPB, :, DA + 1:2 * DA + 1].rearrange("p t h c -> p (t h) c"),
                    B[b][:, :].rearrange("p (t c) -> p t c", c=DA), G_X,
                    v17[:, b * TPB:(b + 1) * TPB, :, 0:DA].rearrange("p t h c -> p (t h) c"),
                    ALU.mult, ALU.subtract).then_inc(s["v_lo"], 1)
            v.wait_ge(s["stack"], 2 * GROUPS * NB)

            def head_queries(h):
                v.tensor_scalar(q_hd[:, h & 1, :], q_st[:, quarter(h), :], hd_mask[:, ds(h & 3, 1)], None,
                                ALU.mult).then_inc(s["qh"], 1)

            def max_unit(h, u):
                t, kb, w = unit_span(u)
                v.wait_ge(s["mx_ps"], h * NS + (u + 1))
                v.tensor_reduce(cmx[:, t, kb:kb + 1], B[4 + u % 2][:, 0:w], AX.X, ALU.max).then_inc(s["mx"], 1)

            def shift_of(h):
                v.wait_ge(s["mx"], h * NS + NS)
                v.tensor_reduce(cneg[:, :], cmx[:, :, :], AX.X, ALU.max, negate=True).then_inc(s["neg"], 1)
                v.wait_ge(s["neg"], h + 1)
                v.tensor_scalar(csh[:, :], cneg[:, :], G_M / G_S, G_M * LOG_P, ALU.mult, ALU.add).then_inc(s["shift"], 1)

            def outputs(h):
                v.wait_ge(s["raw"], h + 1)
                v.reciprocal(c_rec2[:, :], o_raw[:, :, DA]).then_inc(s["rec"], 1)
                v.tensor_tensor(o_sum[:, :, :], o_raw[:, :, 0:DA], o_raw[:, :, DA + 1:2 * DA + 1],
                                ALU.add).then_inc(s["rec"], 1)
                v.wait_ge(s["rec"], h * 2 + 2)
                v.tensor_tensor(o_nat[:, :, ds(h * DA, DA)], o_sum[:, :, :],
                                c_rec2[:, :].rearrange("p (t a) -> p t a", a=1).broadcast_to([P, NT, DA]),
                                ALU.mult).then_inc(s["o"], 1)

            def body(h, nxt, nxt2):
                for n in range(NS):
                    if nxt:
                        for u in UNIT_AT[n]:
                            max_unit(h + 1, u)
                        if n == NS - 4:
                            shift_of(h + 1)
                    m = (n + 2) % NS
                    if ON_VECTOR[m] and (n < NS - 2 or nxt):
                        lo_part(v, s, h if n < NS - 2 else h + 1, m)
                if nxt2:
                    v.wait_ge(s["s_ps"], h * NS + NS)
                    head_queries(h + 2)
                outputs(h)

            head_queries(0)
            head_queries(1)
            for u in range(NS):
                max_unit(0, u)
            shift_of(0)
            assert not ON_VECTOR[0] and not ON_VECTOR[1]
            over_heads(v, body)
            for b in range(NB):
                v.wait_ge(s["y_ps"], b + 1)
                xr = x_res[:, b * TPB:(b + 1) * TPB, :].rearrange("p a b -> p (a b)")
                v.tensor_tensor(xr, B[6 + b % 2][:, :], xr, ALU.add).then_inc(s["res"], 1)

        @block.sync
        def _(sp):
            loads(sp)
            sp.wait_ge(f_s[1]["res"], NT * HF)
            sp.dma_start(out.rearrange("b (t p) c -> p (b t) c", p=P), x_res[:, :, :]).then_inc(out_done, 16)
            sp.wait_ge(out_done, 16)

        @block.tensor
        def _(pe):
            linear_tensor(pe)
            switch_tensor(pe, 0)
            causal_tensor(pe)
            switch_tensor(pe, 1)

        @block.scalar
        def _(a):
            linear_scalar(a)
            switch_scalar(a, 0)
            causal_scalar(a)
            switch_scalar(a, 1)

        @block.vector
        def _(v):
            linear_vector(v)
            switch_vector(v, 0)
            causal_vector(v)
            switch_vector(v, 1)

        @block.gpsimd
        def _(g):
            constants_pool(g)
            switch_pool(g, 0)
            causal_pool(g)
            switch_pool(g, 1)


_INS = ['L0_attn_a_x', 'L0_attn_a_Wq', 'L0_attn_a_bq', 'L0_attn_a_Wk', 'L0_attn_a_bk', 'L0_attn_a_Wv',
        'L0_attn_a_bv', 'L0_attn_a_Wo', 'L0_attn_a_bo', 'L0_attn_b_g_ln', 'L0_attn_b_Wq', 'L0_attn_b_Wkv',
        'L0_attn_b_Wo', 'L0_ffn_q_w', 'L0_ffn_k_w', 'L0_ffn_v_w', 'L0_ffn_o_w', 'L0_ffn_sel_v_w',
        'L0_ffn_sel_o_w', 'L0_ffn_route_scale']


def kernel(**inputs):
    import numpy as _np
    import concourse.bacc as _bacc
    from concourse import mybir as _mybir
    from concourse.bass_utils import run_bass_kernel_spmd as _run

    nc = _bacc.Bacc("TRN2", target_bir_lowering=False, num_devices=1)
    arrays, args = {}, []
    for name in _INS:
        a = _np.ascontiguousarray(inputs[name])
        arrays[f"in_{name}_dram"] = a
        args.append(nc.dram_tensor(f"in_{name}_dram", a.shape, _mybir.dt.from_np(a.dtype), kind="ExternalInput").ap())
    shape = inputs['L0_attn_a_x'].shape
    args.append(nc.dram_tensor("out_0_dram", shape, F32, kind="ExternalOutput").ap())
    hybrid_program(nc, *args)
    r = _run(nc, [arrays], core_ids=[0])
    return r.results[0]["out_0_dram"]
```

```python
from contextlib import ExitStack
import math

import concourse.bass as bass
from concourse import mybir

F32 = mybir.dt.float32
F16 = mybir.dt.float16
BF16 = mybir.dt.bfloat16
ALU = mybir.AluOpType
ACT = mybir.ActivationFunctionType
AX = mybir.AxisListType

P = 128
T = 2048
NT = T // P
BLK = 512
NB = T // BLK
TPB = BLK // P
EPS = 1e-5

HA = 16
DA = P // HA
SCALE_A = DA ** -0.5
ROWS = 32
GROUPS = P // ROWS

HF = 8
EX = 8
SCALE_F = P ** -0.5
QUADS = HF * EX // 4

G_X = 64.0
G_W = 1024.0
G_Y = 128.0
G_C = 256.0
G_S = G_X * G_Y
ONE_K = 2048.0
G_M = G_S / ONE_K
SLOTS_C = 5
AHEAD_C = 4
LOG_P = 8 * math.log(2.0)


def hybrid_program(nc, x_in, Wq, bq, Wk, bk, Wv, bv, Wo, bo, g_ln, Wbq, Wbkv, Wbo,
                   q_w, k_w, v_w, o_w, sel_v_w, sel_o_w, route_scale, out):
    with ExitStack() as ctx:
        def sem(name):
            return ctx.enter_context(nc.semaphore(name))

        def sb(name, shape, dt=F32, stack=ctx):
            return stack.enter_context(nc.sbuf_tensor(name, shape, dt))

        x_res = sb("x_res", [P, NT, P])
        xn = sb("xn", [P, NT, P])
        xT = sb("xT", [P, T])
        stats = sb("stats", [P, NT, 6])
        mv = sb("mv", [P, NT, 2])
        lnv = sb("lnv", [P, 6, NT])
        ident = sb("ident", [P, P])
        ident16 = sb("ident16", [P, P], F16)
        ones = sb("ones", [P, P])
        selT = sb("selT", [P, P])
        rs_col = sb("rs_col", [P, 1])
        m_hi = sb("m_hi", [P, HF, P], F16)
        m_lo = sb("m_lo", [P, HF, P], F16)
        vw_hi = sb("vw_hi", [P, HF * EX, P], F16)
        vw_lo = sb("vw_lo", [P, HF * EX, P], F16)
        ow_hi = sb("ow_hi", [P, HF * EX, P], F16)
        ow_lo = sb("ow_lo", [P, HF * EX, P], F16)
        wbq = sb("wbq", [P, P])
        wbkv = sb("wbkv", [P, 2 * P])
        wbo = sb("wbo", [P, P])
        g_col = sb("g_col", [P, 1])
        stage = sb("stage", [P, 4, EX * P])
        place = sb("place", [P, 2, 2, GROUPS * P], F16)
        row_one = sb("row_one", [P, 1])
        hd_mk = sb("hd_mk", [P, GROUPS, ROWS])
        dg = sb("dg", [P, 2, P], BF16)
        big_id = sb("big_id", [P, P], BF16)

        with ExitStack() as a:
            def sa(name, shape, dt=F32):
                return sb(name, shape, dt, a)
            w_nat = sa("w_nat", [P, 4, P])
            wT = sa("wT", [P, 4, P])
            sel_nat = sa("sel_nat", [P, P])
            bq_col = sa("bq_col", [P, 1])
            bkv_row = sa("bkv_row", [1, 2 * P])
            bo_row = sa("bo_row", [1, P])
            qk_w = sa("qk_w", [P, 2, HF, P])
            cen = sa("cen", [P, 2, HF])
            head_mask = sa("head_mask", [P, P])
            qT = sa("qT", [P, T])
            q_exp = sa("q_exp", [P, 2, BLK])
            q_pos = sa("q_pos", [P, 2, BLK])
            k_exp = sa("k_exp", [P, 2, 2, P])
            k_pos = sa("k_pos", [P, 2, 2, P])
            k_nat = sa("k_nat", [P, NT, P])
            v_nat = sa("v_nat", [P, NT, P + 1])
            kv_sb = sa("kv_sb", [P, P + HA])
            den = sa("den", [P, 2, TPB, HA])
            rden = sa("rden", [P, 2, TPB, HA])
            a_nat = sa("a_nat", [P, 2, TPB, P])
            aT = sa("aT", [P, T])

        with ExitStack() as a:
            def sf(name, shape, dt=F32):
                return sb(name, shape, dt, a)
            x_hi = sf("x_hi", [P, T], F16)
            x_lo = sf("x_lo", [P, T], F16)
            xk_hi = sf("xk_hi", [P, T], F16)
            xk_lo = sf("xk_lo", [P, T], F16)
            gates = sf("gates", [P, NT, P])
            gp = xn
            gt = sf("gt", [P, 2, NT, P // 2])
            g1 = sf("g1", [P, 2, NT * HF])
            tie = sf("tie", [P, EX])
            y_hi = sf("y_hi", [P, NB, BLK], F16)
            y_lo = sf("y_lo", [P, NB, BLK], F16)
            mx = sf("mx", [P, TPB, NB])
            negm = sf("negm", [P, TPB])
            shift = sf("shift", [P, TPB], F16)
            p32 = sf("p32", [P, 4, BLK])
            p_lo = sf("p_lo", [P, 4, BLK], F16)
            va = sf("va", [P, 4, 2, P])
            v32 = sf("v32", [P, 4, P])
            v_hi = sf("v_hi", [P, 2, NT, P + 2], F16)
            v_lo = sf("v_lo", [P, 2, NT, P], F16)
            o_b = sf("o_b", [P, 2, P])
            c_raw = sf("c_raw", [P, TPB, P + 1])
            c_rec = sf("c_rec", [P, TPB])
            c32 = sf("c32", [P, TPB, P])
            c16 = sf("c16", [P, 2, TPB, P], F16)
            cT = sf("cT", [P, 2, BLK], F16)

        with ExitStack() as a:
            def sc(name, shape, dt=F32):
                return sb(name, shape, dt, a)
            kq_hi = sc("kq_hi", [P, 2, BLK], F16)
            kq_lo = sc("kq_lo", [P, 2, BLK], F16)
            k_st = sc("k_st", [P, GROUPS, T], F16)
            q_st = sc("q_st", [P, GROUPS, T], F16)
            q_hd = sc("q_hd", [P, 2, T], F16)
            hd_mask = sc("hd_mask", [P, GROUPS])
            v17 = sc("v17", [P, NT, HA, 2 * DA + 2], F16)
            cmx = sc("cmx", [P, NT, NB])
            cneg = sc("cneg", [P, NT])
            csh = sc("csh", [P, NT], F16)
            p_c = sc("p_c", [P, SLOTS_C, BLK])
            pl_c = sc("pl_c", [P, SLOTS_C, BLK], F16)
            o_raw = sc("o_raw", [P, NT, 2 * DA + 1])
            o_sum = sc("o_sum", [P, NT, DA])
            c_rec2 = sc("c_rec2", [P, NT])
            o_nat = sc("o_nat", [P, NT, P])

        B = [ctx.enter_context(nc.psum_tensor(f"bank{i}", [P, BLK], F32)) for i in range(8)]
        ds = bass.ds

        def quarter(i):
            return i >> 2 if isinstance(i, int) else (i >> 2).with_bounds(min_val=i.min_val >> 2, max_val=i.max_val >> 2)

        ld_x, ld_w, ld_qk, ld_b, ld_c = (sem("ld_" + n) for n in ("x", "w", "qk", "b", "c"))
        ld_e = [sem(f"ld_e{n}") for n in range(4)]
        e_up, e_hi, e_lo = sem("e_up"), sem("e_hi"), sem("e_lo")
        zeroed = sem("zeroed")
        consts = sem("consts")
        consts_c = sem("consts_c")
        vconst = sem("vconst")
        qk_cen = sem("qk_cen")
        out_done = sem("out_done")
        a_s = {n: sem("a_" + n) for n in (
            "wt_ps", "wt", "sel_ps", "sel", "xt_ps", "xt", "m_ps", "m_hi", "m_lo",
            "q_ps", "q_exp", "q_pos", "q", "k_ps", "k_exp", "v", "k_pos", "k",
            "kv_ps", "kv", "cen", "nd_ps", "den", "rden", "an", "at_ps", "at", "y_ps", "res")}
        ln_names = ("stats", "mv", "var", "root", "chain", "xn")
        ln_s = {n: sem("ln_" + n) for n in ln_names}
        f_s = [{n: sem(f"f{k}_{n}") for n in (
            "xt_ps", "xt", "x_hi", "x_lo", "xk", "lg_ps", "lg", "choice", "gates", "ones",
            "y_ps", "y_hi", "y_lo", "mx_ps", "mx", "negm", "shift", "sh_ps", "row",
            "vo_ps", "gated", "vsum", "v_hi", "v_lo", "st_ps", "p", "p_lo", "pv_ps",
            "c_raw", "c_rec", "c32", "c_hi", "c_lo", "ct_ps", "ct", "res")} for k in range(2)]
        c_s = {n: sem("c_" + n) for n in (
            "zero", "xt_ps", "xt", "kq_ps", "kq_hi", "kq_lo", "st_ps", "st_v", "st_a",
            "v_ps", "v_hi", "v_lo", "qh", "mx_ps", "mx", "neg", "shift", "sh_ps", "row", "s_ps", "p",
            "lo_v", "lo_g", "pv_ps", "raw", "rec", "o", "ot_ps", "ot", "y_ps", "res")}

        block = ctx.enter_context(nc.Block())

        def top_half(x):
            return x.bitcast(BF16)[:, 1::2]

        def norm_vector(v, k, src, dst):
            s = ln_s
            for t in range(NT):
                v.bn_stats(stats[:, t, :], src[:, t, :]).then_inc(s["stats"], 1)
            for t in range(NT):
                v.wait_ge(s["stats"], NT * k + t + 1)
                v.bn_aggr(mv[:, t, :], stats[:, t, :]).then_inc(s["mv"], 1)
            v.wait_ge(s["mv"], NT * (k + 1))
            v.tensor_scalar(lnv[:, 0, :], mv[:, :, 1], EPS, None, ALU.add).then_inc(s["var"], 1)
            v.wait_ge(s["var"], k + 1)
            v.wait_ge(s["root"], k + 1)
            v.reciprocal(lnv[:, 2, :], lnv[:, 1, :]).then_inc(s["chain"], 1)
            v.wait_ge(s["chain"], 5 * k + 1)
            v.tensor_tensor(lnv[:, 3, :], lnv[:, 2, :], lnv[:, 2, :], ALU.mult).then_inc(s["chain"], 1)
            v.wait_ge(s["chain"], 5 * k + 2)
            v.tensor_tensor(lnv[:, 4, :], lnv[:, 3, :], lnv[:, 0, :], ALU.mult).then_inc(s["chain"], 1)
            v.wait_ge(s["chain"], 5 * k + 3)
            v.tensor_scalar(lnv[:, 3, :], lnv[:, 4, :], -0.5, 1.5, ALU.mult, ALU.add).then_inc(s["chain"], 1)
            v.wait_ge(s["chain"], 5 * k + 4)
            v.tensor_tensor(lnv[:, 5, :], lnv[:, 3, :], lnv[:, 2, :], ALU.mult).then_inc(s["chain"], 1)
            v.wait_ge(s["chain"], 5 * k + 5)
            for t in range(NT):
                v.tensor_scalar(dst[:, t, :], src[:, t, :], mv[:, t, 0:1], lnv[:, 5, t:t + 1],
                                ALU.subtract, ALU.mult).then_inc(s["xn"], 1)

        def norm_scalar(a, k):
            a.wait_ge(ln_s["var"], k + 1)
            a.activation(lnv[:, 1, :], lnv[:, 0, :], ACT.Sqrt).then_inc(ln_s["root"], 1)

        def linear_tensor(pe):
            s = a_s
            pe.wait_ge(consts, 2)
            pe.wait_ge(ld_w, 16 * 4)
            for w in range(4):
                mm = pe.transpose(B[0][:, w * P:(w + 1) * P], w_nat[:, w, :], ident[:, :])
            mm.then_inc(s["wt_ps"], 1)
            pe.wait_ge(ld_b, 16 * 8)
            pe.transpose(B[1][:, 0:P], sel_nat[:, :], ident[:, :]).then_inc(s["sel_ps"], 1)
            for b in range(NB):
                pe.wait_ge(ln_s["xn"], TPB * (b + 1))
                for t in range(TPB):
                    mm = pe.transpose(B[2 + b][:, t * P:(t + 1) * P], xn[:, b * TPB + t, :], ident[:, :])
                mm.then_inc(s["xt_ps"], 1)
            for g in range(2):
                pe.wait_ge(qk_cen, 2 * HF // 2 * (g + 1))
                for h in range(HF // 2):
                    hh = g * HF // 2 + h
                    mm = pe.matmul(B[6 + g][:, h * P:(h + 1) * P], qk_w[:, 0, hh, :], qk_w[:, 1, hh, :],
                                   start=True, stop=True)
                mm.then_inc(s["m_ps"], 1)
            pe.wait_ge(s["wt"], 1)
            pe.wait_ge(s["sel"], 1)
            for b in range(NB):
                pe.wait_ge(s["xt"], b + 1)
                if b >= 2:
                    pe.wait_ge(s["q_pos"], b - 1)
                pe.matmul(B[b % 2][:, :], wT[:, 0, :], xT[:, b * BLK:(b + 1) * BLK],
                          start=True, stop=True).then_inc(s["q_ps"], 1)
            pe.wait_ge(consts, 3)
            for n in range(NT // 2):
                bank = B[2 + n % 2]
                pe.wait_ge(s["xt"], NB)
                if n >= 2:
                    pe.wait_ge(s["v"], n - 1)
                for r in range(2):
                    t = 2 * n + r
                    o = bank[:, r * 2 * P:(r + 1) * 2 * P]
                    pe.matmul(o, ones[0:1, :], bkv_row[:, :], start=True, stop=False)
                    mm = pe.matmul(o, xT[:, t * P:(t + 1) * P],
                                   wT[:, 1:3, :].rearrange("p a b -> p (a b)"), start=False, stop=True)
                mm.then_inc(s["k_ps"], 1)
            pe.wait_ge(vconst, 1)
            for t in range(NT):
                if t % 2 == 0:
                    pe.wait_ge(s["k"], t // 2 + 1)
                    pe.wait_ge(s["v"], t // 2 + 1)
                mm = pe.matmul(B[4][:, 0:P + 1], k_nat[:, t, :], v_nat[:, t, :],
                               start=(t == 0), stop=(t == NT - 1))
            mm.then_inc(s["kv_ps"], 1)
            pe.wait_ge(s["kv"], 2)
            pe.wait_ge(s["q"], NB)
            for b in range(NB):
                if b >= 2:
                    pe.wait_ge(s["an"], b - 1)
                for t in range(TPB):
                    o = B[2 * (b % 2) + t // 2][:, (t % 2) * (P + HA):(t % 2 + 1) * (P + HA)]
                    tt = b * TPB + t
                    mm = pe.matmul(o, qT[:, tt * P:(tt + 1) * P], kv_sb[:, :], start=True, stop=True)
                mm.then_inc(s["nd_ps"], 1)
            pe.wait_ge(s["m_lo"], 2)
            for b in range(NB):
                pe.wait_ge(s["an"], b + 1)
                if b >= 2:
                    pe.wait_ge(s["at"], b - 1)
                for t in range(TPB):
                    mm = pe.transpose(B[4 + b % 2][:, t * P:(t + 1) * P], a_nat[:, b % 2, t, :], ident[:, :])
                mm.then_inc(s["at_ps"], 1)
                pe.wait_ge(s["at"], b + 1)
                if b >= 2:
                    pe.wait_ge(s["res"], b - 1)
                for t in range(TPB):
                    o = B[6 + b % 2][:, t * P:(t + 1) * P]
                    pe.matmul(o, ones[0:1, :], bo_row[:, :], start=True, stop=False)
                    mm = pe.matmul(o, aT[:, (b * TPB + t) * P:(b * TPB + t + 1) * P], wT[:, 3, :],
                                   start=False, stop=True)
                mm.then_inc(s["y_ps"], 1)

        def linear_scalar(a):
            s = a_s
            norm_scalar(a, 0)
            a.wait_ge(s["wt_ps"], 1)
            a.activation(wT[:, :, :].rearrange("p a b -> p (a b)"), B[0][:, :], ACT.Copy).then_inc(s["wt"], 1)
            a.wait_ge(s["sel_ps"], 1)
            a.activation(selT[:, :], B[1][:, 0:P], ACT.Copy).then_inc(s["sel"], 1)
            for b in range(NB):
                a.wait_ge(s["xt_ps"], b + 1)
                a.activation(xT[:, b * BLK:(b + 1) * BLK], B[2 + b][:, :], ACT.Copy).then_inc(s["xt"], 1)
            for g in range(2):
                a.wait_ge(s["m_ps"], g + 1)
                a.activation(m_hi[:, 4 * g:4 * g + 4, :].rearrange("p a b -> p (a b)"), B[6 + g][:, :],
                             ACT.Copy, scale=SCALE_F * G_W).then_inc(s["m_hi"], 1)
            for b in range(NB):
                a.wait_ge(s["q_ps"], b + 1)
                if b >= 2:
                    a.wait_ge(s["q"], b - 1)
                a.activation(q_exp[:, b % 2, :], B[b % 2][:, :], ACT.Exp,
                             bias=bq_col[:, 0:1]).then_inc(s["q_exp"], 1)
                a.activation(q_pos[:, b % 2, :], B[b % 2][:, :], ACT.Relu,
                             bias=bq_col[:, 0:1]).then_inc(s["q_pos"], 1)
            a.wait_ge(vconst, 1)
            for n in range(NT // 2):
                ps = B[2 + n % 2][:, :].rearrange("p (r a c) -> p r a c", r=2, a=2)
                a.wait_ge(s["k_ps"], n + 1)
                if n >= 2:
                    a.wait_ge(s["k"], n - 1)
                a.activation(k_exp[:, n % 2, :, :], ps[:, :, 0, :], ACT.Exp).then_inc(s["k_exp"], 1)
                a.activation(k_pos[:, n % 2, :, :], ps[:, :, 0, :], ACT.Relu).then_inc(s["k_pos"], 1)
                a.activation(v_nat[:, 2 * n:2 * n + 2, 0:P], ps[:, :, 1, :], ACT.Copy).then_inc(s["v"], 1)
            experts_scalar(a, 0, 3)
            for b in range(NB):
                a.wait_ge(s["at_ps"], b + 1)
                a.activation(aT[:, b * BLK:(b + 1) * BLK], B[4 + b % 2][:, :], ACT.Copy).then_inc(s["at"], 1)
            experts_scalar(a, 3, 8)

        def linear_vector(v):
            s = a_s
            v.memset(v_nat[:, :, P:P + 1], 1.0).then_inc(vconst, 1)
            v.wait_ge(ld_x, 16)
            norm_vector(v, 0, x_res, xn)
            v.wait_ge(ld_qk, 32)
            v.tensor_copy(cen[:, :, :], qk_w[:, :, :, 0]).then_inc(s["cen"], 1)
            v.wait_ge(s["cen"], 1)
            for h in range(HF):
                for w in range(2):
                    v.tensor_scalar(qk_w[:, w, h, :], qk_w[:, w, h, :], cen[:, w, h:h + 1], None,
                                    ALU.subtract).then_inc(qk_cen, 1)
            for g in range(2):
                v.wait_ge(s["m_hi"], g + 1)
                v.scalar_tensor_tensor(m_lo[:, 4 * g:4 * g + 4, :].rearrange("p a b -> p (a b)"),
                                       B[6 + g][:, :], SCALE_F * G_W,
                                       m_hi[:, 4 * g:4 * g + 4, :].rearrange("p a b -> p (a b)"),
                                       ALU.mult, ALU.subtract).then_inc(s["m_lo"], 1)
            for b in range(NB):
                v.wait_ge(s["q_pos"], b + 1)
                v.scalar_tensor_tensor(qT[:, b * BLK:(b + 1) * BLK], q_exp[:, b % 2, :], 1.0,
                                       q_pos[:, b % 2, :], ALU.min, ALU.add).then_inc(s["q"], 1)
            for n in range(NT // 2):
                v.wait_ge(s["k_pos"], n + 1)
                v.scalar_tensor_tensor(k_nat[:, 2 * n:2 * n + 2, :].rearrange("p a b -> p (a b)"),
                                       k_exp[:, n % 2, :, :].rearrange("p a b -> p (a b)"), 1.0,
                                       k_pos[:, n % 2, :, :].rearrange("p a b -> p (a b)"),
                                       ALU.min, ALU.add).then_inc(s["k"], 1)
            v.wait_ge(s["kv_ps"], 1)
            v.wait_ge(consts, 5)
            v.tensor_tensor(kv_sb[:, 0:P], B[4][:, 0:P], head_mask[:, :], ALU.mult).then_inc(s["kv"], 1)
            v.tensor_scalar(kv_sb[:, P:P + HA], head_mask[:, 0:P:DA], B[4][:, P:P + 1], None,
                            ALU.mult).then_inc(s["kv"], 1)
            for b in range(NB):
                v.wait_ge(s["nd_ps"], b + 1)
                nd = [B[2 * (b % 2) + n][:, 0:2 * (P + HA)].rearrange("p (t c) -> p t c", t=2) for n in range(2)]
                for n in range(2):
                    v.tensor_scalar(den[:, b % 2, 2 * n:2 * n + 2, :], nd[n][:, :, P:P + HA], 1e-6, None,
                                    ALU.max).then_inc(s["den"], 1)
                v.wait_ge(s["den"], 2 * b + 2)
                v.reciprocal(rden[:, b % 2, :, :], den[:, b % 2, :, :]).then_inc(s["rden"], 1)
                v.wait_ge(s["rden"], b + 1)
                if b >= 2:
                    v.wait_ge(s["at_ps"], b - 1)
                for n in range(2):
                    r = rden[:, b % 2, 2 * n:2 * n + 2, :].rearrange("p t (h a) -> p t h a", a=1)
                    ins = v.tensor_tensor(
                        a_nat[:, b % 2, 2 * n:2 * n + 2, :].rearrange("p t (h c) -> p t h c", c=DA),
                        nd[n][:, :, 0:P].rearrange("p t (h c) -> p t h c", c=DA),
                        r.broadcast_to([P, 2, HA, DA]), ALU.mult)
                ins.then_inc(s["an"], 1)
            for b in range(NB):
                v.wait_ge(s["y_ps"], b + 1)
                xr = x_res[:, b * TPB:(b + 1) * TPB, :].rearrange("p a b -> p (a b)")
                v.tensor_tensor(xr, B[6 + b % 2][:, :], xr, ALU.add).then_inc(s["res"], 1)

        def expert_parts(n):
            h = n // 2
            return (x[:, h * EX:(h + 1) * EX, :].rearrange("p a b -> p (a b)")
                    for x in ((vw_hi, vw_lo), (ow_hi, ow_lo))[n % 2])

        def experts_scalar(a, n0, n1):
            for n in range(n0, n1):
                hi, _ = expert_parts(n)
                a.wait_ge(ld_e[n % 4], 16 * (n // 4 + 1))
                a.activation(stage[:, n % 4, :], stage[:, n % 4, :], ACT.Copy, scale=G_W).then_inc(e_up, 1)
                a.wait_ge(e_up, n + 1)
                a.activation(hi, stage[:, n % 4, :], ACT.Copy).then_inc(e_hi, 1)

        def experts_pool(g):
            for n in range(2 * HF):
                hi, lo = expert_parts(n)
                g.wait_ge(e_hi, n + 1)
                g.tensor_tensor(lo, stage[:, n % 4, :], hi, ALU.subtract).then_inc(e_lo, 1)

        def loads(sp):
            sp.dma_start(x_res[:, :, :], x_in.rearrange("b (t p) c -> p (b t) c", p=P)).then_inc(ld_x, 16)
            for w, src in enumerate((Wq, Wk, Wv, Wo)):
                sp.dma_start(w_nat[:, w, :], src).then_inc(ld_w, 16)
            col = lambda x: x.rearrange("(p a) -> p a", a=1)
            row = lambda x: x.rearrange("(a c) -> a c", a=1)
            sp.dma_start(bq_col[:, :], col(bq)).then_inc(ld_b, 16)
            sp.dma_start(bkv_row[:, 0:P], row(bk)).then_inc(ld_b, 16)
            sp.dma_start(bkv_row[:, P:2 * P], row(bv)).then_inc(ld_b, 16)
            sp.dma_start(bo_row[:, :], row(bo)).then_inc(ld_b, 16)
            sp.dma_start(sel_nat[0:P // 2, :], sel_v_w).then_inc(ld_b, 16)
            sp.dma_start(sel_nat[P // 2:P, :], sel_o_w).then_inc(ld_b, 16)
            sp.dma_start(rs_col[:, :], row(route_scale).broadcast_to([P, 1])).then_inc(ld_b, 16)
            sp.dma_start(g_col[:, :], col(g_ln)).then_inc(ld_b, 16)
            sp.dma_start(qk_w[:, 0, :, :], q_w.rearrange("(h p) d -> p h d", p=P)).then_inc(ld_qk, 16)
            sp.dma_start(qk_w[:, 1, :, :], k_w.rearrange("(h p) d -> p h d", p=P)).then_inc(ld_qk, 16)
            sp.dma_start(wbq[:, :], Wbq).then_inc(ld_c, 16)
            sp.dma_start(wbkv[:, :], Wbkv).then_inc(ld_c, 16)
            sp.dma_start(wbo[:, :], Wbo).then_inc(ld_c, 16)
            for n in range(2 * HF):
                src, h = (v_w, o_w)[n % 2], n // 2
                if n >= 4:
                    sp.wait_ge(e_lo, n - 3)
                sp.dma_start(stage[:, n % 4, :].rearrange("p (e c) -> p e c", e=EX),
                             src[h * EX:(h + 1) * EX].rearrange("e p c -> p e c")).then_inc(ld_e[n % 4], 16)

        def constants_pool(g):
            g.memset(ident[:, :], 0.0).then_inc(zeroed, 1)
            g.memset(head_mask[:, :], 1.0).then_inc(zeroed, 1)
            g.wait_ge(zeroed, 1)
            g.affine_select(out=ident[:, :], in_=ident[:, :], compare_op=ALU.not_equal, fill=1.0,
                            base=0, pattern=[[-1, P]], channel_multiplier=1).then_inc(consts, 1)
            g.wait_ge(consts, 1)
            g.tensor_copy(ident16[:, :], ident[:, :]).then_inc(consts, 1)
            g.memset(ones[:, :], 1.0).then_inc(consts, 1)
            hm = head_mask[:, :].rearrange("p (h c) -> p h c", c=DA)
            g.wait_ge(zeroed, 2)
            g.affine_select(out=hm, in_=hm, compare_op=ALU.is_ge, fill=0.0, base=0,
                            pattern=[[-DA, HA], [0, DA]], channel_multiplier=1).then_inc(consts, 1)
            g.wait_ge(consts, 4)
            g.affine_select(out=hm, in_=hm, compare_op=ALU.is_ge, fill=0.0, base=DA - 1,
                            pattern=[[DA, HA], [0, DA]], channel_multiplier=-1).then_inc(consts, 1)

        def causal_constants_pool(g):
            for n, x in enumerate((place[:, :, :, :], hd_mk[:, :, :], dg[:, :, :], big_id[:, :], row_one[:, :])):
                g.memset(x, 0.0).then_inc(zeroed, 1)
            g.wait_ge(zeroed, 7)
            heads = ident16[:, :].rearrange("p (h c) -> p h c", c=DA)
            for kind, part, b in ((0, 0, 0), (0, 0, 1), (0, 1, 2), (1, 0, 0), (1, 1, 1), (1, 0, 2)):
                g.tensor_copy(place[:, kind, part, :].rearrange("p (h r) -> p h r", r=ROWS)
                              [:, :, 1 + b * DA:1 + (b + 1) * DA], heads).then_inc(consts_c, 1)
            g.memset(row_one[0:1, :], ONE_K).then_inc(consts_c, 1)
            g.affine_select(out=hd_mk[:, :, :], in_=hd_mk[:, :, :], base=0, compare_op=ALU.not_equal, fill=1.0,
                            pattern=[[-ROWS, GROUPS], [-1, ROWS]], channel_multiplier=1).then_inc(consts_c, 1)
            g.affine_select(out=big_id[:, :], in_=big_id[:, :], base=0, pattern=[[-1, P]],
                            compare_op=ALU.not_equal, fill=2.0 ** 60, channel_multiplier=1).then_inc(consts_c, 1)
            g.affine_select(out=dg[:, 0, :], in_=dg[:, 0, :], base=0, pattern=[[-1, P]],
                            compare_op=ALU.is_ge, fill=-2.0 ** 60, channel_multiplier=1).then_inc(consts_c, 1)
            g.affine_select(out=dg[:, 1, :], in_=dg[:, 1, :], base=0, pattern=[[1, P]],
                            compare_op=ALU.is_ge, fill=-2.0 ** 60, channel_multiplier=-1).then_inc(consts_c, 1)

        NI = HF * NB
        EXTRA_MX = (5, 7, 11)
        MX_AT = [[] for _ in range(NT)]
        for u in range(NT):
            MX_AT[[k for k in range(13) for _ in range(1 + (k in EXTRA_MX))][u]].append(u)
        MX_BANK = [7 if u in [x[1] for x in MX_AT if len(x) > 1] else 4 for u in range(NT)]
        MX_LAST = [max([w for w in range(u) if MX_BANK[w] == MX_BANK[u]], default=None) for u in range(NT)]

        def first_units():
            steps = []
            for kt in range(NT):
                steps.append([(0, kt + 2, q) for q in range(2) if kt + 2 < NT])
                if kt >= 8:
                    steps[-1].append((1, (kt - 8) // 2, kt % 2))
            return steps

        HEAD_START = [(0, t, q) for t in range(2) for q in range(2)]
        FIRST = first_units()
        FIRST_DONE = [(h, t) for h, t, q in HEAD_START + [u for st in FIRST for u in st] if q == 1]

        def parts(i):
            lo, hi = (i, i) if isinstance(i, int) else (i.min_val, i.max_val)
            return dict(att=hi < NI, mx=hi + 1 < NI, y=hi + 2 < NI, v=hi < NI - NB, o=lo >= 1)

        def f_mx(i):
            return parts(i)["mx"]

        def unit_base(i):
            if isinstance(i, int) and i == 0:
                return 2 * NT
            lo = i if isinstance(i, int) else i.min_val
            if lo < NI - NB:
                return i * 16 + (2 * NT + 8 - 16)
            return i * 8 + (2 * NT + 8 - 16 + 8 * (NI - NB))

        def over_iterations(eng, body):
            body(0)
            body(1)
            with eng.Fori(2, NI - NB) as i:
                body(i)
            with eng.Fori(NI - NB, NI - 2) as i:
                body(i)
            body(NI - 2)
            body(NI - 1)
            body(NI)

        def switch_tensor(pe, k):
            s = f_s[k]

            def queries(j):
                h, b = quarter(j), j & 3
                xs = [x[:, ds(b * BLK, BLK)] for x in (x_hi, x_lo)]
                pe.matmul(B[7][:, :], m_hi[:, h, :], xs[0], start=True, stop=False)
                pe.matmul(B[7][:, :], m_hi[:, h, :], xs[1], start=False, stop=False)
                pe.matmul(B[7][:, :], m_lo[:, h, :], xs[0], start=False, stop=True).then_inc(s["y_ps"], 1)

            def max_unit(j, u, bank, ready=None):
                t, kb = u // NB, u % NB
                if u == 0:
                    pe.wait_ge(s["y_hi"], j + 1)
                if ready is not None:
                    pe.wait_ge(s["mx"], ready)
                pe.matmul(B[bank][:, :], y_hi[:, j & 3, t * P:(t + 1) * P], xk_hi[:, kb * BLK:(kb + 1) * BLK],
                          start=True, stop=True).then_inc(s["mx_ps"], 1)

            def shift_rows(j):
                pe.wait_ge(s["shift"], j + 1)
                for t in range(TPB):
                    mm = pe.matmul(B[7][0:1, t * P:(t + 1) * P], shift[:, t:t + 1], ident16[:, :],
                                   start=True, stop=True)
                mm.then_inc(s["sh_ps"], 1)

            def scores(j, kt):
                if kt == 0:
                    pe.wait_ge(s["row"], j + 1)
                    pe.wait_ge(s["y_lo"], j + 1)
                if not (isinstance(j, int) and 16 * j + kt < 2):
                    pe.wait_ge(s["p"], j * 16 + (kt - 1))
                o, ks, b = B[kt % 2][:, :], slice(kt * P, (kt + 1) * P), j & 3
                pe.matmul(o, xk_hi[:, ks], y_hi[:, b, :], start=True, stop=False)
                pe.matmul(o, xk_hi[:, ks], y_lo[:, b, :], start=False, stop=False)
                pe.matmul(o, xk_lo[:, ks], y_hi[:, b, :], start=False, stop=True).then_inc(s["st_ps"], 1)

            def context(i, kt):
                n = i * 16 + kt
                if kt == 0:
                    if not (isinstance(i, int) and i == 0):
                        pe.wait_ge(s["c_raw"], i * 2)
                    if not (isinstance(i, int) and i == 0):
                        pe.wait_ge(s["v_lo"], quarter(i) * NT + NT)
                if isinstance(i, int) and i == 0:
                    pe.wait_ge(s["v_lo"], FIRST_DONE.index((0, kt)) + 1)
                pe.wait_ge(s["p_lo"], n + 1)
                slot = quarter(i) & 1
                vh = v_hi[:, slot, kt, 0:P + 1]
                vl = v_lo[:, slot, kt, :]
                for t in range(TPB):
                    o = B[2 + t // 2][:, (t % 2) * (P + 1):(t % 2 + 1) * (P + 1)]
                    ph = top_half(p32[:, kt % 4, t * P:(t + 1) * P])
                    pl = p_lo[:, kt % 4, t * P:(t + 1) * P]
                    pe.matmul(o, ph, vh, start=(kt == 0 and t % 2 == 0), stop=False, skip_group_check=True)
                    pe.matmul(o[:, 0:P], ph, vl, start=False, stop=False, skip_group_check=True)
                    mm = pe.matmul(o, pl, vh, start=False, stop=(kt == NT - 1), skip_group_check=True)
                mm.then_inc(s["pv_ps"], 1)

            def unit(n, par, parts3, w_hi, w_lo, first):
                if not first:
                    pe.wait_ge(s["gated"], n * 4 - 4)
                hi, lo = parts3
                o = B[5 + par][:, :]
                wh, wl = (w.rearrange("p a b -> p (a b)") for w in (w_hi, w_lo))
                pe.matmul(o, hi, wh, start=True, stop=False)
                pe.matmul(o, hi, wl, start=False, stop=False)
                pe.matmul(o, lo, wh, start=False, stop=True).then_inc(s["vo_ps"], 1)

            def v_unit(n, par, h, t, q, first=False):
                ts = ds(t * P, P)
                ws = ds(h * EX + 4 * q, 4)
                unit(n, par, (x_hi[:, ts], x_lo[:, ts]), vw_hi[:, ws, :], vw_lo[:, ws, :], first)

            def o_unit(n, par, h, t, q):
                ts = slice(t * P, (t + 1) * P)
                ws = ds(h * EX + 4 * q, 4)
                unit(n, par, (cT[:, 0, ts], cT[:, 1, ts]), ow_hi[:, ws, :], ow_lo[:, ws, :], False)

            def turn_context(i):
                if parts(i)["att"]:
                    pe.wait_ge(s["row"], i + 1)
                pe.wait_ge(s["c_hi"], i)
                pe.wait_ge(s["c_lo"], i)
                turned = B[7][:, :].bitcast(F16)
                for w in range(2):
                    for t in range(TPB):
                        mm = pe.transpose(turned[:, w * BLK + t * P:w * BLK + (t + 1) * P],
                                          c16[:, w, t, :], ident16[:, :])
                mm.then_inc(s["ct_ps"], 1)

            def max_at(i, kt, second):
                if not f_mx(i) or len(MX_AT[kt]) <= second:
                    return
                u = MX_AT[kt][second]
                if u == 0 or MX_BANK[u] == 4:
                    ready = i * 16 + (17 + MX_LAST[u]) if u else i * 16 + 16
                else:
                    f = parts(i)
                    if kt < 8 and f["o"]:
                        pe.wait_ge(s["ct"], i)
                    elif kt > 8 and f["y"]:
                        pe.wait_ge(s["y_lo"], i + 3)
                    ready = None if MX_LAST[u] is None else i * 16 + (17 + MX_LAST[u])
                max_unit(i + 1, u, MX_BANK[u], ready)

            def body(i):
                f = parts(i)
                first = isinstance(i, int) and i == 0
                ub = unit_base(i)
                n0 = len(HEAD_START)
                for kt in range(NT):
                    if first:
                        if kt == 8 and k == 0:
                            pe.wait_ge(e_lo, 2 * HF)
                        for h, t, q in FIRST[kt]:
                            v_unit(n0, n0 % 2, h, t, q)
                            n0 += 1
                    elif f["v"] and kt < 8:
                        v_unit(ub + kt, kt % 2, quarter(i) + 1, (i & 3) * TPB + kt // 2, kt % 2)
                    max_at(i, kt, 0)
                    if f["o"] and kt == 3:
                        turn_context(i)
                    if f["o"] and kt >= 8:
                        if kt == 8:
                            pe.wait_ge(s["ct"], i)
                        j = i - 1
                        m = kt - 8
                        o_unit(ub + (8 if f["v"] else 0) + m, m % 2, quarter(j), m // 2, m % 2)
                    if f["y"] and kt == 8:
                        pe.wait_ge(s["mx"], i * 16 + (17 + MX_AT[7][1]))
                        queries(i + 2)
                    if f["mx"] and kt == 13:
                        pe.wait_ge(s["mx"], i * 16 + 32)
                        shift_rows(i + 1)
                    if f["att"]:
                        context(i, kt)
                        max_at(i, kt, 1)
                        if kt < NT - 2:
                            scores(i, kt + 2)
                        elif f["mx"]:
                            scores(i + 1, kt + 2 - NT)

            pe.wait_ge(ln_s["xn"], NT * (2 + 3 * k))
            for b in range(NB):
                for t in range(TPB):
                    mm = pe.transpose(B[b][:, t * P:(t + 1) * P], xn[:, b * TPB + t, :], ident[:, :])
                mm.then_inc(s["xt_ps"], 1)
            for b in range(NB):
                pe.wait_ge(s["xt"], b + 1)
                for t in range(TPB):
                    tt = b * TPB + t
                    mm = pe.matmul(B[4 + b][:, t * P:(t + 1) * P], xT[:, tt * P:(tt + 1) * P], selT[:, :],
                                   start=True, stop=True)
                mm.then_inc(s["lg_ps"], 1)
            pe.wait_ge(s["lg"], NB)
            pe.wait_ge(s["x_lo"], NB)
            queries(0)
            pe.wait_ge(s["y_lo"], 1)
            queries(1)
            pe.wait_ge(s["xk"], 4)
            for u in range(NT):
                max_unit(0, u, 4 + u % 3, u - 2 if u >= 3 else None)
            pe.wait_ge(s["y_lo"], 2)
            shift_rows(0)
            scores(0, 0)
            scores(0, 1)
            if k == 0:
                pe.wait_ge(e_lo, 1)
            pe.wait_ge(s["mx"], NT)
            for n, (h, t, q) in enumerate(HEAD_START):
                v_unit(n, n % 2, h, t, q, first=n < 2)
            over_iterations(pe, body)

        def first_parts(kt, v_part):
            done = 2 + sum(q == 1 for st in FIRST[:kt] for _, _, q in st)
            for h, t, q in FIRST[kt]:
                if q == 1:
                    v_part(h, t, done % TPB, done)
                    done += 1

        def switch_scalar(a, k):
            s = f_s[k]
            norm_scalar(a, 1 + 3 * k)
            for b in range(NB):
                bs = slice(b * BLK, (b + 1) * BLK)
                a.wait_ge(s["xt_ps"], b + 1)
                a.activation(xT[:, bs], B[b][:, :], ACT.Copy).then_inc(s["xt"], 1)
                a.activation(x_hi[:, bs], B[b][:, :], ACT.Copy, scale=G_X).then_inc(s["x_hi"], 1)
            for b in range(NB):
                a.wait_ge(s["lg_ps"], b + 1)
                a.activation(gp[:, b * TPB:(b + 1) * TPB, :].rearrange("p a b -> p (a b)"), B[4 + b][:, :],
                             ACT.Sigmoid).then_inc(s["lg"], 1)

            def queries(j):
                a.wait_ge(s["y_ps"], j + 1)
                a.activation(y_hi[:, j & 3, :], B[7][:, :], ACT.Copy,
                             scale=G_Y / (G_X * G_W)).then_inc(s["y_hi"], 1)

            def row(j):
                a.wait_ge(s["sh_ps"], j + 1)
                a.activation(y_hi[0:1, j & 3, :], B[7][0:1, :], ACT.Copy).then_inc(s["row"], 1)

            def exps(j, kt):
                n = j * 16 + kt
                a.wait_ge(s["st_ps"], n + 1)
                early = isinstance(j, int) and j == 0
                if not (early and kt < 4):
                    a.wait_ge(s["pv_ps"], n - 3)
                a.activation(p32[:, kt % 4, :], B[kt % 2][:, :], ACT.Exp,
                             scale=1.0 / G_S).then_inc(s["p"], 1)

            def v_part(h, t, tt, n):
                a.wait_ge(s["vsum"], n + 1)
                a.activation(v_hi[:, h & 1, t, 0:P], v32[:, tt, :], ACT.Copy).then_inc(s["v_hi"], 1)

            def body(i):
                f = parts(i)
                for kt in range(NT):
                    if f["att"] and kt == NT - 1:
                        a.wait_ge(s["pv_ps"], i * 16 + 16)
                        if f["o"]:
                            a.wait_ge(s["c32"], i)
                        for t in range(2):
                            a.activation(c_raw[:, 2 * t:2 * t + 2, :].rearrange("p a b -> p (a b)"),
                                         B[2 + t][:, 0:2 * (P + 1)], ACT.Copy).then_inc(s["c_raw"], 1)
                    if f["mx"] and kt == 13:
                        row(i + 1)
                    if f["att"]:
                        if kt < NT - 2:
                            exps(i, kt + 2)
                        elif f["mx"]:
                            exps(i + 1, kt + 2 - NT)
                    if f["o"] and kt == 1:
                        a.wait_ge(s["c32"], i)
                        a.activation(c16[:, 0, :, :].rearrange("p a b -> p (a b)"),
                                     c32[:, :, :].rearrange("p a b -> p (a b)"), ACT.Copy).then_inc(s["c_hi"], 1)
                    if f["o"] and kt == 4:
                        a.wait_ge(s["ct_ps"], i)
                        a.activation(cT[:, :, :].rearrange("p a b -> p (a b)"),
                                     B[7][:, :].bitcast(F16), ACT.Copy).then_inc(s["ct"], 1)
                    if isinstance(i, int) and i == 0:
                        first_parts(kt, v_part)
                    elif f["v"] and kt in (2, 4, 6, 8):
                        tt = kt // 2 - 1
                        v_part(quarter(i) + 1, (i & 3) * TPB + tt, tt, i * TPB + (NT + tt))
                    if f["y"] and kt == 8:
                        queries(i + 2)

            queries(0)
            queries(1)
            if k == 0:
                experts_scalar(a, 8, 2 * HF)
            row(0)
            exps(0, 0)
            exps(0, 1)
            a.wait_ge(s["ones"], 1)
            for n in range(2):
                v_part(0, n, n, n)
            over_iterations(a, body)

        def switch_pool(g, k):
            s = f_s[k]

            def p_part(j, kt):
                g.wait_ge(s["p"], j * 16 + (kt + 1))
                if not (isinstance(j, int) and j == 0 and kt < 4):
                    g.wait_ge(s["pv_ps"], j * 16 + (kt - 3))
                g.tensor_tensor(p_lo[:, kt % 4, :], p32[:, kt % 4, :], top_half(p32[:, kt % 4, :]),
                                ALU.subtract).then_inc(s["p_lo"], 1)

            def v_part(h, t, tt, n):
                g.wait_ge(s["v_hi"], n + 1)
                g.tensor_tensor(v_lo[:, h & 1, t, :], v32[:, tt, :], v_hi[:, h & 1, t, 0:P],
                                ALU.subtract).then_inc(s["v_lo"], 1)

            def body(i):
                f = parts(i)
                for kt in range(NT):
                    if f["att"]:
                        if kt < NT - 2:
                            p_part(i, kt + 2)
                        elif f["mx"]:
                            p_part(i + 1, kt + 2 - NT)
                    if isinstance(i, int) and i == 0:
                        first_parts(kt, v_part)
                    elif f["v"] and kt in (3, 5, 7, 9):
                        tt = kt // 2 - 1
                        v_part(quarter(i) + 1, (i & 3) * TPB + tt, tt, i * TPB + (NT + tt))

            g.wait_ge(s["xk"], 2)
            g.memset(xk_hi[0:1, :], ONE_K).then_inc(s["xk"], 1)
            g.memset(xk_lo[0:1, :], 0.0).then_inc(s["xk"], 1)
            p_part(0, 0)
            p_part(0, 1)
            for n in range(2):
                v_part(0, n, n, n)
            over_iterations(g, body)

        def switch_vector(v, k):
            s = f_s[k]
            prev = a_s["res"] if k == 0 else c_s["res"]
            v.wait_ge(prev, NB)
            norm_vector(v, 1 + 3 * k, x_res, xn)
            for b in range(NB):
                bs = slice(b * BLK, (b + 1) * BLK)
                v.wait_ge(s["x_hi"], b + 1)
                v.scalar_tensor_tensor(x_lo[:, bs], B[b][:, :], G_X, x_hi[:, bs],
                                       ALU.mult, ALU.subtract).then_inc(s["x_lo"], 1)
            v.wait_ge(s["x_lo"], NB)
            v.tensor_copy(xk_hi[:, :], x_hi[:, :]).then_inc(s["xk"], 1)
            v.tensor_copy(xk_lo[:, :], x_lo[:, :]).then_inc(s["xk"], 1)
            v.memset(v_hi[:, :, :, P:P + 1], G_X / G_C).then_inc(s["ones"], 1)
            for e in range(EX):
                v.memset(tie[:, e:e + 1], float(EX - e)).then_inc(s["choice"], 1)
            chain = [EX]

            def link(ins):
                ins.then_inc(s["choice"], 1)
                chain[0] += 1
                v.wait_ge(s["choice"], chain[0])

            def queries(j):
                v.wait_ge(s["y_hi"], j + 1)
                v.scalar_tensor_tensor(y_lo[:, j & 3, :], B[7][:, :], G_Y / (G_X * G_W), y_hi[:, j & 3, :],
                                       ALU.mult, ALU.subtract).then_inc(s["y_lo"], 1)

            def max_unit(j, u, bank):
                v.wait_ge(s["mx_ps"], j * 16 + (u + 1))
                v.tensor_reduce(mx[:, u // NB, u % NB:u % NB + 1], B[bank][:, :], AX.X,
                                ALU.max).then_inc(s["mx"], 1)

            def shift_of(j):
                v.wait_ge(s["mx"], j * 16 + 16)
                v.tensor_reduce(negm[:, :], mx[:, :, :], AX.X, ALU.max, negate=True).then_inc(s["negm"], 1)
                v.wait_ge(s["negm"], j + 1)
                v.tensor_scalar(shift[:, :], negm[:, :], G_M / G_S, G_M * LOG_P,
                                ALU.mult, ALU.add).then_inc(s["shift"], 1)

            def choose(half, h0, h1, gain):
                nh = h1 - h0
                cs = slice(half * 64 + h0 * EX, half * 64 + h1 * EX)
                prob = gp[:, :, cs]
                g_out = gates[:, :, cs]
                four = lambda x: x.rearrange("p t (h e) -> p t h e", e=EX)
                one = lambda n: g1[:, n, 0:NT * nh]
                over = lambda n: one(n).rearrange("p (t h a) -> p t h a", h=nh, a=1).broadcast_to([P, NT, nh, EX])
                ties = tie[:, :].rearrange("p (a b e) -> p a b e", a=1, b=1).broadcast_to([P, NT, nh, EX])
                A, C = gt[:, 0, :, 0:nh * EX], gt[:, 1, :, 0:nh * EX]
                link(v.tensor_reduce(one(0), four(prob), AX.X, ALU.max))
                link(v.tensor_tensor(four(A), four(prob), over(0), ALU.is_equal))
                link(v.tensor_tensor(four(C), four(A), ties, ALU.mult))
                link(v.tensor_reduce(one(1), four(C), AX.X, ALU.max))
                link(v.tensor_tensor(four(A), four(C), over(1), ALU.is_equal))
                link(v.scalar_tensor_tensor(C, A, -4.0, prob, ALU.mult, ALU.add))
                link(v.tensor_reduce(one(0), four(C), AX.X, ALU.max))
                link(v.tensor_tensor(four(g_out), four(C), over(0), ALU.is_equal))
                link(v.tensor_tensor(four(C), four(g_out), ties, ALU.mult))
                link(v.tensor_reduce(one(1), four(C), AX.X, ALU.max))
                link(v.tensor_tensor(four(g_out), four(C), over(1), ALU.is_equal))
                link(v.tensor_tensor(C, A, g_out, ALU.add))
                link(v.tensor_tensor(A, C, prob, ALU.mult))
                link(v.tensor_reduce(one(0), four(A), AX.X, ALU.add))
                link(v.tensor_scalar(one(1), one(0), 1e-9, None, ALU.max))
                link(v.reciprocal(one(0), one(1)))
                link(v.tensor_scalar(one(1), one(0), rs_col[:, 0:1], gain, ALU.mult, ALU.mult))
                link(v.tensor_tensor(four(g_out), four(A), over(1), ALU.mult))

            def gate_unit(n, par, tile, col, q, even, odd):
                v.wait_ge(s["vo_ps"], n + 1)
                for r in range(4):
                    acc = (even, odd)[r % 2]
                    ps = B[5 + par][:, r * P:(r + 1) * P]
                    gate = gates[:, tile, ds(col + r, 1)]
                    fresh = q == 0 and r < 2 and (acc is odd or even is not odd and fresh_even[0])
                    if fresh:
                        v.tensor_scalar(acc, ps, gate, None, ALU.mult).then_inc(s["gated"], 1)
                    else:
                        if not (q == 0 and r < 2):
                            v.wait_ge(s["gated"], n * 4 + (r - 1))
                        v.scalar_tensor_tensor(acc, ps, gate, acc, ALU.mult, ALU.add).then_inc(s["gated"], 1)
                if q == 1:
                    v.wait_ge(s["gated"], n * 4 + 4)

            fresh_even = [True]

            def v_gates(n, par, h, t, tt, q, first):
                fresh_even[0] = True
                gate_unit(n, par, t, h * EX + 4 * q, q, va[:, tt, 0, :], va[:, tt, 1, :])
                if q == 1:
                    if first is not None:
                        v.wait_ge(s["v_lo"], first)
                    v.tensor_tensor(v32[:, tt, :], va[:, tt, 0, :], va[:, tt, 1, :], ALU.add).then_inc(s["vsum"], 1)

            def o_gates(n, par, h, t, tt, q):
                fresh_even[0] = False
                xr = x_res[:, t, :]
                gate_unit(n, par, t, P // 2 + h * EX + 4 * q, q, xr, o_b[:, tt % 2, :])
                if q == 1:
                    v.tensor_tensor(xr, xr, o_b[:, tt % 2, :], ALU.add).then_inc(s["res"], 1)

            def max_at(i, kt, second):
                if f_mx(i) and len(MX_AT[kt]) > second:
                    u = MX_AT[kt][second]
                    max_unit(i + 1, u, MX_BANK[u])

            v_gain, o_gain = G_X / (G_X * G_W), 1.0 / (G_C * G_W)

            def body(i):
                f = parts(i)
                first = isinstance(i, int) and i == 0
                ub = unit_base(i)
                n0 = len(HEAD_START)
                done = n0 // 2
                j = i - 1
                if isinstance(i, int) and i == 1:
                    choose(0, 2, HF, v_gain)
                for kt in range(NT):
                    if first:
                        for h, t, q in FIRST[kt]:
                            slot = FIRST_DONE.index((h, t))
                            v_gates(n0, n0 % 2, h, t, slot % TPB, q, slot - TPB + 1 if slot >= TPB else None)
                            n0 += 1
                    elif f["v"] and kt < 8:
                        tt = kt // 2
                        v_gates(ub + kt, kt % 2, quarter(i) + 1, (i & 3) * TPB + tt, tt, kt % 2,
                                i * TPB + (NT + tt - TPB + 1))
                    max_at(i, kt, 0)
                    if f["mx"] and kt == 12:
                        shift_of(i + 1)
                    if f["o"] and kt == 1:
                        v.wait_ge(s["c_raw"], i * 2)
                        v.reciprocal(c_rec[:, :], c_raw[:, :, P]).then_inc(s["c_rec"], 1)
                        v.wait_ge(s["c_rec"], i)
                        v.tensor_tensor(c32[:, :, :], c_raw[:, :, 0:P],
                                        c_rec[:, :].rearrange("p (t a) -> p t a", a=1).broadcast_to([P, TPB, P]),
                                        ALU.mult).then_inc(s["c32"], 1)
                    if f["o"] and kt == 2:
                        v.wait_ge(s["c_hi"], i)
                        v.tensor_tensor(c16[:, 1], c32[:, :, :], c16[:, 0], ALU.subtract).then_inc(s["c_lo"], 1)
                    if f["o"] and kt >= 8:
                        m = kt - 8
                        if m == 0 and not (isinstance(i, int) and i == 1):
                            v.wait_ge(s["res"], j * TPB)
                        o_gates(ub + (8 if f["v"] else 0) + m, m % 2, quarter(j), (j & 3) * TPB + m // 2,
                                m // 2, m % 2)
                    max_at(i, kt, 1)
                    if f["y"] and kt == 8:
                        queries(i + 2)
                if first:
                    choose(1, 0, HF, o_gain)

            v.wait_ge(s["lg"], NB)
            queries(0)
            queries(1)
            for u in range(NT):
                max_unit(0, u, 4 + u % 3)
            shift_of(0)
            choose(0, 0, 2, v_gain)
            for n, (h, t, q) in enumerate(HEAD_START):
                v_gates(n, n % 2, h, t, t, q, None)
            over_iterations(v, body)

        UNITS = [(t, kb) for t in range(NT) for kb in range(t // TPB + 1)]
        STEPS = [(b, kt) for b in range(NB) for kt in range(TPB * (b + 1))]
        NS = len(STEPS)
        EXTRA_C = 6
        UNIT_AT = [[] for _ in range(NS)]
        for u in range(NS):
            UNIT_AT[[k for k in range(NS - EXTRA_C) for _ in range(1 + (k % 5 == 4))][u]].append(u)
        SHIFT_AT = [next(k for k in range(NS) if 2 * (b + 1) * (b + 2) - 1 in UNIT_AT[k]) for b in range(NB)]
        ROW_AT = [k + 2 for k in SHIFT_AT]
        SCORE_BANK = (0, 1, 3, 6)
        LO_AHEAD = 3

        ON_VECTOR = [n % 3 == 2 for n in range(NS)]
        LO_RANK = [sum(x == ON_VECTOR[n] for x in ON_VECTOR[:n + 1]) for n in range(NS)]

        def lo_part(eng, s, h, n):
            _, q0, q1, _ = step_span(n)
            slot = n % SLOTS_C
            eng.wait_ge(s["p"], h * NS + (n + 1))
            eng.tensor_tensor(pl_c[:, slot, 0:q1 - q0], p_c[:, slot, 0:q1 - q0],
                              top_half(p_c[:, slot, 0:q1 - q0]),
                              ALU.subtract).then_inc(s["lo_v" if ON_VECTOR[n] else "lo_g"], 1)

        def lo_parts(eng, s, h, n, nxt, vector):
            m = (n + LO_AHEAD) % NS
            if ON_VECTOR[m] == vector and (n + LO_AHEAD < NS or nxt):
                lo_part(eng, s, h if n + LO_AHEAD < NS else h + 1, m)

        def unit_span(u):
            t, kb = UNITS[u]
            return t, kb, min(BLK, (t + 1) * P - kb * BLK)

        def step_span(n):
            b, kt = STEPS[n]
            return kt, max(b * BLK, kt * P), (b + 1) * BLK, kt * P >= b * BLK

        def over_heads(eng, body):
            body(0, True, True)
            with eng.Fori(1, HA - 2) as h:
                body(h, True, True)
            body(HA - 2, True, False)
            body(HA - 1, False, False)

        def causal_tensor(pe):
            s = c_s
            for b in range(NB):
                pe.wait_ge(ln_s["xn"], 3 * NT + (b + 1) * TPB)
                for t in range(TPB):
                    mm = pe.transpose(B[b][:, t * P:(t + 1) * P], xn[:, b * TPB + t, :], ident[:, :])
                mm.then_inc(s["xt_ps"], 1)
            pe.wait_ge(ld_c, 48)

            def keys_queries(n):
                b = n % NB
                pe.wait_ge(s["xt"], b + 1)
                if n >= 2:
                    pe.wait_ge(s["kq_lo"], n - 1)
                pe.matmul(B[4 + n % 2][:, :], wbkv[:, 0:P] if n < NB else wbq[:, :],
                          xT[:, b * BLK:(b + 1) * BLK], start=True, stop=True).then_inc(s["kq_ps"], 1)

            def stack(n):
                kind = n // NB
                pe.wait_ge(s["kq_lo"], n + 1)
                for g in range(GROUPS):
                    m = GROUPS * n + g
                    if m >= 4:
                        pe.wait_ge(s["st_v" if m % 2 else "st_a"], (m - 4) // 2 + 1)
                    for part, kq in ((0, kq_hi), (1, kq_lo)):
                        mm = pe.matmul(B[m % 4][:, :], place[:, kind, part, g * P:(g + 1) * P],
                                       kq[:, n % 2, :], start=part == 0, stop=part == 1)
                    mm.then_inc(s["st_ps"], 1)

            keys_queries(0)
            keys_queries(1)
            pe.wait_ge(s["xt"], NB)
            pe.wait_ge(consts_c, 11)
            for n in range(2 * NB):
                stack(n)
                if n + 2 < 2 * NB:
                    keys_queries(n + 2)
                b = n - 2
                if 0 <= b < NB:
                    if b >= 2:
                        pe.wait_ge(s["v_lo"], b - 1)
                    for t in range(TPB):
                        tt = b * TPB + t
                        mm = pe.matmul(B[6 + b % 2][:, t * P:(t + 1) * P], xT[:, tt * P:(tt + 1) * P],
                                       wbkv[:, P:2 * P], start=True, stop=True)
                    mm.then_inc(s["v_ps"], 1)

            def max_unit(h, u):
                t, kb, w = unit_span(u)
                if u == 0:
                    pe.wait_ge(s["qh"], h + 1)
                if not (isinstance(h, int) and h == 0 and u < 2):
                    pe.wait_ge(s["mx"], h * NS + (u - 1))
                o = B[4 + u % 2]
                last = kb == t // TPB
                mm = pe.matmul(o[:, 0:w], q_hd[:, h & 1, t * P:(t + 1) * P],
                               k_st[:, quarter(h), kb * BLK:kb * BLK + w], start=True, stop=not last)
                if last:
                    mm = pe.matmul(o[:, w - P:w], big_id[:, :], dg[:, 0, :], start=False, stop=True)
                mm.then_inc(s["mx_ps"], 1)

            def shift_rows(h, b):
                pe.wait_ge(s["shift"], h * NB + (b + 1))
                if not (isinstance(h, int) and h == 0 and b == 0):
                    pe.wait_ge(s["row"], h * NB + b)
                for t in range(TPB):
                    mm = pe.matmul(B[7][0:1, t * P:(t + 1) * P], csh[:, b * TPB + t:b * TPB + t + 1],
                                   ident16[:, :], start=True, stop=True)
                mm.then_inc(s["sh_ps"], 1)

            def scores(h, n):
                kt, q0, q1, diag = step_span(n)
                if kt == 0:
                    pe.wait_ge(s["row"], h * NB + (STEPS[n][0] + 1))
                if not (isinstance(h, int) and h == 0 and n < 4):
                    pe.wait_ge(s["p"], h * NS + (n - 3))
                o = B[SCORE_BANK[n % 4]]
                mm = pe.matmul(o[:, 0:q1 - q0], k_st[:, quarter(h), kt * P:(kt + 1) * P],
                               q_hd[:, h & 1, q0:q1], start=True, stop=not diag)
                if diag:
                    mm = pe.matmul(o[:, 0:P], big_id[:, :], dg[:, 1, :], start=False, stop=True)
                mm.then_inc(s["s_ps"], 1)

            def context(h, n):
                kt, q0, q1, _ = step_span(n)
                slot = n % SLOTS_C
                if n == 0 and not (isinstance(h, int) and h == 0):
                    pe.wait_ge(s["raw"], h)
                kind = ON_VECTOR[n]
                pe.wait_ge(s["lo_v" if kind else "lo_g"], h * ON_VECTOR.count(kind) + LO_RANK[n])
                for t in range(q0 // P, q1 // P):
                    c = t * P - q0
                    o = B[2][:, t * (2 * DA + 1):(t + 1) * (2 * DA + 1)]
                    pe.matmul(o, top_half(p_c[:, slot, c:c + P]), v17[:, kt, h, 0:2 * DA + 1],
                              start=(n == 0 and t == 0), stop=False, skip_group_check=True)
                    mm = pe.matmul(o[:, 0:DA + 1], pl_c[:, slot, c:c + P], v17[:, kt, h, 0:DA + 1],
                                   start=False, stop=(n == NS - 1), skip_group_check=True)
                mm.then_inc(s["pv_ps"], 1)

            def body(h, nxt, _):
                for n in range(NS):
                    if nxt:
                        for u in UNIT_AT[n]:
                            max_unit(h + 1, u)
                        if n in ROW_AT:
                            shift_rows(h + 1, ROW_AT.index(n))
                    context(h, n)
                    if n + AHEAD_C < NS:
                        scores(h, n + AHEAD_C)
                    elif nxt:
                        scores(h + 1, n + AHEAD_C - NS)

            for u in range(NS):
                max_unit(0, u)
            pe.wait_ge(s["v_lo"], NB)
            pe.wait_ge(s["st_a"], GROUPS * NB)
            pe.wait_ge(s["st_v"], GROUPS * NB)
            for b in range(NB):
                shift_rows(0, b)
            for n in range(AHEAD_C):
                scores(0, n)
            over_heads(pe, body)
            pe.wait_ge(s["o"], HA)
            for b in range(NB):
                for t in range(TPB):
                    mm = pe.transpose(B[4 + b % 2][:, t * P:(t + 1) * P], o_nat[:, b * TPB + t, :], ident[:, :])
                mm.then_inc(s["ot_ps"], 1)
                pe.wait_ge(s["ot"], b + 1)
                if b >= 2:
                    pe.wait_ge(s["res"], b - 1)
                for t in range(TPB):
                    tt = b * TPB + t
                    mm = pe.matmul(B[6 + b % 2][:, t * P:(t + 1) * P], xT[:, tt * P:(tt + 1) * P], wbo[:, :],
                                   start=True, stop=True)
                mm.then_inc(s["y_ps"], 1)

        def causal_scalar(a):
            s = c_s
            norm_scalar(a, 2)
            norm_scalar(a, 3)
            for b in range(NB):
                a.wait_ge(s["xt_ps"], b + 1)
                a.activation(xT[:, b * BLK:(b + 1) * BLK], B[b][:, :], ACT.Copy,
                             scale=g_col[:, 0:1]).then_inc(s["xt"], 1)

            def hi(n):
                a.wait_ge(s["kq_ps"], n + 1)
                if n >= 2:
                    a.wait_ge(s["st_ps"], GROUPS * (n - 1))
                a.activation(kq_hi[:, n % 2, :], B[4 + n % 2][:, :], ACT.Copy,
                             scale=G_X if n < NB else G_Y * SCALE_A).then_inc(s["kq_hi"], 1)

            hi(0)
            hi(1)
            for n in range(2 * NB):
                bs = slice(n % NB * BLK, (n % NB + 1) * BLK)
                for g in range(0, GROUPS, 2):
                    m = GROUPS * n + g
                    a.wait_ge(s["st_ps"], m + 1)
                    if n < NB:
                        a.activation(k_st[:, g, bs], B[m % 4][:, :], ACT.Identity,
                                     bias=row_one[:, 0:1]).then_inc(s["st_a"], 1)
                    else:
                        a.activation(q_st[:, g, bs], B[m % 4][:, :], ACT.Copy).then_inc(s["st_a"], 1)
                if n + 2 < 2 * NB:
                    hi(n + 2)
                b = n - 2
                if 0 <= b < NB:
                    if b == 0:
                        a.wait_ge(s["zero"], 1)
                    a.wait_ge(s["v_ps"], b + 1)
                    a.activation(v17[:, b * TPB:(b + 1) * TPB, :, 0:DA],
                                 B[6 + b % 2][:, :].rearrange("p (t h c) -> p t h c", t=TPB, h=HA), ACT.Copy,
                                 scale=G_X).then_inc(s["v_hi"], 1)

            def row(h, b):
                a.wait_ge(s["sh_ps"], h * NB + (b + 1))
                a.activation(q_hd[0:1, h & 1, b * BLK:(b + 1) * BLK], B[7][0:1, :],
                             ACT.Copy).then_inc(s["row"], 1)

            def exps(h, n):
                _, q0, q1, _ = step_span(n)
                a.wait_ge(s["s_ps"], h * NS + (n + 1))
                if not (isinstance(h, int) and h == 0 and n < SLOTS_C):
                    a.wait_ge(s["pv_ps"], h * NS + (n - (SLOTS_C - 1)))
                a.activation(p_c[:, n % SLOTS_C, 0:q1 - q0], B[SCORE_BANK[n % 4]][:, 0:q1 - q0], ACT.Exp,
                             scale=1.0 / G_S).then_inc(s["p"], 1)

            def body(h, nxt, _):
                for n in range(NS):
                    if nxt and n in ROW_AT:
                        row(h + 1, ROW_AT.index(n))
                    if n == NS - 1:
                        a.wait_ge(s["pv_ps"], h * NS + NS)
                        if not (isinstance(h, int) and h == 0):
                            a.wait_ge(s["o"], h)
                        a.activation(o_raw[:, :, :].rearrange("p a b -> p (a b)"),
                                     B[2][:, 0:NT * (2 * DA + 1)], ACT.Copy).then_inc(s["raw"], 1)
                    if n + AHEAD_C < NS:
                        exps(h, n + AHEAD_C)
                    elif nxt:
                        exps(h + 1, n + AHEAD_C - NS)

            for b in range(NB):
                row(0, b)
            for n in range(AHEAD_C):
                exps(0, n)
            over_heads(a, body)
            for b in range(NB):
                a.wait_ge(s["ot_ps"], b + 1)
                a.activation(xT[:, b * BLK:(b + 1) * BLK], B[4 + b % 2][:, :], ACT.Copy).then_inc(s["ot"], 1)

        def causal_pool(g):
            s = c_s

            def body(h, nxt, _):
                for n in range(NS):
                    lo_parts(g, s, h, n, nxt, False)

            for n in range(LO_AHEAD):
                if not ON_VECTOR[n]:
                    lo_part(g, s, 0, n)
            over_heads(g, body)

        def causal_vector(v):
            s = c_s
            v.wait_ge(f_s[0]["res"], NT * HF)
            norm_vector(v, 2, x_res, xn)
            v.wait_ge(ln_s["xn"], 3 * NT)
            norm_vector(v, 3, xn, xn)
            v.memset(v17[:, :, :, DA:DA + 1], G_X).then_inc(s["zero"], 1)
            v.memset(cmx[:, :, :], -3.0e38).then_inc(s["zero"], 1)
            v.wait_ge(consts_c, 11)
            v.tensor_reduce(hd_mask[:, :], hd_mk[:, :, :], AX.X, ALU.add).then_inc(s["zero"], 1)

            def lo(n):
                v.wait_ge(s["kq_hi"], n + 1)
                v.scalar_tensor_tensor(kq_lo[:, n % 2, :], B[4 + n % 2][:, :], G_X if n < NB else G_Y * SCALE_A,
                                       kq_hi[:, n % 2, :], ALU.mult, ALU.subtract).then_inc(s["kq_lo"], 1)

            lo(0)
            lo(1)
            for n in range(2 * NB):
                bs = slice(n % NB * BLK, (n % NB + 1) * BLK)
                for g in range(1, GROUPS, 2):
                    m = GROUPS * n + g
                    v.wait_ge(s["st_ps"], m + 1)
                    if n < NB:
                        v.tensor_scalar(k_st[:, g, bs], B[m % 4][:, :], row_one[:, 0:1], None,
                                        ALU.add).then_inc(s["st_v"], 1)
                    else:
                        v.tensor_copy(q_st[:, g, bs], B[m % 4][:, :]).then_inc(s["st_v"], 1)
                if n + 2 < 2 * NB:
                    lo(n + 2)
                b = n - 2
                if 0 <= b < NB:
                    v.wait_ge(s["v_hi"], b + 1)
                    v.scalar_tensor_tensor(
                        v17[:, b * TPB:(b + 1) * TPB, :, DA + 1:2 * DA + 1].rearrange("p t h c -> p (t h) c"),
                        B[6 + b % 2][:, :].rearrange("p (t c) -> p t c", c=DA), G_X,
                        v17[:, b * TPB:(b + 1) * TPB, :, 0:DA].rearrange("p t h c -> p (t h) c"),
                        ALU.mult, ALU.subtract).then_inc(s["v_lo"], 1)

            def head_queries(h):
                v.tensor_scalar(q_hd[:, h & 1, :], q_st[:, quarter(h), :], hd_mask[:, ds(h & 3, 1)], None,
                                ALU.mult).then_inc(s["qh"], 1)

            def max_unit(h, u):
                t, kb, w = unit_span(u)
                v.wait_ge(s["mx_ps"], h * NS + (u + 1))
                v.tensor_reduce(cmx[:, t, kb:kb + 1], B[4 + u % 2][:, 0:w], AX.X, ALU.max).then_inc(s["mx"], 1)

            def shift_of(h, b):
                bs = slice(b * TPB, (b + 1) * TPB)
                v.wait_ge(s["mx"], h * NS + 2 * (b + 1) * (b + 2))
                v.tensor_reduce(cneg[:, bs], cmx[:, bs, :], AX.X, ALU.max, negate=True).then_inc(s["neg"], 1)
                v.wait_ge(s["neg"], h * NB + (b + 1))
                v.tensor_scalar(csh[:, bs], cneg[:, bs], G_M / G_S, G_M * LOG_P,
                                ALU.mult, ALU.add).then_inc(s["shift"], 1)

            def outputs(h):
                v.wait_ge(s["raw"], h + 1)
                v.reciprocal(c_rec2[:, :], o_raw[:, :, DA]).then_inc(s["rec"], 1)
                v.tensor_tensor(o_sum[:, :, :], o_raw[:, :, 0:DA], o_raw[:, :, DA + 1:2 * DA + 1],
                                ALU.add).then_inc(s["rec"], 1)
                v.wait_ge(s["rec"], h * 2 + 2)
                v.tensor_tensor(o_nat[:, :, ds(h * DA, DA)], o_sum[:, :, :],
                                c_rec2[:, :].rearrange("p (t a) -> p t a", a=1).broadcast_to([P, NT, DA]),
                                ALU.mult).then_inc(s["o"], 1)

            def body(h, nxt, nxt2):
                for n in range(NS):
                    if nxt:
                        for u in UNIT_AT[n]:
                            max_unit(h + 1, u)
                        if n in SHIFT_AT:
                            shift_of(h + 1, SHIFT_AT.index(n))
                    lo_parts(v, s, h, n, nxt, True)
                    if n == 2 and not (isinstance(h, int) and h == 0):
                        outputs(h - 1)
                    if n == NS - AHEAD_C and nxt2:
                        v.wait_ge(s["s_ps"], h * NS + NS)
                        head_queries(h + 2)

            v.wait_ge(s["st_a"], GROUPS * NB)
            v.wait_ge(s["st_v"], GROUPS * NB)
            v.wait_ge(s["zero"], 3)
            head_queries(0)
            head_queries(1)
            for u in range(NS):
                max_unit(0, u)
            for b in range(NB):
                shift_of(0, b)
            for n in range(LO_AHEAD):
                if ON_VECTOR[n]:
                    lo_part(v, s, 0, n)
            over_heads(v, body)
            outputs(HA - 1)
            for b in range(NB):
                v.wait_ge(s["y_ps"], b + 1)
                xr = x_res[:, b * TPB:(b + 1) * TPB, :].rearrange("p a b -> p (a b)")
                v.tensor_tensor(xr, B[6 + b % 2][:, :], xr, ALU.add).then_inc(s["res"], 1)

        @block.sync
        def _(sp):
            loads(sp)
            sp.wait_ge(f_s[1]["res"], NT * HF)
            sp.dma_start(out.rearrange("b (t p) c -> p (b t) c", p=P), x_res[:, :, :]).then_inc(out_done, 16)
            sp.wait_ge(out_done, 16)

        @block.tensor
        def _(pe):
            linear_tensor(pe)
            switch_tensor(pe, 0)
            causal_tensor(pe)
            switch_tensor(pe, 1)

        @block.scalar
        def _(a):
            linear_scalar(a)
            switch_scalar(a, 0)
            causal_scalar(a)
            switch_scalar(a, 1)

        @block.vector
        def _(v):
            linear_vector(v)
            switch_vector(v, 0)
            causal_vector(v)
            switch_vector(v, 1)

        @block.gpsimd
        def _(g):
            constants_pool(g)
            experts_pool(g)
            causal_constants_pool(g)
            switch_pool(g, 0)
            causal_pool(g)
            switch_pool(g, 1)


_INS = ['L0_attn_a_x', 'L0_attn_a_Wq', 'L0_attn_a_bq', 'L0_attn_a_Wk', 'L0_attn_a_bk', 'L0_attn_a_Wv',
        'L0_attn_a_bv', 'L0_attn_a_Wo', 'L0_attn_a_bo', 'L0_attn_b_g_ln', 'L0_attn_b_Wq', 'L0_attn_b_Wkv',
        'L0_attn_b_Wo', 'L0_ffn_q_w', 'L0_ffn_k_w', 'L0_ffn_v_w', 'L0_ffn_o_w', 'L0_ffn_sel_v_w',
        'L0_ffn_sel_o_w', 'L0_ffn_route_scale']


def kernel(**inputs):
    import numpy as _np
    import concourse.bacc as _bacc
    from concourse import mybir as _mybir
    from concourse.bass_utils import run_bass_kernel_spmd as _run

    nc = _bacc.Bacc("TRN2", target_bir_lowering=False, num_devices=1)
    arrays, args = {}, []
    for name in _INS:
        a = _np.ascontiguousarray(inputs[name])
        arrays[f"in_{name}_dram"] = a
        args.append(nc.dram_tensor(f"in_{name}_dram", a.shape, _mybir.dt.from_np(a.dtype), kind="ExternalInput").ap())
    shape = inputs['L0_attn_a_x'].shape
    args.append(nc.dram_tensor("out_0_dram", shape, F32, kind="ExternalOutput").ap())
    hybrid_program(nc, *args)
    r = _run(nc, [arrays], core_ids=[0])
    return r.results[0]["out_0_dram"]
```

```python
from contextlib import ExitStack
import math

import concourse.bass as bass
from concourse import mybir

F32 = mybir.dt.float32
F16 = mybir.dt.float16
BF16 = mybir.dt.bfloat16
ALU = mybir.AluOpType
ACT = mybir.ActivationFunctionType
AX = mybir.AxisListType

P = 128
T = 2048
NT = T // P
BLK = 512
NB = T // BLK
TPB = BLK // P
EPS = 1e-5

HA = 16
DA = P // HA
SCALE_A = DA ** -0.5
ROWS = 32
GROUPS = P // ROWS

HF = 8
EX = 8
SCALE_F = P ** -0.5
QUADS = HF * EX // 4

G_X = 64.0
G_W = 1024.0
G_Y = 128.0
G_C = 256.0
G_S = G_X * G_Y
ONE_K = 2048.0
G_M = G_S / ONE_K
SLOTS_C = 8
AHEAD_C = 7
LOG_P = 8 * math.log(2.0)


def hybrid_program(nc, x_in, Wq, bq, Wk, bk, Wv, bv, Wo, bo, g_ln, Wbq, Wbkv, Wbo,
                   q_w, k_w, v_w, o_w, sel_v_w, sel_o_w, route_scale, out):
    with ExitStack() as ctx:
        def sem(name):
            return ctx.enter_context(nc.semaphore(name))

        def sb(name, shape, dt=F32, stack=ctx):
            return stack.enter_context(nc.sbuf_tensor(name, shape, dt))

        x_res = sb("x_res", [P, NT, P])
        xn = sb("xn", [P, NT, P])
        xT = sb("xT", [P, T])
        stats = sb("stats", [P, NT, 6])
        mv = sb("mv", [P, NT, 2])
        lnv = sb("lnv", [P, 7, NT])
        ident = sb("ident", [P, P])
        ident16 = sb("ident16", [P, P], F16)
        ones = sb("ones", [P, P])
        selT = sb("selT", [P, P])
        rs_col = sb("rs_col", [P, 1])
        m_hi = sb("m_hi", [P, HF, P], F16)
        m_lo = sb("m_lo", [P, HF, P], F16)
        vw_hi = sb("vw_hi", [P, HF * EX, P], F16)
        vw_lo = sb("vw_lo", [P, HF * EX, P], F16)
        ow_hi = sb("ow_hi", [P, HF * EX, P], F16)
        ow_lo = sb("ow_lo", [P, HF * EX, P], F16)
        wbq = sb("wbq", [P, P])
        wbkv = sb("wbkv", [P, 2 * P])
        wbo = sb("wbo", [P, P])
        g_col = sb("g_col", [P, 1])
        stage = sb("stage", [P, 4, EX * P])
        place = sb("place", [P, 2, 2, GROUPS * P], F16)
        row_one = sb("row_one", [P, 1])
        hd_mk = sb("hd_mk", [P, GROUPS, ROWS])
        dg = sb("dg", [P, 2, P], BF16)
        big_id = sb("big_id", [P, P], BF16)

        with ExitStack() as a:
            def sa(name, shape, dt=F32):
                return sb(name, shape, dt, a)
            w_nat = sa("w_nat", [P, 4, P])
            wT = sa("wT", [P, 4, P])
            sel_nat = sa("sel_nat", [P, P])
            bq_col = sa("bq_col", [P, 1])
            bkv_row = sa("bkv_row", [1, 2 * P])
            bo_row = sa("bo_row", [1, P])
            qk_w = sa("qk_w", [P, 2, HF, P])
            cen = sa("cen", [P, 2, HF])
            head_mask = sa("head_mask", [P, P])
            qT = sa("qT", [P, T])
            q_exp = sa("q_exp", [P, 2, BLK])
            q_pos = sa("q_pos", [P, 2, BLK])
            k_exp = sa("k_exp", [P, 2, 2, P])
            k_pos = sa("k_pos", [P, 2, 2, P])
            k_nat = sa("k_nat", [P, NT, P])
            v_nat = sa("v_nat", [P, NT, P + 1])
            kv_sb = sa("kv_sb", [P, P + HA])
            den = sa("den", [P, 2, TPB, HA])
            rden = sa("rden", [P, 2, TPB, HA])
            a_nat = sa("a_nat", [P, 2, TPB, P])
            aT = sa("aT", [P, T])

        with ExitStack() as a:
            def sf(name, shape, dt=F32):
                return sb(name, shape, dt, a)
            x_hi = sf("x_hi", [P, T], F16)
            x_lo = sf("x_lo", [P, T], F16)
            xk_hi = sf("xk_hi", [P, T], F16)
            xk_lo = sf("xk_lo", [P, T], F16)
            gates = sf("gates", [P, NT, P])
            gp = xn
            gt = sf("gt", [P, 2, NT, P // 2])
            g1 = sf("g1", [P, 3, NT * HF])
            tie = sf("tie", [P, EX])
            y_hi = sf("y_hi", [P, NB, BLK], F16)
            y_lo = sf("y_lo", [P, NB, BLK], F16)
            mx = sf("mx", [P, TPB, NB])
            negm = sf("negm", [P, TPB])
            shift = sf("shift", [P, TPB], F16)
            p32 = sf("p32", [P, 4, BLK])
            p_lo = sf("p_lo", [P, 4, BLK], F16)
            va = sf("va", [P, 4, 2, P])
            v32 = sf("v32", [P, 4, P])
            v_hi = sf("v_hi", [P, 2, NT, P + 2], F16)
            v_lo = sf("v_lo", [P, 2, NT, P], F16)
            o_b = sf("o_b", [P, 2, P])
            c_raw = sf("c_raw", [P, TPB, P + 1])
            c_rec = sf("c_rec", [P, TPB])
            c32 = sf("c32", [P, TPB, P])
            c16 = sf("c16", [P, 2, TPB, P], F16)
            cT = sf("cT", [P, 2, BLK], F16)

        with ExitStack() as a:
            def sc(name, shape, dt=F32):
                return sb(name, shape, dt, a)
            kq_hi = sc("kq_hi", [P, 2, BLK], F16)
            kq_lo = sc("kq_lo", [P, 2, BLK], F16)
            k_st = sc("k_st", [P, GROUPS, T], F16)
            q_st = sc("q_st", [P, GROUPS, T], F16)
            q_hd = sc("q_hd", [P, 2, T], F16)
            hd_mask = sc("hd_mask", [P, GROUPS])
            v17 = sc("v17", [P, NT, HA, 2 * DA + 2], F16)
            cmx = sc("cmx", [P, NT, NB])
            cneg = sc("cneg", [P, NT])
            csh = sc("csh", [P, NT], F16)
            p_c = sc("p_c", [P, SLOTS_C, BLK])
            pl_c = sc("pl_c", [P, SLOTS_C, BLK], F16)
            o_raw = sc("o_raw", [P, NT, 2 * DA + 1])
            o_sum = sc("o_sum", [P, NT, DA])
            c_rec2 = sc("c_rec2", [P, NT])
            o_nat = xn

        B = [ctx.enter_context(nc.psum_tensor(f"bank{i}", [P, BLK], F32)) for i in range(8)]
        ds = bass.ds

        def quarter(i):
            return i >> 2 if isinstance(i, int) else (i >> 2).with_bounds(min_val=i.min_val >> 2, max_val=i.max_val >> 2)

        ld_x, ld_w, ld_qk, ld_b, ld_c = (sem("ld_" + n) for n in ("x", "w", "qk", "b", "c"))
        ld_e = [sem(f"ld_e{n}") for n in range(4)]
        e_up, e_hi, e_lo = sem("e_up"), sem("e_hi"), sem("e_lo")
        zeroed = sem("zeroed")
        consts = sem("consts")
        consts_c = sem("consts_c")
        vconst = sem("vconst")
        qk_cen = sem("qk_cen")
        out_done = sem("out_done")
        a_s = {n: sem("a_" + n) for n in (
            "wt_ps", "wt", "sel_ps", "sel", "xt_ps", "xt", "m_ps", "m_hi", "m_lo",
            "q_ps", "q_exp", "q_pos", "q", "k_ps", "k_exp", "v", "k_pos", "k",
            "kv_ps", "kv", "cen", "nd_ps", "den", "rden", "an", "at_ps", "at", "y_ps", "res")}
        ln_names = ("stats", "mv", "var", "root", "chain", "shift", "xn", "xn_a")
        ln_s = {n: sem("ln_" + n) for n in ln_names}
        f_s = [{n: sem(f"f{k}_{n}") for n in (
            "xt_ps", "xt", "x_hi", "x_lo", "xk", "lg_ps", "lg", "choice", "ones",
            "y_ps", "y_hi", "y_lo", "mx_ps", "mx", "negm", "shift", "sh_ps", "row",
            "vo_ps", "gated", "vsum", "v_hi", "v_lo", "st_ps", "p", "p_lo", "pv_ps",
            "c_raw", "c_rec", "c32", "c_hi", "c_lo", "ct_ps", "ct", "res")} for k in range(2)]
        c_s = {n: sem("c_" + n) for n in (
            "zero", "xt_ps", "xt", "kq_ps", "kq_hi", "kq_lo", "st_ps", "st_v", "st_a",
            "v_ps", "v_hi", "v_lo", "qh", "mx_ps", "mx", "neg", "shift", "sh_ps", "row", "s_ps", "p",
            "lo_v", "lo_g", "pv_ps", "raw", "rec", "o", "ot_ps", "ot", "y_ps", "res")}

        block = ctx.enter_context(nc.Block())

        def top_half(x):
            return x.bitcast(BF16)[:, 1::2]

        def norm_vector(v, k, src, dst):
            s = ln_s
            for t in range(NT):
                v.bn_stats(stats[:, t, :], src[:, t, :]).then_inc(s["stats"], 1)
            for t in range(NT):
                v.wait_ge(s["stats"], NT * k + t + 1)
                v.bn_aggr(mv[:, t, :], stats[:, t, :]).then_inc(s["mv"], 1)
            v.wait_ge(s["mv"], NT * (k + 1))
            v.tensor_scalar(lnv[:, 0, :], mv[:, :, 1], EPS, None, ALU.add).then_inc(s["var"], 1)
            v.wait_ge(s["var"], k + 1)
            v.wait_ge(s["root"], k + 1)
            v.reciprocal(lnv[:, 2, :], lnv[:, 1, :]).then_inc(s["chain"], 1)
            v.wait_ge(s["chain"], 5 * k + 1)
            v.tensor_tensor(lnv[:, 3, :], lnv[:, 2, :], lnv[:, 2, :], ALU.mult).then_inc(s["chain"], 1)
            v.wait_ge(s["chain"], 5 * k + 2)
            v.tensor_tensor(lnv[:, 4, :], lnv[:, 3, :], lnv[:, 0, :], ALU.mult).then_inc(s["chain"], 1)
            v.wait_ge(s["chain"], 5 * k + 3)
            v.tensor_scalar(lnv[:, 3, :], lnv[:, 4, :], -0.5, 1.5, ALU.mult, ALU.add).then_inc(s["chain"], 1)
            v.wait_ge(s["chain"], 5 * k + 4)
            v.tensor_tensor(lnv[:, 5, :], lnv[:, 3, :], lnv[:, 2, :], ALU.mult).then_inc(s["chain"], 1)
            v.wait_ge(s["chain"], 5 * k + 5)
            v.scalar_tensor_tensor(lnv[:, 6, :], mv[:, :, 0], -1.0, lnv[:, 5, :],
                                   ALU.mult, ALU.mult).then_inc(s["shift"], 1)
            for t in range(0, NT, 2):
                v.tensor_scalar(dst[:, t, :], src[:, t, :], mv[:, t, 0:1], lnv[:, 5, t:t + 1],
                                ALU.subtract, ALU.mult).then_inc(s["xn"], 1)

        def norm_scalar(a, k, src, dst):
            a.wait_ge(ln_s["var"], k + 1)
            a.activation(lnv[:, 1, :], lnv[:, 0, :], ACT.Sqrt).then_inc(ln_s["root"], 1)
            a.wait_ge(ln_s["shift"], k + 1)
            for t in range(1, NT, 2):
                a.activation(dst[:, t, :], src[:, t, :], ACT.Identity, scale=lnv[:, 5, t:t + 1],
                             bias=lnv[:, 6, t:t + 1]).then_inc(ln_s["xn_a"], 1)

        def normed(eng, n):
            eng.wait_ge(ln_s["xn"], n // 2)
            eng.wait_ge(ln_s["xn_a"], n // 2)

        def linear_tensor(pe):
            s = a_s
            pe.wait_ge(consts, 2)
            pe.wait_ge(ld_w, 16 * 4)
            for w in range(4):
                mm = pe.transpose(B[0][:, w * P:(w + 1) * P], w_nat[:, w, :], ident[:, :])
            mm.then_inc(s["wt_ps"], 1)
            pe.wait_ge(ld_b, 16 * 8)
            pe.transpose(B[1][:, 0:P], sel_nat[:, :], ident[:, :]).then_inc(s["sel_ps"], 1)
            for b in range(NB):
                normed(pe, TPB * (b + 1))
                for t in range(TPB):
                    mm = pe.transpose(B[2 + b][:, t * P:(t + 1) * P], xn[:, b * TPB + t, :], ident[:, :])
                mm.then_inc(s["xt_ps"], 1)
            for g in range(2):
                pe.wait_ge(qk_cen, 2 * HF // 2 * (g + 1))
                for h in range(HF // 2):
                    hh = g * HF // 2 + h
                    mm = pe.matmul(B[6 + g][:, h * P:(h + 1) * P], qk_w[:, 0, hh, :], qk_w[:, 1, hh, :],
                                   start=True, stop=True)
                mm.then_inc(s["m_ps"], 1)
            pe.wait_ge(s["wt"], 1)
            pe.wait_ge(s["sel"], 1)
            for b in range(NB):
                pe.wait_ge(s["xt"], b + 1)
                if b >= 2:
                    pe.wait_ge(s["q_pos"], b - 1)
                pe.matmul(B[b % 2][:, :], wT[:, 0, :], xT[:, b * BLK:(b + 1) * BLK],
                          start=True, stop=True).then_inc(s["q_ps"], 1)
            pe.wait_ge(consts, 3)
            for n in range(NT // 2):
                bank = B[2 + n % 2]
                pe.wait_ge(s["xt"], NB)
                if n >= 2:
                    pe.wait_ge(s["v"], n - 1)
                for r in range(2):
                    t = 2 * n + r
                    o = bank[:, r * 2 * P:(r + 1) * 2 * P]
                    pe.matmul(o, ones[0:1, :], bkv_row[:, :], start=True, stop=False)
                    mm = pe.matmul(o, xT[:, t * P:(t + 1) * P],
                                   wT[:, 1:3, :].rearrange("p a b -> p (a b)"), start=False, stop=True)
                mm.then_inc(s["k_ps"], 1)
            pe.wait_ge(vconst, 1)
            for t in range(NT):
                if t % 2 == 0:
                    pe.wait_ge(s["k"], t // 2 + 1)
                    pe.wait_ge(s["v"], t // 2 + 1)
                mm = pe.matmul(B[4][:, 0:P + 1], k_nat[:, t, :], v_nat[:, t, :],
                               start=(t == 0), stop=(t == NT - 1))
            mm.then_inc(s["kv_ps"], 1)
            pe.wait_ge(s["kv"], 2)
            pe.wait_ge(s["q"], NB)
            for b in range(NB):
                if b >= 2:
                    pe.wait_ge(s["an"], b - 1)
                for t in range(TPB):
                    o = B[2 * (b % 2) + t // 2][:, (t % 2) * (P + HA):(t % 2 + 1) * (P + HA)]
                    tt = b * TPB + t
                    mm = pe.matmul(o, qT[:, tt * P:(tt + 1) * P], kv_sb[:, :], start=True, stop=True)
                mm.then_inc(s["nd_ps"], 1)
            pe.wait_ge(s["m_lo"], 2)
            for b in range(NB):
                pe.wait_ge(s["an"], b + 1)
                if b >= 2:
                    pe.wait_ge(s["at"], b - 1)
                for t in range(TPB):
                    mm = pe.transpose(B[4 + b % 2][:, t * P:(t + 1) * P], a_nat[:, b % 2, t, :], ident[:, :])
                mm.then_inc(s["at_ps"], 1)
                pe.wait_ge(s["at"], b + 1)
                if b >= 2:
                    pe.wait_ge(s["res"], b - 1)
                for t in range(TPB):
                    o = B[6 + b % 2][:, t * P:(t + 1) * P]
                    pe.matmul(o, ones[0:1, :], bo_row[:, :], start=True, stop=False)
                    mm = pe.matmul(o, aT[:, (b * TPB + t) * P:(b * TPB + t + 1) * P], wT[:, 3, :],
                                   start=False, stop=True)
                mm.then_inc(s["y_ps"], 1)

        def linear_scalar(a):
            s = a_s
            norm_scalar(a, 0, x_res, xn)
            a.wait_ge(s["wt_ps"], 1)
            a.activation(wT[:, :, :].rearrange("p a b -> p (a b)"), B[0][:, :], ACT.Copy).then_inc(s["wt"], 1)
            a.wait_ge(s["sel_ps"], 1)
            a.activation(selT[:, :], B[1][:, 0:P], ACT.Copy).then_inc(s["sel"], 1)
            for b in range(NB):
                a.wait_ge(s["xt_ps"], b + 1)
                a.activation(xT[:, b * BLK:(b + 1) * BLK], B[2 + b][:, :], ACT.Copy).then_inc(s["xt"], 1)
            for g in range(2):
                a.wait_ge(s["m_ps"], g + 1)
                a.activation(m_hi[:, 4 * g:4 * g + 4, :].rearrange("p a b -> p (a b)"), B[6 + g][:, :],
                             ACT.Copy, scale=SCALE_F * G_W).then_inc(s["m_hi"], 1)
            for b in range(NB):
                a.wait_ge(s["q_ps"], b + 1)
                if b >= 2:
                    a.wait_ge(s["q"], b - 1)
                a.activation(q_exp[:, b % 2, :], B[b % 2][:, :], ACT.Exp,
                             bias=bq_col[:, 0:1]).then_inc(s["q_exp"], 1)
                a.activation(q_pos[:, b % 2, :], B[b % 2][:, :], ACT.Relu,
                             bias=bq_col[:, 0:1]).then_inc(s["q_pos"], 1)
            a.wait_ge(vconst, 1)
            for n in range(NT // 2):
                ps = B[2 + n % 2][:, :].rearrange("p (r a c) -> p r a c", r=2, a=2)
                a.wait_ge(s["k_ps"], n + 1)
                if n >= 2:
                    a.wait_ge(s["k"], n - 1)
                a.activation(k_exp[:, n % 2, :, :], ps[:, :, 0, :], ACT.Exp).then_inc(s["k_exp"], 1)
                a.activation(k_pos[:, n % 2, :, :], ps[:, :, 0, :], ACT.Relu).then_inc(s["k_pos"], 1)
                a.activation(v_nat[:, 2 * n:2 * n + 2, 0:P], ps[:, :, 1, :], ACT.Copy).then_inc(s["v"], 1)
            experts_scalar(a, 0, HALVES_0)
            for b in range(NB):
                a.wait_ge(s["at_ps"], b + 1)
                a.activation(aT[:, b * BLK:(b + 1) * BLK], B[4 + b % 2][:, :], ACT.Copy).then_inc(s["at"], 1)

        def linear_vector(v):
            s = a_s
            v.memset(v_nat[:, :, P:P + 1], 1.0).then_inc(vconst, 1)
            v.wait_ge(ld_x, 16)
            norm_vector(v, 0, x_res, xn)
            v.wait_ge(ld_qk, 32)
            v.tensor_copy(cen[:, :, :], qk_w[:, :, :, 0]).then_inc(s["cen"], 1)
            v.wait_ge(s["cen"], 1)
            for h in range(HF):
                for w in range(2):
                    v.tensor_scalar(qk_w[:, w, h, :], qk_w[:, w, h, :], cen[:, w, h:h + 1], None,
                                    ALU.subtract).then_inc(qk_cen, 1)
            for g in range(2):
                v.wait_ge(s["m_hi"], g + 1)
                v.scalar_tensor_tensor(m_lo[:, 4 * g:4 * g + 4, :].rearrange("p a b -> p (a b)"),
                                       B[6 + g][:, :], SCALE_F * G_W,
                                       m_hi[:, 4 * g:4 * g + 4, :].rearrange("p a b -> p (a b)"),
                                       ALU.mult, ALU.subtract).then_inc(s["m_lo"], 1)
            for b in range(NB):
                v.wait_ge(s["q_pos"], b + 1)
                v.scalar_tensor_tensor(qT[:, b * BLK:(b + 1) * BLK], q_exp[:, b % 2, :], 1.0,
                                       q_pos[:, b % 2, :], ALU.min, ALU.add).then_inc(s["q"], 1)
            for n in range(NT // 2):
                v.wait_ge(s["k_pos"], n + 1)
                v.scalar_tensor_tensor(k_nat[:, 2 * n:2 * n + 2, :].rearrange("p a b -> p (a b)"),
                                       k_exp[:, n % 2, :, :].rearrange("p a b -> p (a b)"), 1.0,
                                       k_pos[:, n % 2, :, :].rearrange("p a b -> p (a b)"),
                                       ALU.min, ALU.add).then_inc(s["k"], 1)
            v.wait_ge(s["kv_ps"], 1)
            v.wait_ge(consts, 5)
            v.tensor_tensor(kv_sb[:, 0:P], B[4][:, 0:P], head_mask[:, :], ALU.mult).then_inc(s["kv"], 1)
            v.tensor_scalar(kv_sb[:, P:P + HA], head_mask[:, 0:P:DA], B[4][:, P:P + 1], None,
                            ALU.mult).then_inc(s["kv"], 1)
            for b in range(NB):
                v.wait_ge(s["nd_ps"], b + 1)
                nd = [B[2 * (b % 2) + n][:, 0:2 * (P + HA)].rearrange("p (t c) -> p t c", t=2) for n in range(2)]
                for n in range(2):
                    v.tensor_scalar(den[:, b % 2, 2 * n:2 * n + 2, :], nd[n][:, :, P:P + HA], 1e-6, None,
                                    ALU.max).then_inc(s["den"], 1)
                v.wait_ge(s["den"], 2 * b + 2)
                v.reciprocal(rden[:, b % 2, :, :], den[:, b % 2, :, :]).then_inc(s["rden"], 1)
                v.wait_ge(s["rden"], b + 1)
                if b >= 2:
                    v.wait_ge(s["at_ps"], b - 1)
                for n in range(2):
                    r = rden[:, b % 2, 2 * n:2 * n + 2, :].rearrange("p t (h a) -> p t h a", a=1)
                    ins = v.tensor_tensor(
                        a_nat[:, b % 2, 2 * n:2 * n + 2, :].rearrange("p t (h c) -> p t h c", c=DA),
                        nd[n][:, :, 0:P].rearrange("p t (h c) -> p t h c", c=DA),
                        r.broadcast_to([P, 2, HA, DA]), ALU.mult)
                ins.then_inc(s["an"], 1)
            for b in range(NB):
                v.wait_ge(s["y_ps"], b + 1)
                xr = x_res[:, b * TPB:(b + 1) * TPB, :].rearrange("p a b -> p (a b)")
                v.tensor_tensor(xr, B[6 + b % 2][:, :], xr, ALU.add).then_inc(s["res"], 1)

        HALVES_0 = 6
        HALVES = 4 * HF

        def halves_at(i, kt):
            n = HALVES_0 + (NT * i + kt) // 2 if isinstance(i, int) else HALVES
            return [n] if kt % 2 == 1 and n < HALVES else []

        def expert_half(n):
            chunk, e0 = n // 2, n % 2 * (EX // 2)
            es = slice(chunk // 2 * EX + e0, chunk // 2 * EX + e0 + EX // 2)
            hi, lo = (x[:, es, :].rearrange("p a b -> p (a b)") for x in ((vw_hi, vw_lo), (ow_hi, ow_lo))[chunk % 2])
            return stage[:, chunk % 4, e0 * P:(e0 + EX // 2) * P], hi, lo

        def experts_scalar(a, n0, n1):
            for n in range(n0, n1):
                w, hi, _ = expert_half(n)
                a.wait_ge(ld_e[n // 2 % 4], 16 * (n // 8 + 1))
                a.activation(w, w, ACT.Copy, scale=G_W).then_inc(e_up, 1)
                a.wait_ge(e_up, n + 1)
                a.activation(hi, w, ACT.Copy).then_inc(e_hi, 1)

        def experts_pool(g, n0, n1):
            for n in range(n0, n1):
                w, hi, lo = expert_half(n)
                g.wait_ge(e_hi, n + 1)
                g.tensor_tensor(lo, w, hi, ALU.subtract).then_inc(e_lo, 1)

        def loads(sp):
            sp.dma_start(x_res[:, :, :], x_in.rearrange("b (t p) c -> p (b t) c", p=P)).then_inc(ld_x, 16)
            for w, src in enumerate((Wq, Wk, Wv, Wo)):
                sp.dma_start(w_nat[:, w, :], src).then_inc(ld_w, 16)
            col = lambda x: x.rearrange("(p a) -> p a", a=1)
            row = lambda x: x.rearrange("(a c) -> a c", a=1)
            sp.dma_start(bq_col[:, :], col(bq)).then_inc(ld_b, 16)
            sp.dma_start(bkv_row[:, 0:P], row(bk)).then_inc(ld_b, 16)
            sp.dma_start(bkv_row[:, P:2 * P], row(bv)).then_inc(ld_b, 16)
            sp.dma_start(bo_row[:, :], row(bo)).then_inc(ld_b, 16)
            sp.dma_start(sel_nat[0:P // 2, :], sel_v_w).then_inc(ld_b, 16)
            sp.dma_start(sel_nat[P // 2:P, :], sel_o_w).then_inc(ld_b, 16)
            sp.dma_start(rs_col[:, :], row(route_scale).broadcast_to([P, 1])).then_inc(ld_b, 16)
            sp.dma_start(g_col[:, :], col(g_ln)).then_inc(ld_b, 16)
            sp.dma_start(qk_w[:, 0, :, :], q_w.rearrange("(h p) d -> p h d", p=P)).then_inc(ld_qk, 16)
            sp.dma_start(qk_w[:, 1, :, :], k_w.rearrange("(h p) d -> p h d", p=P)).then_inc(ld_qk, 16)
            sp.dma_start(wbq[:, :], Wbq).then_inc(ld_c, 16)
            sp.dma_start(wbkv[:, :], Wbkv).then_inc(ld_c, 16)
            sp.dma_start(wbo[:, :], Wbo).then_inc(ld_c, 16)
            for n in range(2 * HF):
                src, h = (v_w, o_w)[n % 2], n // 2
                if n >= 4:
                    sp.wait_ge(e_lo, 2 * (n - 3))
                sp.dma_start(stage[:, n % 4, :].rearrange("p (e c) -> p e c", e=EX),
                             src[h * EX:(h + 1) * EX].rearrange("e p c -> p e c")).then_inc(ld_e[n % 4], 16)

        def constants_pool(g):
            g.memset(ident[:, :], 0.0).then_inc(zeroed, 1)
            g.memset(head_mask[:, :], 1.0).then_inc(zeroed, 1)
            g.wait_ge(zeroed, 1)
            g.affine_select(out=ident[:, :], in_=ident[:, :], compare_op=ALU.not_equal, fill=1.0,
                            base=0, pattern=[[-1, P]], channel_multiplier=1).then_inc(consts, 1)
            g.wait_ge(consts, 1)
            g.tensor_copy(ident16[:, :], ident[:, :]).then_inc(consts, 1)
            g.memset(ones[:, :], 1.0).then_inc(consts, 1)
            hm = head_mask[:, :].rearrange("p (h c) -> p h c", c=DA)
            g.wait_ge(zeroed, 2)
            g.affine_select(out=hm, in_=hm, compare_op=ALU.is_ge, fill=0.0, base=0,
                            pattern=[[-DA, HA], [0, DA]], channel_multiplier=1).then_inc(consts, 1)
            g.wait_ge(consts, 4)
            g.affine_select(out=hm, in_=hm, compare_op=ALU.is_ge, fill=0.0, base=DA - 1,
                            pattern=[[DA, HA], [0, DA]], channel_multiplier=-1).then_inc(consts, 1)

        def causal_constants_pool(g):
            for n, x in enumerate((place[:, :, :, :], hd_mk[:, :, :], dg[:, :, :], big_id[:, :], row_one[:, :])):
                g.memset(x, 0.0).then_inc(zeroed, 1)
            g.wait_ge(zeroed, 7)
            heads = ident16[:, :].rearrange("p (h c) -> p h c", c=DA)
            for kind, part, b in ((0, 0, 0), (0, 0, 1), (0, 1, 2), (1, 0, 0), (1, 1, 1), (1, 0, 2)):
                g.tensor_copy(place[:, kind, part, :].rearrange("p (h r) -> p h r", r=ROWS)
                              [:, :, 1 + b * DA:1 + (b + 1) * DA], heads).then_inc(consts_c, 1)
            g.memset(row_one[0:1, :], ONE_K).then_inc(consts_c, 1)
            g.affine_select(out=hd_mk[:, :, :], in_=hd_mk[:, :, :], base=0, compare_op=ALU.not_equal, fill=1.0,
                            pattern=[[-ROWS, GROUPS], [-1, ROWS]], channel_multiplier=1).then_inc(consts_c, 1)
            g.affine_select(out=big_id[:, :], in_=big_id[:, :], base=0, pattern=[[-1, P]],
                            compare_op=ALU.not_equal, fill=2.0 ** 60, channel_multiplier=1).then_inc(consts_c, 1)
            g.affine_select(out=dg[:, 0, :], in_=dg[:, 0, :], base=0, pattern=[[-1, P]],
                            compare_op=ALU.is_ge, fill=-2.0 ** 60, channel_multiplier=1).then_inc(consts_c, 1)
            g.affine_select(out=dg[:, 1, :], in_=dg[:, 1, :], base=0, pattern=[[1, P]],
                            compare_op=ALU.is_ge, fill=-2.0 ** 60, channel_multiplier=-1).then_inc(consts_c, 1)

        NI = HF * NB
        CHOICES_END = NB + 3
        EXTRA_MX = (6, 9, 11)
        MX_AT = [[] for _ in range(NT)]
        for u in range(NT):
            MX_AT[[k for k in range(13) for _ in range(1 + (k in EXTRA_MX))][u]].append(u)
        MX_BANK = [7 if u in [x[1] for x in MX_AT if len(x) > 1] else 4 for u in range(NT)]
        MX_LAST = [max([w for w in range(u) if MX_BANK[w] == MX_BANK[u]], default=None) for u in range(NT)]

        def first_units():
            steps = []
            for kt in range(NT):
                steps.append([(0, kt + 2, q) for q in range(2) if kt + 2 < NT])
                if kt >= 8:
                    steps[-1].append((1, (kt - 8) // 2, kt % 2))
            return steps

        HEAD_START = [(0, t, q) for t in range(2) for q in range(2)]
        FIRST = first_units()
        FIRST_DONE = [(h, t) for h, t, q in HEAD_START + [u for st in FIRST for u in st] if q == 1]

        def parts(i):
            lo, hi = (i, i) if isinstance(i, int) else (i.min_val, i.max_val)
            return dict(att=hi < NI, mx=hi + 1 < NI, y=hi + 2 < NI, v=hi < NI - NB, o=lo >= 1)

        def f_mx(i):
            return parts(i)["mx"]

        def unit_base(i):
            if isinstance(i, int) and i == 0:
                return 2 * NT
            lo = i if isinstance(i, int) else i.min_val
            if lo < NI - NB:
                return i * 16 + (2 * NT + 8 - 16)
            return i * 8 + (2 * NT + 8 - 16 + 8 * (NI - NB))

        def over_iterations(eng, body):
            body(0)
            for i in range(1, NB):
                body(i)
            with eng.Fori(NB, CHOICES_END) as i:
                body(i)
            with eng.Fori(CHOICES_END, NI - NB) as i:
                body(i)
            with eng.Fori(NI - NB, NI - 2) as i:
                body(i)
            body(NI - 2)
            body(NI - 1)
            body(NI)

        def switch_tensor(pe, k):
            s = f_s[k]

            def queries(j):
                h, b = quarter(j), j & 3
                xs = [x[:, ds(b * BLK, BLK)] for x in (x_hi, x_lo)]
                pe.matmul(B[7][:, :], m_hi[:, h, :], xs[0], start=True, stop=False)
                pe.matmul(B[7][:, :], m_hi[:, h, :], xs[1], start=False, stop=False)
                pe.matmul(B[7][:, :], m_lo[:, h, :], xs[0], start=False, stop=True).then_inc(s["y_ps"], 1)

            def max_unit(j, u, bank, ready=None):
                t, kb = u // NB, u % NB
                if u == 0:
                    pe.wait_ge(s["y_hi"], j + 1)
                if ready is not None:
                    pe.wait_ge(s["mx"], ready)
                pe.matmul(B[bank][:, :], y_hi[:, j & 3, t * P:(t + 1) * P], xk_hi[:, kb * BLK:(kb + 1) * BLK],
                          start=True, stop=True).then_inc(s["mx_ps"], 1)

            def shift_rows(j):
                pe.wait_ge(s["shift"], j + 1)
                for t in range(TPB):
                    mm = pe.matmul(B[7][0:1, t * P:(t + 1) * P], shift[:, t:t + 1], ident16[:, :],
                                   start=True, stop=True)
                mm.then_inc(s["sh_ps"], 1)

            def scores(j, kt):
                if kt == 0:
                    pe.wait_ge(s["row"], j + 1)
                    pe.wait_ge(s["y_lo"], j + 1)
                if not (isinstance(j, int) and 16 * j + kt < 2):
                    pe.wait_ge(s["p"], j * 16 + (kt - 1))
                o, ks, b = B[kt % 2][:, :], slice(kt * P, (kt + 1) * P), j & 3
                pe.matmul(o, xk_hi[:, ks], y_hi[:, b, :], start=True, stop=False)
                pe.matmul(o, xk_hi[:, ks], y_lo[:, b, :], start=False, stop=False)
                pe.matmul(o, xk_lo[:, ks], y_hi[:, b, :], start=False, stop=True).then_inc(s["st_ps"], 1)

            def context(i, kt):
                n = i * 16 + kt
                if kt == 0:
                    if not (isinstance(i, int) and i == 0):
                        pe.wait_ge(s["c_raw"], i * 2)
                    if not (isinstance(i, int) and i == 0):
                        pe.wait_ge(s["v_lo"], quarter(i) * NT + NT)
                if isinstance(i, int) and i == 0:
                    pe.wait_ge(s["v_lo"], FIRST_DONE.index((0, kt)) + 1)
                pe.wait_ge(s["p_lo"], n + 1)
                slot = quarter(i) & 1
                vh = v_hi[:, slot, kt, 0:P + 1]
                vl = v_lo[:, slot, kt, :]
                for t in range(TPB):
                    o = B[2 + t // 2][:, (t % 2) * (P + 1):(t % 2 + 1) * (P + 1)]
                    ph = top_half(p32[:, kt % 4, t * P:(t + 1) * P])
                    pl = p_lo[:, kt % 4, t * P:(t + 1) * P]
                    pe.matmul(o, ph, vh, start=(kt == 0 and t % 2 == 0), stop=False, skip_group_check=True)
                    pe.matmul(o[:, 0:P], ph, vl, start=False, stop=False, skip_group_check=True)
                    mm = pe.matmul(o, pl, vh, start=False, stop=(kt == NT - 1), skip_group_check=True)
                mm.then_inc(s["pv_ps"], 1)

            def unit(n, par, parts3, w_hi, w_lo, first):
                if not first:
                    pe.wait_ge(s["gated"], n * 4 - 4)
                hi, lo = parts3
                o = B[5 + par][:, :]
                wh, wl = (w.rearrange("p a b -> p (a b)") for w in (w_hi, w_lo))
                pe.matmul(o, hi, wh, start=True, stop=False)
                pe.matmul(o, hi, wl, start=False, stop=False)
                pe.matmul(o, lo, wh, start=False, stop=True).then_inc(s["vo_ps"], 1)

            def v_unit(n, par, h, t, q, first=False):
                ts = ds(t * P, P)
                ws = ds(h * EX + 4 * q, 4)
                unit(n, par, (x_hi[:, ts], x_lo[:, ts]), vw_hi[:, ws, :], vw_lo[:, ws, :], first)

            def o_unit(n, par, h, t, q):
                ts = slice(t * P, (t + 1) * P)
                ws = ds(h * EX + 4 * q, 4)
                unit(n, par, (cT[:, 0, ts], cT[:, 1, ts]), ow_hi[:, ws, :], ow_lo[:, ws, :], False)

            def turn_context(i):
                if parts(i)["att"]:
                    pe.wait_ge(s["row"], i + 1)
                pe.wait_ge(s["c_hi"], i)
                pe.wait_ge(s["c_lo"], i)
                turned = B[7][:, :].bitcast(F16)
                for w in range(2):
                    for t in range(TPB):
                        mm = pe.transpose(turned[:, w * BLK + t * P:w * BLK + (t + 1) * P],
                                          c16[:, w, t, :], ident16[:, :])
                mm.then_inc(s["ct_ps"], 1)

            def max_at(i, kt, second):
                if not f_mx(i) or len(MX_AT[kt]) <= second:
                    return
                u = MX_AT[kt][second]
                if u == 0 or MX_BANK[u] == 4:
                    ready = i * 16 + (17 + MX_LAST[u]) if u else i * 16 + 16
                else:
                    f = parts(i)
                    if kt < 8 and f["o"]:
                        pe.wait_ge(s["ct"], i)
                    elif kt > 8 and f["y"]:
                        pe.wait_ge(s["y_lo"], i + 3)
                    ready = None if MX_LAST[u] is None else i * 16 + (17 + MX_LAST[u])
                max_unit(i + 1, u, MX_BANK[u], ready)

            def body(i):
                f = parts(i)
                first = isinstance(i, int) and i == 0
                ub = unit_base(i)
                n0 = len(HEAD_START)
                if k == 0 and not isinstance(i, int) and i.min_val == NB:
                    pe.wait_ge(e_lo, HALVES)
                for kt in range(NT):
                    max_at(i, kt, 0)
                    if first:
                        if kt == 8 and k == 0:
                            pe.wait_ge(e_lo, 6)
                        for h, t, q in FIRST[kt]:
                            v_unit(n0, n0 % 2, h, t, q)
                            n0 += 1
                    elif f["v"] and kt < 8:
                        v_unit(ub + kt, kt % 2, quarter(i) + 1, (i & 3) * TPB + kt // 2, kt % 2)
                    if f["o"] and kt == 5:
                        turn_context(i)
                    if f["o"] and kt >= 8:
                        if kt == 8:
                            pe.wait_ge(s["ct"], i)
                        j = i - 1
                        m = kt - 8
                        o_unit(ub + (8 if f["v"] else 0) + m, m % 2, quarter(j), m // 2, m % 2)
                    if f["y"] and kt == 8:
                        pe.wait_ge(s["mx"], i * 16 + (17 + MX_AT[EXTRA_MX[0]][1]))
                        queries(i + 2)
                    if f["mx"] and kt == 13:
                        pe.wait_ge(s["mx"], i * 16 + 32)
                        shift_rows(i + 1)
                    if f["att"]:
                        context(i, kt)
                        max_at(i, kt, 1)
                        if kt < NT - 2:
                            scores(i, kt + 2)
                        elif f["mx"]:
                            scores(i + 1, kt + 2 - NT)

            normed(pe, NT * (2 + 3 * k))
            for b in range(NB):
                for t in range(TPB):
                    mm = pe.transpose(B[b][:, t * P:(t + 1) * P], xn[:, b * TPB + t, :], ident[:, :])
                mm.then_inc(s["xt_ps"], 1)
            for b in range(NB):
                pe.wait_ge(s["xt"], b + 1)
                for t in range(TPB):
                    tt = b * TPB + t
                    mm = pe.matmul(B[4 + b][:, t * P:(t + 1) * P], xT[:, tt * P:(tt + 1) * P], selT[:, :],
                                   start=True, stop=True)
                mm.then_inc(s["lg_ps"], 1)
            pe.wait_ge(s["lg"], NB)
            pe.wait_ge(s["x_lo"], NB)
            queries(0)
            pe.wait_ge(s["y_lo"], 1)
            queries(1)
            pe.wait_ge(s["xk"], 4)
            for u in range(NT):
                max_unit(0, u, 4 + u % 3, u - 2 if u >= 3 else None)
            pe.wait_ge(s["y_lo"], 2)
            shift_rows(0)
            scores(0, 0)
            scores(0, 1)
            if k == 0:
                pe.wait_ge(e_lo, 2)
            pe.wait_ge(s["mx"], NT)
            for n, (h, t, q) in enumerate(HEAD_START):
                v_unit(n, n % 2, h, t, q, first=n < 2)
            over_iterations(pe, body)

        def first_parts(kt, v_part):
            done = 2 + sum(q == 1 for st in FIRST[:kt] for _, _, q in st)
            for h, t, q in FIRST[kt]:
                if q == 1:
                    v_part(h, t, done % TPB, done)
                    done += 1

        CHOICES = [(0, 0, 2), (1, 0, 2), (0, 2, 4), (0, 4, HF)]
        CHOICE_STEPS = 18

        def choice_done(c):
            return (c + 1) * CHOICE_STEPS + EX

        def choice_step(v, s, c, n):
            if isinstance(c, int):
                half, h0, h1 = CHOICES[c]
                nh = h1 - h0
                cs = slice(half * 64 + h0 * EX, half * 64 + h1 * EX)
            else:
                half, nh = 1, 2
                cs = ds(c * (2 * EX) + (64 - (2 * NB - 2) * EX), 2 * EX)
            prob, gate = gp[:, :, cs], gates[:, :, cs]
            four = lambda x: x.rearrange("p t (h e) -> p t h e", e=EX)
            one = lambda n: g1[:, n, 0:NT * nh]
            over = lambda n: one(n).rearrange("p (t h a) -> p t h a", h=nh, a=1).broadcast_to([P, NT, nh, EX])
            ties = tie[:, :].rearrange("p (a b e) -> p a b e", a=1, b=1).broadcast_to([P, NT, nh, EX])
            A, C = gt[:, 0, :, 0:nh * EX], gt[:, 1, :, 0:nh * EX]
            v.wait_ge(s["choice"], c * CHOICE_STEPS + (EX + n))
            if n == 0:
                ins = v.tensor_reduce(one(0), four(prob), AX.X, ALU.max)
            elif n == 1:
                ins = v.tensor_tensor(four(A), four(prob), over(0), ALU.is_equal)
            elif n == 2:
                ins = v.tensor_tensor(four(C), four(A), ties, ALU.mult)
            elif n == 3:
                ins = v.tensor_reduce(one(2), four(C), AX.X, ALU.max)
            elif n == 4:
                ins = v.tensor_tensor(four(A), four(C), over(2), ALU.is_equal)
            elif n == 5:
                ins = v.scalar_tensor_tensor(C, A, -4.0, prob, ALU.mult, ALU.add)
            elif n == 6:
                ins = v.tensor_reduce(one(1), four(C), AX.X, ALU.max)
            elif n == 7:
                ins = v.tensor_tensor(four(gate), four(C), over(1), ALU.is_equal)
            elif n == 8:
                ins = v.tensor_tensor(four(C), four(gate), ties, ALU.mult)
            elif n == 9:
                ins = v.tensor_reduce(one(2), four(C), AX.X, ALU.max)
            elif n == 10:
                ins = v.tensor_tensor(four(gate), four(C), over(2), ALU.is_equal)
            elif n == 11:
                ins = v.tensor_tensor(C, A, gate, ALU.add)
            elif n == 12:
                ins = v.tensor_tensor(A, C, prob, ALU.mult)
            elif n == 13:
                ins = v.tensor_tensor(one(2), one(0), one(1), ALU.add)
            elif n == 14:
                ins = v.tensor_scalar(one(0), one(2), 1e-9, None, ALU.max)
            elif n == 15:
                ins = v.reciprocal(one(1), one(0))
            elif n == 16:
                ins = v.tensor_scalar(one(2), one(1), rs_col[:, 0:1], (G_X / (G_X * G_W), 1.0 / (G_C * G_W))[half],
                                      ALU.mult, ALU.mult)
            else:
                ins = v.tensor_tensor(four(gate), four(A), over(2), ALU.mult)
            ins.then_inc(s["choice"], 1)

        def choice_at(v, s, i, kt):
            if (i if isinstance(i, int) else i.min_val) not in range(1, CHOICES_END):
                return
            for n in range(CHOICE_STEPS):
                if n * (7 if isinstance(i, int) and i == 1 else NT) // CHOICE_STEPS == kt:
                    choice_step(v, s, i, n)

        def switch_scalar(a, k):
            s = f_s[k]
            norm_scalar(a, 1 + 3 * k, x_res, xn)
            for b in range(NB):
                bs = slice(b * BLK, (b + 1) * BLK)
                a.wait_ge(s["xt_ps"], b + 1)
                a.activation(xT[:, bs], B[b][:, :], ACT.Copy).then_inc(s["xt"], 1)
                a.activation(x_hi[:, bs], B[b][:, :], ACT.Copy, scale=G_X).then_inc(s["x_hi"], 1)
            for b in range(NB):
                a.wait_ge(s["lg_ps"], b + 1)
                a.activation(gp[:, b * TPB:(b + 1) * TPB, :].rearrange("p a b -> p (a b)"), B[4 + b][:, :],
                             ACT.Sigmoid).then_inc(s["lg"], 1)

            def queries(j):
                a.wait_ge(s["y_ps"], j + 1)
                a.activation(y_hi[:, j & 3, :], B[7][:, :], ACT.Copy,
                             scale=G_Y / (G_X * G_W)).then_inc(s["y_hi"], 1)

            def row(j):
                a.wait_ge(s["sh_ps"], j + 1)
                a.activation(y_hi[0:1, j & 3, :], B[7][0:1, :], ACT.Copy).then_inc(s["row"], 1)

            def exps(j, kt):
                n = j * 16 + kt
                a.wait_ge(s["st_ps"], n + 1)
                early = isinstance(j, int) and j == 0
                if not (early and kt < 4):
                    a.wait_ge(s["pv_ps"], n - 3)
                a.activation(p32[:, kt % 4, :], B[kt % 2][:, :], ACT.Exp,
                             scale=1.0 / G_S).then_inc(s["p"], 1)

            def v_part(h, t, tt, n):
                a.wait_ge(s["vsum"], n + 1)
                a.activation(v_hi[:, h & 1, t, 0:P], v32[:, tt, :], ACT.Copy).then_inc(s["v_hi"], 1)

            def body(i):
                f = parts(i)
                for kt in range(NT):
                    if f["att"] and kt == NT - 1:
                        a.wait_ge(s["pv_ps"], i * 16 + 16)
                        if f["o"]:
                            a.wait_ge(s["c32"], i)
                        for t in range(2):
                            a.activation(c_raw[:, 2 * t:2 * t + 2, :].rearrange("p a b -> p (a b)"),
                                         B[2 + t][:, 0:2 * (P + 1)], ACT.Copy).then_inc(s["c_raw"], 1)
                    if f["mx"] and kt == 13:
                        row(i + 1)
                    if f["y"] and kt == 8:
                        queries(i + 2)
                    if f["att"]:
                        if kt < NT - 2:
                            exps(i, kt + 2)
                        elif f["mx"]:
                            exps(i + 1, kt + 2 - NT)
                    if f["o"] and kt == 1:
                        a.wait_ge(s["c32"], i)
                        a.activation(c16[:, 0, :, :].rearrange("p a b -> p (a b)"),
                                     c32[:, :, :].rearrange("p a b -> p (a b)"), ACT.Copy).then_inc(s["c_hi"], 1)
                    if f["o"] and kt == 5:
                        a.wait_ge(s["ct_ps"], i)
                        a.activation(cT[:, :, :].rearrange("p a b -> p (a b)"),
                                     B[7][:, :].bitcast(F16), ACT.Copy).then_inc(s["ct"], 1)
                    if isinstance(i, int) and i == 0:
                        first_parts(kt, v_part)
                    elif f["v"] and kt in (2, 4, 6, 8):
                        tt = kt // 2 - 1
                        v_part(quarter(i) + 1, (i & 3) * TPB + tt, tt, i * TPB + (NT + tt))
                    if k == 0:
                        for n in halves_at(i, kt):
                            experts_scalar(a, n, n + 1)

            queries(0)
            queries(1)
            row(0)
            exps(0, 0)
            exps(0, 1)
            a.wait_ge(s["ones"], 1)
            for n in range(2):
                v_part(0, n, n, n)
            over_iterations(a, body)

        def switch_pool(g, k):
            s = f_s[k]

            def p_part(j, kt):
                g.wait_ge(s["p"], j * 16 + (kt + 1))
                if not (isinstance(j, int) and j == 0 and kt < 4):
                    g.wait_ge(s["pv_ps"], j * 16 + (kt - 3))
                g.tensor_tensor(p_lo[:, kt % 4, :], p32[:, kt % 4, :], top_half(p32[:, kt % 4, :]),
                                ALU.subtract).then_inc(s["p_lo"], 1)

            def v_part(h, t, tt, n):
                g.wait_ge(s["v_hi"], n + 1)
                g.tensor_tensor(v_lo[:, h & 1, t, :], v32[:, tt, :], v_hi[:, h & 1, t, 0:P],
                                ALU.subtract).then_inc(s["v_lo"], 1)

            def body(i):
                f = parts(i)
                for kt in range(NT):
                    if f["att"]:
                        if kt < NT - 2:
                            p_part(i, kt + 2)
                        elif f["mx"]:
                            p_part(i + 1, kt + 2 - NT)
                    if isinstance(i, int) and i == 0:
                        first_parts(kt, v_part)
                    elif f["v"] and kt in (3, 5, 7, 9):
                        tt = kt // 2 - 1
                        v_part(quarter(i) + 1, (i & 3) * TPB + tt, tt, i * TPB + (NT + tt))
                    if k == 0:
                        for n in halves_at(i, kt):
                            experts_pool(g, n, n + 1)

            g.wait_ge(s["xk"], 2)
            g.memset(xk_hi[0:1, :], ONE_K).then_inc(s["xk"], 1)
            g.memset(xk_lo[0:1, :], 0.0).then_inc(s["xk"], 1)
            p_part(0, 0)
            p_part(0, 1)
            for n in range(2):
                v_part(0, n, n, n)
            over_iterations(g, body)

        def switch_vector(v, k):
            s = f_s[k]
            prev = a_s["res"] if k == 0 else c_s["res"]
            v.wait_ge(prev, NB)
            norm_vector(v, 1 + 3 * k, x_res, xn)
            for b in range(NB):
                bs = slice(b * BLK, (b + 1) * BLK)
                v.wait_ge(s["x_hi"], b + 1)
                v.scalar_tensor_tensor(x_lo[:, bs], B[b][:, :], G_X, x_hi[:, bs],
                                       ALU.mult, ALU.subtract).then_inc(s["x_lo"], 1)
            v.wait_ge(s["x_lo"], NB)
            v.tensor_copy(xk_hi[:, :], x_hi[:, :]).then_inc(s["xk"], 1)
            v.tensor_copy(xk_lo[:, :], x_lo[:, :]).then_inc(s["xk"], 1)
            v.memset(v_hi[:, :, :, P:P + 1], G_X / G_C).then_inc(s["ones"], 1)
            for e in range(EX):
                v.memset(tie[:, e:e + 1], float(EX - e)).then_inc(s["choice"], 1)

            def queries(j):
                v.wait_ge(s["y_hi"], j + 1)
                v.scalar_tensor_tensor(y_lo[:, j & 3, :], B[7][:, :], G_Y / (G_X * G_W), y_hi[:, j & 3, :],
                                       ALU.mult, ALU.subtract).then_inc(s["y_lo"], 1)

            def max_unit(j, u, bank):
                v.wait_ge(s["mx_ps"], j * 16 + (u + 1))
                v.tensor_reduce(mx[:, u // NB, u % NB:u % NB + 1], B[bank][:, :], AX.X,
                                ALU.max).then_inc(s["mx"], 1)

            def shift_of(j):
                v.wait_ge(s["mx"], j * 16 + 16)
                v.tensor_reduce(negm[:, :], mx[:, :, :], AX.X, ALU.max, negate=True).then_inc(s["negm"], 1)
                v.wait_ge(s["negm"], j + 1)
                v.tensor_scalar(shift[:, :], negm[:, :], G_M / G_S, G_M * LOG_P,
                                ALU.mult, ALU.add).then_inc(s["shift"], 1)

            def gate_unit(n, par, tile, col, q, even, odd):
                v.wait_ge(s["vo_ps"], n + 1)
                for r in range(4):
                    acc = (even, odd)[r % 2]
                    ps = B[5 + par][:, r * P:(r + 1) * P]
                    gate = gates[:, tile, ds(col + r, 1)]
                    fresh = q == 0 and r < 2 and (acc is odd or even is not odd and fresh_even[0])
                    if fresh:
                        v.tensor_scalar(acc, ps, gate, None, ALU.mult).then_inc(s["gated"], 1)
                    else:
                        if not (q == 0 and r < 2):
                            v.wait_ge(s["gated"], n * 4 + (r - 1))
                        v.scalar_tensor_tensor(acc, ps, gate, acc, ALU.mult, ALU.add).then_inc(s["gated"], 1)
                if q == 1:
                    v.wait_ge(s["gated"], n * 4 + 4)

            fresh_even = [True]

            def v_gates(n, par, h, t, tt, q, first):
                fresh_even[0] = True
                gate_unit(n, par, t, h * EX + 4 * q, q, va[:, tt, 0, :], va[:, tt, 1, :])
                if q == 1:
                    if first is not None:
                        v.wait_ge(s["v_lo"], first)
                    v.tensor_tensor(v32[:, tt, :], va[:, tt, 0, :], va[:, tt, 1, :], ALU.add).then_inc(s["vsum"], 1)

            def o_gates(n, par, h, t, tt, q):
                fresh_even[0] = False
                xr = x_res[:, t, :]
                gate_unit(n, par, t, P // 2 + h * EX + 4 * q, q, xr, o_b[:, tt % 2, :])
                if q == 1:
                    v.tensor_tensor(xr, xr, o_b[:, tt % 2, :], ALU.add).then_inc(s["res"], 1)

            def max_at(i, kt, second):
                if f_mx(i) and len(MX_AT[kt]) > second:
                    u = MX_AT[kt][second]
                    max_unit(i + 1, u, MX_BANK[u])

            def body(i):
                f = parts(i)
                first = isinstance(i, int) and i == 0
                ub = unit_base(i)
                n0 = len(HEAD_START)
                if not isinstance(i, int) and i.min_val == NB:
                    v.wait_ge(s["choice"], i * CHOICE_STEPS + EX)
                elif not isinstance(i, int):
                    v.wait_ge(s["choice"], choice_done(CHOICES_END - 1))
                j = i - 1
                for kt in range(NT):
                    max_at(i, kt, 0)
                    if f["mx"] and kt == 12:
                        shift_of(i + 1)
                    if f["y"] and kt == 9:
                        queries(i + 2)
                    if isinstance(i, int) and i == 1 and kt == 8:
                        v.wait_ge(s["choice"], choice_done(1))
                    choice_at(v, s, i, kt)
                    if first:
                        for h, t, q in FIRST[kt]:
                            slot = FIRST_DONE.index((h, t))
                            v_gates(n0, n0 % 2, h, t, slot % TPB, q, slot - TPB + 1 if slot >= TPB else None)
                            n0 += 1
                    elif f["v"] and kt < 8:
                        tt = kt // 2
                        v_gates(ub + kt, kt % 2, quarter(i) + 1, (i & 3) * TPB + tt, tt, kt % 2,
                                i * TPB + (NT + tt - TPB + 1))
                    if f["o"] and kt == 1:
                        v.wait_ge(s["c_raw"], i * 2)
                        v.reciprocal(c_rec[:, :], c_raw[:, :, P]).then_inc(s["c_rec"], 1)
                        v.wait_ge(s["c_rec"], i)
                        v.tensor_tensor(c32[:, :, :], c_raw[:, :, 0:P],
                                        c_rec[:, :].rearrange("p (t a) -> p t a", a=1).broadcast_to([P, TPB, P]),
                                        ALU.mult).then_inc(s["c32"], 1)
                    if f["o"] and kt == 2:
                        v.wait_ge(s["c_hi"], i)
                        v.tensor_tensor(c16[:, 1], c32[:, :, :], c16[:, 0], ALU.subtract).then_inc(s["c_lo"], 1)
                    if f["o"] and kt >= 8:
                        m = kt - 8
                        if m == 0 and not (isinstance(i, int) and i == 1):
                            v.wait_ge(s["res"], j * TPB)
                        o_gates(ub + (8 if f["v"] else 0) + m, m % 2, quarter(j), (j & 3) * TPB + m // 2,
                                m // 2, m % 2)
                    max_at(i, kt, 1)

            v.wait_ge(s["lg"], NB)
            queries(0)
            queries(1)
            for u in range(NT):
                max_unit(0, u, 4 + u % 3)
            shift_of(0)
            for n in range(CHOICE_STEPS):
                choice_step(v, s, 0, n)
            v.wait_ge(s["choice"], choice_done(0))
            for n, (h, t, q) in enumerate(HEAD_START):
                v_gates(n, n % 2, h, t, t, q, None)
            over_iterations(v, body)

        UNITS = [(b * TPB + t, kb) for b in range(NB) for kb in range(b + 1) for t in range(TPB)]
        STEPS = [(b, kt) for b in range(NB) for kt in range(TPB * (b + 1))]
        NS = len(STEPS)
        SCORE_BANK, UNIT_BANK = (0, 1, 3), (4, 5, 6)
        LO_AHEAD = 4

        def blocks_at(h, n, nxt, lag):
            found = []
            for b in range(NB):
                step = 2 * (b + 1) * (b + 2) - 1 + lag
                if step % NS == n and (step >= NS or nxt):
                    found.append((h if step >= NS else h + 1, b))
            return found

        ROW_LAG = 4

        def first_at(u, lag):
            return [b for b in range(NB) if 2 * (b + 1) * (b + 2) - 1 + lag == u]

        FIRST_SCORES = 20
        assert 2 * 2 * 3 - 1 + ROW_LAG < FIRST_SCORES and STEPS[AHEAD_C - 1][0] <= 1

        LO_POOL, LO_VECTOR = range(2)
        LO_BY = [(LO_POOL, LO_POOL, LO_VECTOR)[n % 3] for n in range(NS)]
        LO_RANK = [sum(x == LO_BY[n] for x in LO_BY[:n + 1]) for n in range(NS)]

        def lo_part(eng, s, h, n):
            _, q0, q1, _ = step_span(n)
            slot = n % SLOTS_C
            eng.wait_ge(s["p"], h * NS + (n + 1))
            eng.tensor_tensor(pl_c[:, slot, 0:q1 - q0], p_c[:, slot, 0:q1 - q0],
                              top_half(p_c[:, slot, 0:q1 - q0]),
                              ALU.subtract).then_inc(s["lo_v" if LO_BY[n] == LO_VECTOR else "lo_g"], 1)

        def lo_parts(eng, s, h, n, nxt, who):
            m = (n + LO_AHEAD) % NS
            if LO_BY[m] == who and (n + LO_AHEAD < NS or nxt):
                lo_part(eng, s, h if n + LO_AHEAD < NS else h + 1, m)

        def unit_span(u):
            t, kb = UNITS[u]
            return t, kb, min(BLK, (t + 1) * P - kb * BLK)

        def step_span(n):
            b, kt = STEPS[n]
            return kt, max(b * BLK, kt * P), (b + 1) * BLK, kt * P >= b * BLK

        def over_heads(eng, body):
            body(0, True, True)
            with eng.Fori(1, HA - 2) as h:
                body(h, True, True)
            body(HA - 2, True, False)
            body(HA - 1, False, False)

        def causal_tensor(pe):
            s = c_s
            for b in range(NB):
                normed(pe, 3 * NT + (b + 1) * TPB)
                for t in range(TPB):
                    mm = pe.transpose(B[b][:, t * P:(t + 1) * P], xn[:, b * TPB + t, :], ident[:, :])
                mm.then_inc(s["xt_ps"], 1)
            pe.wait_ge(ld_c, 48)

            def keys_queries(n):
                b = n % NB
                pe.wait_ge(s["xt"], b + 1)
                if n >= 2:
                    pe.wait_ge(s["kq_lo"], n - 1)
                pe.matmul(B[4 + n % 2][:, :], wbkv[:, 0:P] if n < NB else wbq[:, :],
                          xT[:, b * BLK:(b + 1) * BLK], start=True, stop=True).then_inc(s["kq_ps"], 1)

            def stack(n):
                kind = n // NB
                pe.wait_ge(s["kq_lo"], n + 1)
                for g in range(GROUPS):
                    m = GROUPS * n + g
                    if m >= 4:
                        pe.wait_ge(s["st_v" if m % 2 else "st_a"], (m - 4) // 2 + 1)
                    for part, kq in ((0, kq_hi), (1, kq_lo)):
                        mm = pe.matmul(B[m % 4][:, :], place[:, kind, part, g * P:(g + 1) * P],
                                       kq[:, n % 2, :], start=part == 0, stop=part == 1)
                    mm.then_inc(s["st_ps"], 1)

            keys_queries(0)
            keys_queries(1)
            pe.wait_ge(s["xt"], NB)
            pe.wait_ge(consts_c, 11)
            for n in range(2 * NB):
                stack(n)
                if n + 2 < 2 * NB:
                    keys_queries(n + 2)
                b = n - 2
                if 0 <= b < NB:
                    if b >= 2:
                        pe.wait_ge(s["v_lo"], b - 1)
                    for t in range(TPB):
                        tt = b * TPB + t
                        mm = pe.matmul(B[6 + b % 2][:, t * P:(t + 1) * P], xT[:, tt * P:(tt + 1) * P],
                                       wbkv[:, P:2 * P], start=True, stop=True)
                    mm.then_inc(s["v_ps"], 1)

            def max_unit(h, u):
                t, kb, w = unit_span(u)
                if u == 0:
                    pe.wait_ge(s["qh"], h + 1)
                if u >= 3:
                    pe.wait_ge(s["mx"], (h + 1) * NS + (u - 2 - NS))
                elif not (isinstance(h, int) and h == 0):
                    pe.wait_ge(s["mx"], h * NS)
                o = B[UNIT_BANK[u % 3]]
                last = kb == t // TPB
                mm = pe.matmul(o[:, 0:w], q_hd[:, h & 1, t * P:(t + 1) * P],
                               k_st[:, quarter(h), kb * BLK:kb * BLK + w], start=True, stop=not last)
                if last:
                    mm = pe.matmul(o[:, w - P:w], big_id[:, :], dg[:, 0, :], start=False, stop=True)
                mm.then_inc(s["mx_ps"], 1)

            def shift_rows(h, b):
                pe.wait_ge(s["shift"], h * NB + (b + 1))
                if not (isinstance(h, int) and h == 0 and b == 0):
                    pe.wait_ge(s["row"], h * NB + b)
                for t in range(TPB):
                    mm = pe.matmul(B[7][0:1, t * P:(t + 1) * P], csh[:, b * TPB + t:b * TPB + t + 1],
                                   ident16[:, :], start=True, stop=True)
                mm.then_inc(s["sh_ps"], 1)

            def scores(h, n):
                kt, q0, q1, diag = step_span(n)
                if kt == 0:
                    pe.wait_ge(s["row"], h * NB + (STEPS[n][0] + 1))
                if n >= 3:
                    pe.wait_ge(s["p"], h * NS + (n - 2))
                elif not (isinstance(h, int) and h == 0):
                    pe.wait_ge(s["p"], h * NS + max(m + 1 - NS for m in range(NS) if m % 3 == n))
                o = B[SCORE_BANK[n % 3]]
                mm = pe.matmul(o[:, 0:q1 - q0], k_st[:, quarter(h), kt * P:(kt + 1) * P],
                               q_hd[:, h & 1, q0:q1], start=True, stop=not diag)
                if diag:
                    mm = pe.matmul(o[:, 0:P], big_id[:, :], dg[:, 1, :], start=False, stop=True)
                mm.then_inc(s["s_ps"], 1)

            def context(h, n):
                kt, q0, q1, _ = step_span(n)
                slot = n % SLOTS_C
                if n == 0 and not (isinstance(h, int) and h == 0):
                    pe.wait_ge(s["raw"], h)
                kind = LO_BY[n]
                pe.wait_ge(s["lo_v" if kind == LO_VECTOR else "lo_g"], h * LO_BY.count(kind) + LO_RANK[n])
                for t in range(q0 // P, q1 // P):
                    c = t * P - q0
                    o = B[2][:, t * (2 * DA + 1):(t + 1) * (2 * DA + 1)]
                    pe.matmul(o, top_half(p_c[:, slot, c:c + P]), v17[:, kt, h, 0:2 * DA + 1],
                              start=(n == 0 and t == 0), stop=False, skip_group_check=True)
                    mm = pe.matmul(o[:, 0:DA + 1], pl_c[:, slot, c:c + P], v17[:, kt, h, 0:DA + 1],
                                   start=False, stop=(n == NS - 1), skip_group_check=True)
                mm.then_inc(s["pv_ps"], 1)

            def body(h, nxt, _):
                for n in range(NS):
                    if nxt:
                        max_unit(h + 1, n)
                    for head, b in blocks_at(h, n, nxt, ROW_LAG):
                        shift_rows(head, b)
                    context(h, n)
                    if n + AHEAD_C < NS:
                        scores(h, n + AHEAD_C)
                    elif nxt:
                        scores(h + 1, n + AHEAD_C - NS)

            pe.wait_ge(s["v_lo"], NB)
            pe.wait_ge(s["st_a"], GROUPS * NB)
            pe.wait_ge(s["st_v"], GROUPS * NB)
            for u in range(NS):
                max_unit(0, u)
                for b in first_at(u, ROW_LAG):
                    shift_rows(0, b)
                if FIRST_SCORES <= u < FIRST_SCORES + AHEAD_C:
                    scores(0, u - FIRST_SCORES)
            over_heads(pe, body)
            pe.wait_ge(s["o"], HA)
            for b in range(NB):
                for t in range(TPB):
                    mm = pe.transpose(B[4 + b % 2][:, t * P:(t + 1) * P], o_nat[:, b * TPB + t, :], ident[:, :])
                mm.then_inc(s["ot_ps"], 1)
                pe.wait_ge(s["ot"], b + 1)
                if b >= 2:
                    pe.wait_ge(s["res"], b - 1)
                for t in range(TPB):
                    tt = b * TPB + t
                    mm = pe.matmul(B[6 + b % 2][:, t * P:(t + 1) * P], xT[:, tt * P:(tt + 1) * P], wbo[:, :],
                                   start=True, stop=True)
                mm.then_inc(s["y_ps"], 1)

        def causal_scalar(a):
            s = c_s
            norm_scalar(a, 2, x_res, xn)
            norm_scalar(a, 3, xn, xn)
            for b in range(NB):
                a.wait_ge(s["xt_ps"], b + 1)
                a.activation(xT[:, b * BLK:(b + 1) * BLK], B[b][:, :], ACT.Copy,
                             scale=g_col[:, 0:1]).then_inc(s["xt"], 1)

            def hi(n):
                a.wait_ge(s["kq_ps"], n + 1)
                if n >= 2:
                    a.wait_ge(s["st_ps"], GROUPS * (n - 1))
                a.activation(kq_hi[:, n % 2, :], B[4 + n % 2][:, :], ACT.Copy,
                             scale=G_X if n < NB else G_Y * SCALE_A).then_inc(s["kq_hi"], 1)

            hi(0)
            hi(1)
            for n in range(2 * NB):
                bs = slice(n % NB * BLK, (n % NB + 1) * BLK)
                for g in range(0, GROUPS, 2):
                    m = GROUPS * n + g
                    a.wait_ge(s["st_ps"], m + 1)
                    if n < NB:
                        a.activation(k_st[:, g, bs], B[m % 4][:, :], ACT.Identity,
                                     bias=row_one[:, 0:1]).then_inc(s["st_a"], 1)
                    else:
                        a.activation(q_st[:, g, bs], B[m % 4][:, :], ACT.Copy).then_inc(s["st_a"], 1)
                if n + 2 < 2 * NB:
                    hi(n + 2)
                b = n - 2
                if 0 <= b < NB:
                    if b == 0:
                        a.wait_ge(s["zero"], 1)
                    a.wait_ge(s["v_ps"], b + 1)
                    a.activation(v17[:, b * TPB:(b + 1) * TPB, :, 0:DA],
                                 B[6 + b % 2][:, :].rearrange("p (t h c) -> p t h c", t=TPB, h=HA), ACT.Copy,
                                 scale=G_X).then_inc(s["v_hi"], 1)

            def row(h, b):
                a.wait_ge(s["sh_ps"], h * NB + (b + 1))
                a.activation(q_hd[0:1, h & 1, b * BLK:(b + 1) * BLK], B[7][0:1, :],
                             ACT.Copy).then_inc(s["row"], 1)

            def exps(h, n):
                _, q0, q1, _ = step_span(n)
                a.wait_ge(s["s_ps"], h * NS + (n + 1))
                if not (isinstance(h, int) and h == 0 and n < SLOTS_C):
                    a.wait_ge(s["pv_ps"], h * NS + (n - (SLOTS_C - 1)))
                a.activation(p_c[:, n % SLOTS_C, 0:q1 - q0], B[SCORE_BANK[n % 3]][:, 0:q1 - q0], ACT.Exp,
                             scale=1.0 / G_S).then_inc(s["p"], 1)

            def body(h, nxt, _):
                for n in range(NS):
                    for head, b in blocks_at(h, n, nxt, ROW_LAG):
                        row(head, b)
                    if n == NS - 1:
                        a.wait_ge(s["pv_ps"], h * NS + NS)
                        if not (isinstance(h, int) and h == 0):
                            a.wait_ge(s["o"], h)
                        a.activation(o_raw[:, :, :].rearrange("p a b -> p (a b)"),
                                     B[2][:, 0:NT * (2 * DA + 1)], ACT.Copy).then_inc(s["raw"], 1)
                    if n + AHEAD_C < NS:
                        exps(h, n + AHEAD_C)
                    elif nxt:
                        exps(h + 1, n + AHEAD_C - NS)

            for u in range(NS):
                for b in first_at(u, ROW_LAG):
                    row(0, b)
                if FIRST_SCORES <= u < FIRST_SCORES + AHEAD_C:
                    exps(0, u - FIRST_SCORES)
            over_heads(a, body)
            for b in range(NB):
                a.wait_ge(s["ot_ps"], b + 1)
                a.activation(xT[:, b * BLK:(b + 1) * BLK], B[4 + b % 2][:, :], ACT.Copy).then_inc(s["ot"], 1)

        def causal_pool(g):
            s = c_s

            def body(h, nxt, _):
                for n in range(NS):
                    lo_parts(g, s, h, n, nxt, LO_POOL)

            for n in range(LO_AHEAD):
                if LO_BY[n] == LO_POOL:
                    lo_part(g, s, 0, n)
            over_heads(g, body)

        def causal_vector(v):
            s = c_s
            v.wait_ge(f_s[0]["res"], NT * HF)
            norm_vector(v, 2, x_res, xn)
            normed(v, 3 * NT)
            norm_vector(v, 3, xn, xn)
            v.memset(v17[:, :, :, DA:DA + 1], G_X).then_inc(s["zero"], 1)
            v.memset(cmx[:, :, :], -3.0e38).then_inc(s["zero"], 1)
            v.wait_ge(consts_c, 11)
            v.tensor_reduce(hd_mask[:, :], hd_mk[:, :, :], AX.X, ALU.add).then_inc(s["zero"], 1)

            def lo(n):
                v.wait_ge(s["kq_hi"], n + 1)
                v.scalar_tensor_tensor(kq_lo[:, n % 2, :], B[4 + n % 2][:, :], G_X if n < NB else G_Y * SCALE_A,
                                       kq_hi[:, n % 2, :], ALU.mult, ALU.subtract).then_inc(s["kq_lo"], 1)

            lo(0)
            lo(1)
            for n in range(2 * NB):
                bs = slice(n % NB * BLK, (n % NB + 1) * BLK)
                for g in range(1, GROUPS, 2):
                    m = GROUPS * n + g
                    v.wait_ge(s["st_ps"], m + 1)
                    if n < NB:
                        v.tensor_scalar(k_st[:, g, bs], B[m % 4][:, :], row_one[:, 0:1], None,
                                        ALU.add).then_inc(s["st_v"], 1)
                    else:
                        v.tensor_copy(q_st[:, g, bs], B[m % 4][:, :]).then_inc(s["st_v"], 1)
                if n + 2 < 2 * NB:
                    lo(n + 2)
                b = n - 2
                if 0 <= b < NB:
                    v.wait_ge(s["v_hi"], b + 1)
                    v.scalar_tensor_tensor(
                        v17[:, b * TPB:(b + 1) * TPB, :, DA + 1:2 * DA + 1].rearrange("p t h c -> p (t h) c"),
                        B[6 + b % 2][:, :].rearrange("p (t c) -> p t c", c=DA), G_X,
                        v17[:, b * TPB:(b + 1) * TPB, :, 0:DA].rearrange("p t h c -> p (t h) c"),
                        ALU.mult, ALU.subtract).then_inc(s["v_lo"], 1)

            def head_queries(h):
                v.tensor_scalar(q_hd[:, h & 1, :], q_st[:, quarter(h), :], hd_mask[:, ds(h & 3, 1)], None,
                                ALU.mult).then_inc(s["qh"], 1)

            def max_unit(h, u):
                t, kb, w = unit_span(u)
                v.wait_ge(s["mx_ps"], h * NS + (u + 1))
                v.tensor_reduce(cmx[:, t, kb:kb + 1], B[UNIT_BANK[u % 3]][:, 0:w], AX.X, ALU.max).then_inc(s["mx"], 1)

            def shift_of(h, b):
                bs = slice(b * TPB, (b + 1) * TPB)
                v.wait_ge(s["mx"], h * NS + 2 * (b + 1) * (b + 2))
                v.tensor_reduce(cneg[:, bs], cmx[:, bs, :], AX.X, ALU.max, negate=True).then_inc(s["neg"], 1)
                v.wait_ge(s["neg"], h * NB + (b + 1))
                v.tensor_scalar(csh[:, bs], cneg[:, bs], G_M / G_S, G_M * LOG_P,
                                ALU.mult, ALU.add).then_inc(s["shift"], 1)

            def outputs(h):
                v.wait_ge(s["raw"], h + 1)
                v.reciprocal(c_rec2[:, :], o_raw[:, :, DA]).then_inc(s["rec"], 1)
                v.tensor_tensor(o_sum[:, :, :], o_raw[:, :, 0:DA], o_raw[:, :, DA + 1:2 * DA + 1],
                                ALU.add).then_inc(s["rec"], 1)
                v.wait_ge(s["rec"], h * 2 + 2)
                v.tensor_tensor(o_nat[:, :, ds(h * DA, DA)], o_sum[:, :, :],
                                c_rec2[:, :].rearrange("p (t a) -> p t a", a=1).broadcast_to([P, NT, DA]),
                                ALU.mult).then_inc(s["o"], 1)

            def body(h, nxt, nxt2):
                for n in range(NS):
                    if nxt:
                        max_unit(h + 1, n)
                    for head, b in blocks_at(h, n, nxt, 0):
                        shift_of(head, b)
                    lo_parts(v, s, h, n, nxt, LO_VECTOR)
                    if n == 2 and not (isinstance(h, int) and h == 0):
                        outputs(h - 1)
                    if n == NS - AHEAD_C and nxt2:
                        v.wait_ge(s["s_ps"], h * NS + NS)
                        head_queries(h + 2)

            v.wait_ge(s["st_a"], GROUPS * NB)
            v.wait_ge(s["st_v"], GROUPS * NB)
            v.wait_ge(s["zero"], 3)
            head_queries(0)
            head_queries(1)
            for u in range(NS):
                max_unit(0, u)
                for b in first_at(u, 0):
                    shift_of(0, b)
            for n in range(LO_AHEAD):
                if LO_BY[n] == LO_VECTOR:
                    lo_part(v, s, 0, n)
            over_heads(v, body)
            outputs(HA - 1)
            for b in range(NB):
                v.wait_ge(s["y_ps"], b + 1)
                xr = x_res[:, b * TPB:(b + 1) * TPB, :].rearrange("p a b -> p (a b)")
                v.tensor_tensor(xr, B[6 + b % 2][:, :], xr, ALU.add).then_inc(s["res"], 1)

        @block.sync
        def _(sp):
            loads(sp)
            sp.wait_ge(f_s[1]["res"], NT * HF)
            sp.dma_start(out.rearrange("b (t p) c -> p (b t) c", p=P), x_res[:, :, :]).then_inc(out_done, 16)
            sp.wait_ge(out_done, 16)

        @block.tensor
        def _(pe):
            linear_tensor(pe)
            switch_tensor(pe, 0)
            causal_tensor(pe)
            switch_tensor(pe, 1)

        @block.scalar
        def _(a):
            linear_scalar(a)
            switch_scalar(a, 0)
            causal_scalar(a)
            switch_scalar(a, 1)

        @block.vector
        def _(v):
            linear_vector(v)
            switch_vector(v, 0)
            causal_vector(v)
            switch_vector(v, 1)

        @block.gpsimd
        def _(g):
            constants_pool(g)
            experts_pool(g, 0, HALVES_0)
            causal_constants_pool(g)
            switch_pool(g, 0)
            causal_pool(g)
            switch_pool(g, 1)


_INS = ['L0_attn_a_x', 'L0_attn_a_Wq', 'L0_attn_a_bq', 'L0_attn_a_Wk', 'L0_attn_a_bk', 'L0_attn_a_Wv',
        'L0_attn_a_bv', 'L0_attn_a_Wo', 'L0_attn_a_bo', 'L0_attn_b_g_ln', 'L0_attn_b_Wq', 'L0_attn_b_Wkv',
        'L0_attn_b_Wo', 'L0_ffn_q_w', 'L0_ffn_k_w', 'L0_ffn_v_w', 'L0_ffn_o_w', 'L0_ffn_sel_v_w',
        'L0_ffn_sel_o_w', 'L0_ffn_route_scale']


def kernel(**inputs):
    import numpy as _np
    import concourse.bacc as _bacc
    from concourse import mybir as _mybir
    from concourse.bass_utils import run_bass_kernel_spmd as _run

    nc = _bacc.Bacc("TRN2", target_bir_lowering=False, num_devices=1)
    arrays, args = {}, []
    for name in _INS:
        a = _np.ascontiguousarray(inputs[name])
        arrays[f"in_{name}_dram"] = a
        args.append(nc.dram_tensor(f"in_{name}_dram", a.shape, _mybir.dt.from_np(a.dtype), kind="ExternalInput").ap())
    shape = inputs['L0_attn_a_x'].shape
    args.append(nc.dram_tensor("out_0_dram", shape, F32, kind="ExternalOutput").ap())
    hybrid_program(nc, *args)
    r = _run(nc, [arrays], core_ids=[0])
    return r.results[0]["out_0_dram"]
```
